# Optimizing a Trainium2 kernel written in Bass

```python
import numpy as np
import jax
import jax.numpy as jnp

def _softmax(x, axis=-1):
    return jax.nn.softmax(x, axis=axis)

def _gelu(x):
    return jax.nn.gelu(x, approximate=True)

def _silu(x):
    return jax.nn.silu(x)

def _sigmoid(x):
    return jax.nn.sigmoid(x)

def _layernorm(x, axis=-1, eps=1e-05):
    m = jnp.mean(x, axis=axis, keepdims=True)
    v = jnp.var(x, axis=axis, keepdims=True)
    return (x - m) / jnp.sqrt(v + eps)

def _scatter_add(tgt, idx, src, axis=0):
    return tgt.at[idx].add(src)

def _segment_sum(src, seg, n):
    return jax.ops.segment_sum(src, seg, n)
kernel_name = 'mk_decoder_preln_d1_seqx_r8_d85b9a'

def setup_inputs(seed: int=0):
    np.random.seed(seed)
    _w = jnp.asarray

    def _rec_inputs():
        import jax
        import jax.numpy as jnp
        _rk = jax.random.key(seed)
        x = -0.0002928 + 1 * jax.random.normal(jax.random.fold_in(_rk, 1), (16, 56, 128), jnp.float32)
        _lenS = 56 - jax.random.randint(jax.random.fold_in(_rk, 7), (16,), 0, max(1, 56 // 4) + 1, jnp.int32)
        _lenS2 = 1500 - jax.random.randint(jax.random.fold_in(_rk, 8), (16,), 0, max(1, 1500 // 4) + 1, jnp.int32)
        _ctx_1024P = jax.random.normal(jax.random.fold_in(_rk, 11), (16, 16, 128), jnp.float32)
        _ctx_1024c = jax.random.dirichlet(jax.random.fold_in(_rk, 511), 0.3 * jnp.ones((16,), jnp.float32), (16, 1500))
        _ctx_1024t = jnp.einsum('bsk,bkd->bsd', _ctx_1024c, _ctx_1024P)
        _ctx_1024t = _ctx_1024t * jax.lax.rsqrt(jnp.mean(jnp.square(_ctx_1024t)) + 1e-12) * 0.953939
        ctx_1024 = -1.39393e-06 + 0.999914 * (_ctx_1024t + 0.3 * jax.random.normal(jax.random.fold_in(_rk, 611), (16, 1500, 128), jnp.float32))
        fside_BxS2_0 = -0.00600047 + 0.990131 * jax.random.normal(jax.random.fold_in(_rk, 12), (16, 1500), jnp.float32)
        return (x, ctx_1024, fside_BxS2_0)
    x, ctx_1024, fside_BxS2_0 = _rec_inputs()

    def _L0_attn_setup():
        import jax, jax.numpy as jnp
        import numpy as np
        B, S, D, H = (2, 256, 128, 16)
        HD = D // H
        key = jax.random.key(seed)
        ks = jax.random.split(key, 5)
        return {'x': jax.random.normal(ks[0], (B, S, D), dtype=jnp.float32), 'qkv_w': jax.random.normal(ks[1], (3 * D, D), dtype=jnp.float32) * (1.0 / np.sqrt(D)), 'qkv_b': jax.random.normal(ks[2], (3 * D,), dtype=jnp.float32) * 0.02, 'proj_w': jax.random.normal(ks[3], (D, D), dtype=jnp.float32) * (1.0 / np.sqrt(D)), 'proj_b': jax.random.normal(ks[4], (D,), dtype=jnp.float32) * 0.02}
    _L0_attn_all = _L0_attn_setup()
    _L0_attn_in = {k: v for k, v in _L0_attn_all.items() if k in ('qkv_w', 'qkv_b', 'proj_w', 'proj_b')}
    del _L0_attn_all

    def _L0_xattn_setup():
        import jax, jax.numpy as jnp
        import numpy as np
        EMBED = 128
        NHEAD = 16
        HEAD_DIM = EMBED // NHEAD
        key = jax.random.key(seed)
        ks = jax.random.split(key, 8)
        B, SQ, SKV = (2, 256, 256)
        scale = 1.0 / np.sqrt(EMBED)
        return {'query': jax.random.normal(ks[0], (B, SQ, EMBED), dtype=jnp.float32), 'key': jax.random.normal(ks[1], (B, SKV, EMBED), dtype=jnp.float32), 'value': jax.random.normal(ks[2], (B, SKV, EMBED), dtype=jnp.float32), 'attention_bias': jax.random.normal(ks[3], (B, SKV), dtype=jnp.float32), 'Wq': jax.random.normal(ks[4], (EMBED, EMBED), dtype=jnp.float32) * scale, 'Wk': jax.random.normal(ks[5], (EMBED, EMBED), dtype=jnp.float32) * scale, 'Wv': jax.random.normal(ks[6], (EMBED, EMBED), dtype=jnp.float32) * scale, 'Wo': jax.random.normal(ks[7], (EMBED, EMBED), dtype=jnp.float32) * scale}
    _L0_xattn_all = _L0_xattn_setup()
    _L0_xattn_in = {k: v for k, v in _L0_xattn_all.items() if k in ('Wq', 'Wk', 'Wv', 'Wo')}
    del _L0_xattn_all

    def _L0_ffn_setup():
        import jax, jax.numpy as jnp
        import numpy as np
        TOP_K = 4
        CAP_FACTOR = 4

        def swiglu(x, w1, w2, w3):
            return jax.nn.silu(x @ w1) * (x @ w3) @ w2
        key = jax.random.key(seed)
        ks = jax.random.split(key, 8)
        B, S, D, H, E = (2, 256, 128, 64, 32)
        Hs = 2 * H
        sd = lambda *sh: 1.0 / np.sqrt(sh[-2])
        x = jax.random.normal(ks[0], (B, S, D), dtype=jnp.float32)
        Wg = jax.random.normal(ks[1], (D, E), dtype=jnp.float32) * (1.0 / np.sqrt(D))
        W1 = jax.random.normal(ks[2], (E, D, H), dtype=jnp.float32) * (1.0 / np.sqrt(D))
        W3 = jax.random.normal(ks[3], (E, D, H), dtype=jnp.float32) * (1.0 / np.sqrt(D))
        W2 = jax.random.normal(ks[4], (E, H, D), dtype=jnp.float32) * (1.0 / np.sqrt(H))
        Ws1 = jax.random.normal(ks[5], (D, Hs), dtype=jnp.float32) * (1.0 / np.sqrt(D))
        Ws3 = jax.random.normal(ks[6], (D, Hs), dtype=jnp.float32) * (1.0 / np.sqrt(D))
        Ws2 = jax.random.normal(ks[7], (Hs, D), dtype=jnp.float32) * (1.0 / np.sqrt(Hs))
        return {'x': x, 'Wg': Wg, 'W1': W1, 'W2': W2, 'W3': W3, 'Ws1': Ws1, 'Ws2': Ws2, 'Ws3': Ws3}
    _L0_ffn_all = _L0_ffn_setup()
    _L0_ffn_in = {k: v for k, v in _L0_ffn_all.items() if k in ('Wg', 'W1', 'W2', 'W3', 'Ws1', 'Ws2', 'Ws3')}
    del _L0_ffn_all
    return {'x': x, 'ctx_1024': ctx_1024, 'fside_BxS2_0': fside_BxS2_0, 'L0_attn_qkv_w': _L0_attn_in['qkv_w'], 'L0_attn_qkv_b': _L0_attn_in['qkv_b'], 'L0_attn_proj_w': _L0_attn_in['proj_w'], 'L0_attn_proj_b': _L0_attn_in['proj_b'], 'L0_xattn_Wq': _L0_xattn_in['Wq'], 'L0_xattn_Wk': _L0_xattn_in['Wk'], 'L0_xattn_Wv': _L0_xattn_in['Wv'], 'L0_xattn_Wo': _L0_xattn_in['Wo'], 'L0_ffn_Wg': _L0_ffn_in['Wg'], 'L0_ffn_W1': _L0_ffn_in['W1'], 'L0_ffn_W2': _L0_ffn_in['W2'], 'L0_ffn_W3': _L0_ffn_in['W3'], 'L0_ffn_Ws1': _L0_ffn_in['Ws1'], 'L0_ffn_Ws2': _L0_ffn_in['Ws2'], 'L0_ffn_Ws3': _L0_ffn_in['Ws3']}

def reference(x, ctx_1024, fside_BxS2_0, L0_attn_qkv_w, L0_attn_qkv_b, L0_attn_proj_w, L0_attn_proj_b, L0_xattn_Wq, L0_xattn_Wk, L0_xattn_Wv, L0_xattn_Wo, L0_ffn_Wg, L0_ffn_W1, L0_ffn_W2, L0_ffn_W3, L0_ffn_Ws1, L0_ffn_Ws2, L0_ffn_Ws3):
    import jax
    import jax.numpy as jnp

    def _L0_attn_ref(x, qkv_w, qkv_b, proj_w, proj_b):
        import jax, jax.numpy as jnp
        import numpy as np
        B, S, D, H = (2, 256, 128, 16)
        HD = D // H
        b, s, d = x.shape
        qkv = jnp.einsum('bsd,ed->bse', x, qkv_w) + qkv_b
        qkv = qkv.reshape(b, s, 3, H, HD)
        q = jnp.transpose(qkv[:, :, 0], (0, 2, 1, 3))
        k = jnp.transpose(qkv[:, :, 1], (0, 2, 1, 3))
        v = jnp.transpose(qkv[:, :, 2], (0, 2, 1, 3))
        scale = 1.0 / jnp.sqrt(jnp.asarray(HD, dtype=x.dtype))
        scores = jnp.einsum('bhqe,bhke->bhqk', q, k) * scale
        attn = jax.nn.softmax(scores, axis=-1)
        out = jnp.einsum('bhqk,bhke->bhqe', attn, v)
        out = jnp.transpose(out, (0, 2, 1, 3)).reshape(b, s, d)
        out = jnp.einsum('bsd,ed->bse', out, proj_w) + proj_b
        return out

    def _L0_xattn_ref(query, key, value, attention_bias, Wq, Wk, Wv, Wo):
        import jax, jax.numpy as jnp
        import numpy as np
        EMBED = 128
        NHEAD = 16
        HEAD_DIM = EMBED // NHEAD
        B, SQ, _ = query.shape
        SKV = key.shape[1]

        def proj(x, W, S):
            return (x @ W.T).reshape(B, S, NHEAD, HEAD_DIM).transpose(0, 2, 1, 3)
        q = proj(query, Wq, SQ)
        k = proj(key, Wk, SKV)
        v = proj(value, Wv, SKV)
        scores = jnp.einsum('bhqd,bhkd->bhqk', q, k) / np.sqrt(HEAD_DIM)
        scores = scores + attention_bias[:, None, None, :]
        probs = jax.nn.softmax(scores, axis=-1)
        out = jnp.einsum('bhqk,bhkd->bhqd', probs, v)
        out = out.transpose(0, 2, 1, 3).reshape(B, SQ, EMBED)
        return out @ Wo.T

    def _L0_ffn_ref(x, Wg, W1, W2, W3, Ws1, Ws2, Ws3):
        import jax, jax.numpy as jnp
        import numpy as np
        TOP_K = 4
        CAP_FACTOR = 4

        def swiglu(x, w1, w2, w3):
            return jax.nn.silu(x @ w1) * (x @ w3) @ w2
        B, S, D = x.shape
        E = Wg.shape[1]
        T = B * S
        xf = x.reshape(T, D)
        scores = jax.nn.softmax(xf @ Wg, axis=-1)
        weights, indices = jax.lax.top_k(scores, TOP_K)
        P = T * TOP_K
        pair_expert = indices.reshape(-1)
        pair_token = jnp.repeat(jnp.arange(T), TOP_K)
        pair_weight = weights.reshape(-1).astype(xf.dtype)
        C = CAP_FACTOR * P // E
        y = jnp.zeros_like(xf)
        for e in range(E):
            pos = jnp.nonzero(pair_expert == e, size=C, fill_value=P)[0]
            valid = pos < P
            safe = jnp.minimum(pos, P - 1)
            tok = jnp.where(valid, pair_token[safe], 0)
            w = jnp.where(valid, pair_weight[safe], 0.0)
            xg = xf[tok]
            out = swiglu(xg, W1[e], W2[e], W3[e]) * w[:, None]
            y = y.at[tok].add(out)
        z = swiglu(xf, Ws1, Ws2, Ws3)
        return (y + z).reshape(B, S, D)
    x = x + _L0_attn_ref(_layernorm(x, axis=-1), L0_attn_qkv_w, L0_attn_qkv_b, L0_attn_proj_w, L0_attn_proj_b)
    x = x + _L0_xattn_ref(_layernorm(x, axis=-1), ctx_1024, ctx_1024, fside_BxS2_0, L0_xattn_Wq, L0_xattn_Wk, L0_xattn_Wv, L0_xattn_Wo)
    x = x + _L0_ffn_ref(_layernorm(x, axis=-1), L0_ffn_Wg, L0_ffn_W1, L0_ffn_W2, L0_ffn_W3, L0_ffn_Ws1, L0_ffn_Ws2, L0_ffn_Ws3)
    return x

_drawn_inputs = setup_inputs


def setup_inputs(seed=0):
    import zlib

    import numpy as np

    out = dict(_drawn_inputs(seed))
    spreads = {}
    factors = {}
    for name, (base, spread) in spreads.items():
        noise = np.random.default_rng([zlib.crc32(name.encode()), seed]).standard_normal(out[name].shape)
        drawn = base * np.exp(spread * noise) if base else spread * noise
        out[name] = jnp.asarray(drawn.astype(out[name].dtype))
    for name, factor in factors.items():
        out[name] = (out[name] * factor).astype(out[name].dtype)
    return out
```

```python
from contextlib import ExitStack

import numpy as np
import concourse.bass as bass
from concourse import mybir
from concourse.alu_op_type import AluOpType as ALU

F32 = mybir.dt.float32
F16 = mybir.dt.float16
U32 = mybir.dt.uint32
ACT = mybir.ActivationFunctionType
AX = mybir.AxisListType

B, S, D, H = 16, 56, 128, 16
HD = D // H
NKEY, KT = 1500, 12
KP = NKEY // KT
T = B * S
TT = T // 128
G = 4
HG = H // G
ROWS = 98
BIG = 32768.0
TWO_BIGS = float(np.array([BIG, BIG], np.float16).view(np.float32)[0])
SQ = float(HD) ** 0.5
SCALE = 1.0 / SQ
VW = 176
NE, TOPK, HE = 32, 4, 64
CAP = 4 * T * TOPK // NE
NP = NE // 2
CH = NKEY // 3
NCH = 24
EPS = 1e-5
HALF = T // 2
NFIRST, NREST = 5, 4 * (G - 1)

MISC = dict(enumerate(["T0", "K0", "T1", "K1", "T2", "K2", "sel", "V0", "V1", "mt", "V2", "tr"]))
OFFSET = {"T": 2, "K": 2, "V": 2, "s": -1, "t": -1, "m": 1}
SELF_MISC = 3 * B


def self_uses(j):
    return [u for u, lag in (("V", 0), ("tr", 3), ("sel", 2)) if 0 <= j - lag < B]


def self_index(r, c, use):
    j = 2 * r + c if isinstance(r, int) else c
    n = sum(len(self_uses(k)) for k in range(j)) + self_uses(j).index(use)
    return n if isinstance(r, int) else n + 2 * 3 * r


def self_live(r, c):
    return not isinstance(r, int) or 0 <= 2 * r + c < B


def live(r, c):
    return not isinstance(r, int) or 0 <= 3 * r + c < B


def uses(i):
    return [u for u in MISC.values() if 0 <= i + OFFSET[u[0]] < B]


def misc_index(r, c, use):
    i = 3 * r + c if isinstance(r, int) else c
    n = SELF_MISC + sum(len(uses(j)) for j in range(-2, i)) + uses(i).index(use)
    return n if isinstance(r, int) else n + 3 * 12 * r


def chunks(s):
    return [(1, 6 + 2 * s + j) if s < 9 else (2, 2 * (s - 9) + j) for j in range(2)]


def build(nc, x_d, ctx_d, bias_d, qkv_w, qkv_b, proj_w, proj_b, wq, wk, wv, wo,
          wg, w1, w2, w3, ws1, ws2, ws3, out_d):
    with ExitStack() as stack:
        sb = lambda n, s, d: stack.enter_context(nc.sbuf_tensor(n, s, d))
        sem = lambda n: stack.enter_context(nc.semaphore(n))

        ident = sb("ident", [128, 128], F32)
        identh = sb("identh", [128, 128], F16)
        grp = sb("grp", [128, G, HG], F32)
        headmask = sb("headmask", [128, HG], F32)
        pick = sb("pick", [128, 3, 4, 9], F32)
        mhalf = sb("mhalf", [128, TT], F32)
        zero = sb("zero", [128, 1, 1], F32)
        ones_h = sb("ones_h", [128, 128], F16)
        before = sb("before", [128, 128], F16)
        pairsel = sb("pairsel", [64, NP, 2, HE], F16)
        expert_no = sb("expert_no", [128, NE], F32)
        wnat = sb("wnat", [128, 8, 128], F32)
        wt32 = sb("wt32", [128, 2, 128], F32)
        wt1 = sb("wt1", [128, 8, 128], F16)
        wt2 = sb("wt2", [128, 8, 128], F16)
        wg_sb = sb("wg_sb", [128, NE], F32)
        bq = sb("bq", [128, 2], F32)
        bv = sb("bv", [S, D], F32)
        bp = sb("bp", [128, D], F32)
        xs = sb("xs", [128, TT, D], F32)
        xn = sb("xn", [128, TT, D], F32)
        stats = sb("stats", [128, TT, 6], F32)
        mv = sb("mv", [128, TT, 2], F32)
        veps = sb("veps", [128, TT], F32)
        rstd = sb("rstd", [128, TT], F32)
        xt1 = sb("xt1", [128, T], F16)
        xt2 = sb("xt2", [128, T], F16)
        q1 = sb("q1", [128, T], F16)
        q2 = sb("q2", [128, T], F16)
        attn = sb("attn", [128, T], F32)
        qs = sb("qs", [128, B, H, S], F16)
        late = sb("late", [128, 2, T], F32)
        qd = [late[:].rearrange("p a t -> p (a t)").bitcast(F16).rearrange("p (b h q) -> p b h q", b=B, h=HG),
              sb("qd2", [128, B, HG, S], F16)[:]]
        xt32, yt = late[:, 0], late[:, 1]
        qsb = [sb(f"qsb{n}", [128, H, S], F16) for n in range(3)]
        ks = [sb(f"ks{n}", [128, G, NKEY], F16) for n in range(3)]
        kself = ks[0][:, :, 0:T]
        ctx = [sb(f"ctx{n}", [128, KT, D], F32) for n in range(3)]
        ch = [sb(f"ch{n}", [128, 2, KT, D], F16) for n in range(3)]
        ct = sb("ct", [128, 2, KT, 128], F16)
        k12 = sb("k12", [128, 2, NKEY], F16)
        v = [sb(f"v{n}", [128, KT, VW], F32) for n in range(3)]
        bcol = sb("bcol", [KP, B, KT], F32)
        bh = sb("bh", [KP, B, KT], F16)
        bh32 = sb("bh32", [KP, B, KT], F32)
        bres = sb("bres", [KP, B, KT], F32)
        brow = sb("brow", [KT, B, KP], F16)
        p = [sb(f"p{n}", [128, H * S], F32) for n in range(2)]
        mx = sb("mx", [112, 8, 3], F32)
        mcol = sb("mcol", [112, 8], F32)
        mrow = sb("mrow", [8, 112], F16)
        mself = sb("mself", [112, B, 8], F32)
        mrow_self = sb("mrow_self", [128, 112], F16)
        osb = sb("osb", [128, 224], F32)
        rec = sb("rec", [S, 4, 4], F32)
        tok = sb("tok", [128, D], F32)

        flat = lambda t, d, n, o=0: t[:].rearrange("p a b -> p (a b)").bitcast(d)[:, o:o + n]
        wf = [flat(ks[n], F32, 3 * 128).rearrange("p (a b) -> p a b", a=3) for n in range(2)]
        wh = [flat(ks[n], F16, 4 * 128, 1000).rearrange("p (a b) -> p a b", a=4) for n in range(2)]
        act_sb = [flat(v[0], F32, HALF, HALF * n) for n in range(2)]
        mid_sb = [flat(v[1], F32, HALF, HALF * n) for n in range(2)]
        u_sb = [flat(v[2], F32, HALF, HALF * n) for n in range(2)]
        logit = flat(ctx[1], F32, 224).rearrange("p (j e) -> p j e", e=NE)
        prob = flat(ctx[1], F32, 224, 224).rearrange("p (j e) -> p j e", e=NE)
        chosen = flat(ctx[1], F32, 224, 448).rearrange("p (j e) -> p j e", e=NE)
        gate = flat(ctx[1], F32, 224, 672).rearrange("p (j e) -> p j e", e=NE)
        eq = flat(ctx[2], F32, 896).rearrange("p (j k e) -> p j k e", j=TT, k=TOPK)
        top8 = flat(ctx[2], F32, 56, 896).rearrange("p (j k) -> p j k", k=8)
        idx8 = flat(ctx[2], U32, 56, 960).rearrange("p (j k) -> p j k", k=8)
        idxf = flat(ctx[2], F32, 56, 1024).rearrange("p (j k) -> p j k", k=8)
        rmax = flat(ctx[2], F32, TT, 1088)
        rsum = flat(ctx[2], F32, TT, 1096)
        rrec = flat(ctx[2], F32, TT, 1104)
        chosen_h = flat(ks[2], F16, 224).rearrange("p (j e) -> p j e", e=NE)
        gpair = flat(ks[2], F16, 448, 256).rearrange("p (j e) -> p j e", e=64)
        gt = flat(ks[2], F16, T, 1024)[0:64]

        ps = stack.enter_context(nc.psum_tensor("ps", [128, 8, 512], F32))
        sbank = [ps[:, 0:2, :], ps[:, 2:4, :]]
        mbank = [ps[:, 4, :], ps[:, 5, :]]
        misc = ps[:, 6, :]
        misch = misc.bitcast(F16)
        obank = ps[:, 7, :]

        const_ok = sem("const_ok")
        const_step = sem("const_step")
        mask_ok = sem("mask_ok")
        w_loaded = sem("w_loaded")
        x_loaded = sem("x_loaded")
        bias_loaded = sem("bias_loaded")
        wt_psum = sem("wt_psum")
        wt1_ok = sem("wt1_ok")
        wt2_ok = sem("wt2_ok")
        ln_step = sem("ln_step")
        rstd_ok = sem("rstd_ok")
        xn_ok = sem("xn_ok")
        xt_psum = sem("xt_psum")
        xt1_ok = sem("xt1_ok")
        xt2_ok = sem("xt2_ok")
        q_psum = sem("q_psum")
        k_psum = sem("k_psum")
        q1_ok = sem("q1_ok")
        q2_ok = sem("q2_ok")
        ks1_ok = sem("ks1_ok")
        ks2_ok = sem("ks2_ok")
        qd_ok = sem("qd_ok")
        qs_rows = sem("qs_rows")
        qs_ok = sem("qs_ok")
        kself_ok = sem("kself_ok")
        mself_psum = sem("mself_psum")
        mself_ok = sem("mself_ok")
        mselft_psum = sem("mselft_psum")
        mselfr_ok = sem("mselfr_ok")
        mself_row = sem("mself_row")
        st_done = sem("st_done")
        exp_done = sem("exp_done")
        pv_done = sem("pv_done")
        o_read = sem("o_read")
        misc_done = sem("misc_done")
        misc_read = sem("misc_read")
        norm_step = sem("norm_step")
        o_psum = sem("o_psum")
        xb_ok = sem("xb_ok")
        x_ok = sem("x_ok")
        bias_step = sem("bias_step")
        bt_psum = sem("bt_psum")
        brow_ok = sem("brow_ok")
        ctx_loaded = [sem(f"ctx_loaded{n}") for n in range(3)]
        ch_step = sem("ch_step")
        ch_ok = sem("ch_ok")
        k1_ok = sem("k1_ok")
        first_ok = [sem(f"first_ok{n}") for n in range(3)]
        rest_ok = [sem(f"rest_ok{n}") for n in range(3)]
        mrow_in = [sem(f"mrow_in{n}") for n in range(3)]
        mx_psum = sem("mx_psum")
        mx_read = sem("mx_read")
        mcol_ok = sem("mcol_ok")
        zero_ok = sem("zero_ok")

        we_loaded = [sem(f"we_loaded{n}") for n in range(2)]
        wh_step = sem("wh_step")
        wh_ok = sem("wh_ok")
        lg_psum = sem("lg_psum")
        rt_step = sem("rt_step")
        rt_exp = sem("rt_exp")
        rank_psum = sem("rank_psum")
        gt_psum = sem("gt_psum")
        gt_ok = sem("gt_ok")
        h_psum = sem("h_psum")
        silu_ok = sem("silu_ok")
        mid_ok = sem("mid_ok")
        u_ok = sem("u_ok")
        y_done = sem("y_done")
        yt_ok = sem("yt_ok")
        yt_psum = sem("yt_psum")
        res_ok = sem("res_ok")
        out_ok = sem("out_ok")

        XA, XB = (0, 512), (512, T)
        SELF_W, CROSS_W = 0, 4

        def split_matmul(out, a1, a2, b1, b2):
            nc.tensor.matmul(out, a1, b1, start=True, stop=False)
            nc.tensor.matmul(out, a1, b2, start=False, stop=False)
            return nc.tensor.matmul(out, a2, b1, start=False, stop=True)

        block = stack.enter_context(nc.Block())

        @block.sync
        def _(sp):
            sp.dma_start(xs[:], x_d.rearrange("b s d -> (b s) d").rearrange("(j p) d -> p j d", p=128)
                         ).then_inc(x_loaded, 16)
            for n in range(3):
                sp.dma_start(wnat[:, n, :], qkv_w[n * 128:(n + 1) * 128, :]).then_inc(w_loaded, 16)
            for n, w in enumerate((proj_w, wq, wk, wv, wo)):
                sp.dma_start(wnat[:, 3 + n, :], w).then_inc(w_loaded, 16)
            qb = qkv_b.rearrange("(n p a) -> n p a", n=3, a=1)
            for n in range(2):
                sp.dma_start(bq[:, n:n + 1], qb[n]).then_inc(w_loaded, 16)
            row = lambda a: a.rearrange("(o n) -> o n", o=1)
            sp.dma_start(bv[:], row(qkv_b[256:384]).to_broadcast([S, D])).then_inc(w_loaded, 16)
            sp.dma_start(bp[:], row(proj_b).to_broadcast([128, D])).then_inc(w_loaded, 16)
            sp.dma_start(wg_sb[:], wg).then_inc(w_loaded, 16)
            sp.dma_start(bcol[:], bias_d.rearrange("b (p t) -> p b t", t=KT)).then_inc(bias_loaded, 16)

            def load_ctx(r, c):
                if not live(r, c):
                    return
                if not isinstance(r, int) or 3 * r + c >= 3:
                    sp.wait_ge(ch_ok, 3 * r + c - 2)
                else:
                    sp.wait_ge(zero_ok, 1)
                sp.dma_start(ctx[c % 3][0:KP], ctx_d[3 * r + c].rearrange("(p t) d -> p t d", t=KT)
                             ).then_inc(ctx_loaded[c % 3], 16)

            load_ctx(0, 0)

            def query_stacks(n):
                sp.wait_ge(qd_ok, 5 * n + 5)
                sp.wait_ge(qs_rows, n + 1)
                for g in range(G):
                    for row0, part in ((0, 0), (32, 0), (64, 1)):
                        sp.dma_start(qs[row0:row0 + 32, :, HG * g:HG * g + HG, :],
                                     qd[part][32 * g:32 * g + 32]).then_inc(qs_ok, 16)

            sp.wait_ge(ks2_ok, 2)
            sp.wait_ge(zero_ok, 2)
            for g in range(G):
                for row0, part in ((0, 0), (32, 1), (64, 0)):
                    sp.dma_start(kself[row0:row0 + 32, g, :], k12[32 * g:32 * g + 32, part, 0:T]
                                 ).then_inc(kself_ok, 16)
            query_stacks(0)
            sp.wait_ge(mselfr_ok, 1)
            sp.dma_start(qs[97:98].rearrange("o b (k h) q -> o (b k) (h q)", k=8), mrow_self[:]
                         ).then_inc(mself_row, 16)

            query_stacks(1)
            sp.wait_ge(qs_ok, 2 * 12 * 16)
            sp.wait_ge(brow_ok, 1)

            def iteration(r, c):
                load_ctx(r, c + 3)
                if live(r, c + 2):
                    n = (c + 2) % 3
                    b = 3 * r + c + 2
                    if not isinstance(r, int) or b >= 3:
                        sp.wait_ge(st_done, B + KT * (b - 2))
                    sp.dma_start(qsb[n][0:ROWS], qs[0:ROWS, bass.ds(b, 1)].rearrange("p o h q -> p (o h) q")
                                 ).then_inc(first_ok[n], 16)
                    for g in range(G):
                        sp.dma_start(ks[n][96:97, g, :].rearrange("o (t k) -> o t k", t=KT),
                                     brow[:, bass.ds(b, 1), :]
                                     ).then_inc((rest_ok if g else first_ok)[n], 16)
                    sp.wait_ge(misc_read, misc_index(r, c, "K2") + 1)
                    for g in range(G):
                        for row0, part in ((0, 0), (32, 1), (64, 0)):
                            sp.dma_start(ks[n][row0:row0 + 32, g, :], k12[32 * g:32 * g + 32, part, :]
                                         ).then_inc((rest_ok if g else first_ok)[n], 16)
                if live(r, c + 1):
                    sp.wait_ge(misc_read, misc_index(r, c, "mt") + 1)
                    sp.dma_start(qsb[(c + 1) % 3][97:98].rearrange("o (k h) q -> o k (h q)", k=8), mrow[:]
                                 ).then_inc(mrow_in[(c + 1) % 3], 16)

            for c in (-2, -1, 0):
                iteration(0, c)
            with sp.Fori(0, 4, 1) as r:
                for c in (1, 2, 3):
                    iteration(r, c)
            for c in (1, 2, 3, 4):
                iteration(4, c)

            def load_experts(n, a, b_, c_):
                for k, w in enumerate((a, b_, c_)):
                    dst = wf[n][:, k, :]
                    sp.dma_start(dst.rearrange("p (e h) -> p e h", e=2) if k < 2 and len(w.shape) == 3 else dst, w
                                 ).then_inc(we_loaded[n], 16)

            sp.wait_ge(st_done, B + KT * B)
            load_experts(0, ws1, ws3, ws2)
            w1v = w1.rearrange("(n e) d h -> n d e h", e=2)
            w3v = w3.rearrange("(n e) d h -> n d e h", e=2)
            w2v = w2.rearrange("(n e) h d -> n (e h) d", e=2)

            def load_pair(pr, n, first=False):
                if not first:
                    sp.wait_ge(y_done, 2 * pr)
                load_experts(n, w1v[pr], w3v[pr], w2v[pr])

            load_pair(0, 1, first=True)
            with sp.Fori(0, NP // 2 - 1, 1) as r:
                load_pair(2 * r + 1, 0)
                load_pair(2 * r + 2, 1)
            load_pair(NP - 1, 0)

            outv = out_d.rearrange("b s d -> (b s) d").rearrange("(j p) d -> p j d", p=128)
            sp.wait_ge(res_ok, 1)
            sp.dma_start(outv[:, 0:4], xs[:, 0:4]).then_inc(out_ok, 16)
            sp.wait_ge(res_ok, 2)
            sp.dma_start(outv[:, 4:7], xs[:, 4:7]).then_inc(out_ok, 16)
            sp.wait_ge(out_ok, 32)

        @block.gpsimd
        def _(pool):
            steps = [0]

            def step(ins):
                steps[0] += 1
                ins.then_inc(const_step, 1)
                pool.wait_ge(const_step, steps[0])

            for n in range(3):
                last = nc.gpsimd.memset(ctx[n][96:128], 0.0)
            last.then_inc(zero_ok, 1)
            pool.wait_ge(zero_ok, 1)
            for n in range(3):
                last = nc.gpsimd.memset(ks[n][96:ROWS].rearrange("p g k -> p (g k)").bitcast(F32), TWO_BIGS)
            step(last)
            for n in range(3):
                nc.gpsimd.memset(v[n][:], 1.0)
            for n in range(2):
                nc.gpsimd.memset(p[n][:], 0.0)
            nc.gpsimd.memset(tok[:], 0.0).then_inc(zero_ok, 1)
            select = nc.gpsimd.affine_select
            nc.gpsimd.memset(ident[:], 0.0)
            nc.gpsimd.memset(grp[:], 1.0)
            nc.gpsimd.memset(zero[:], 0.0)
            nc.gpsimd.memset(pick[:], 0.0)
            nc.gpsimd.memset(mhalf[:], -0.5)
            nc.gpsimd.memset(ones_h[:], 1.0)
            nc.gpsimd.memset(before[:], 1.0)
            step(nc.gpsimd.memset(pairsel[:], 0.0))
            nc.gpsimd.iota(expert_no[:], pattern=[[1, NE]], base=0, channel_multiplier=0,
                           allow_small_or_imprecise_dtypes=True)
            select(out=ident[:], in_=ident[:], compare_op=ALU.not_equal, fill=1.0, base=0,
                   pattern=[[-1, 128]], channel_multiplier=1)
            step(select(out=grp[:], in_=grp[:], compare_op=ALU.is_ge, fill=0.0, base=0,
                        pattern=[[-32, G], [-HD, HG]], channel_multiplier=1))
            step(select(out=grp[:], in_=grp[:], compare_op=ALU.is_ge, fill=0.0, base=HD - 1,
                        pattern=[[32, G], [HD, HG]], channel_multiplier=-1))
            select(out=pick[:], in_=pick[:], compare_op=ALU.not_equal, fill=1.0, base=0,
                   pattern=[[-9, 3], [-32, 4], [-1, 9]], channel_multiplier=1)
            select(out=before[:], in_=before[:], compare_op=ALU.is_gt, fill=0.0, base=0,
                   pattern=[[1, 128]], channel_multiplier=-1)
            step(select(out=pairsel[:], in_=pairsel[:], compare_op=ALU.not_equal, fill=1.0, base=0,
                        pattern=[[-2, NP], [-1, 2], [0, HE]], channel_multiplier=1))
            step(select(out=pairsel[:], in_=pairsel[:], compare_op=ALU.not_equal, fill=1.0, base=-32,
                        pattern=[[-2, NP], [-1, 2], [0, HE]], channel_multiplier=1))
            nc.gpsimd.tensor_copy(identh[:], ident[:]).then_inc(const_ok, 1)

            def rstd_of(n):
                pool.wait_ge(ln_step, 3 * n + 3)
                nc.gpsimd.tensor_tensor(rstd[:], veps[:], mhalf[:], ALU.pow).then_inc(rstd_ok, 1)

            def split_ctx(r, c):
                if not live(r, c):
                    return
                n, b = c % 3, 3 * r + c
                pool.wait_ge(ctx_loaded[n], 16 * (r + c // 3 + 1))
                if not isinstance(r, int) or b >= 3:
                    pool.wait_ge(misc_done, misc_index(r, c - 5, "T2") + 1)
                nc.gpsimd.tensor_tensor(ch[n][:, 0], ctx[n][:], zero[:].to_broadcast([128, KT, D]), ALU.add
                                        ).then_inc(ch_step, 1)
                pool.wait_ge(ch_step, b + 1)
                nc.gpsimd.tensor_tensor(ch[n][:, 1], ctx[n][:], ch[n][:, 0], ALU.subtract).then_inc(ch_ok, 1)

            rstd_of(0)
            split_ctx(0, 0)
            rstd_of(1)
            for c in (-2, -1, 0):
                split_ctx(0, c + 3)
            with pool.Fori(0, 4, 1) as r:
                for c in (1, 2, 3):
                    split_ctx(r, c + 3)
            for c in (1, 2, 3, 4):
                split_ctx(4, c + 3)
            rstd_of(2)

            def split_experts(u, n, it):
                pool.wait_ge(we_loaded[n], 48 * (it + 1))
                if not (isinstance(u, int) and u < 2):
                    pool.wait_ge(h_psum, 2 * u - 2)
                nc.gpsimd.tensor_tensor(wh[n][:, 0:2], wf[n][:, 0:2], zero[:].to_broadcast([128, 2, 128]), ALU.add
                                        ).then_inc(wh_step, 1)
                pool.wait_ge(wh_step, u + 1)
                nc.gpsimd.tensor_tensor(wh[n][:, 2:4], wf[n][:, 0:2], wh[n][:, 0:2], ALU.subtract
                                        ).then_inc(wh_ok, 1)

            split_experts(0, 0, 0)
            split_experts(1, 1, 0)
            with pool.Fori(1, NP // 2, 1) as r:
                split_experts(2 * r, 0, r)
                split_experts(2 * r + 1, 1, r)
            split_experts(NP, 0, NP // 2)

        @block.tensor
        def _(pe):
            mm, tr = nc.tensor.matmul, nc.tensor.transpose

            pe.wait_ge(const_ok, 1)
            pe.wait_ge(w_loaded, 13 * 16)
            for half in range(2):
                for n in range(4):
                    last = tr(ps[:, half, 128 * n:128 * n + 128], wnat[:, 4 * half + n], ident[:])
                last.then_inc(wt_psum, 1)

            def transpose_norm(n):
                for half, (a, z) in enumerate((XA, XB)):
                    pe.wait_ge(xn_ok, TT * n + z // 128)
                    for j in range(a // 128, z // 128):
                        last = tr(ps[:, 2 + half, 128 * j - a:128 * j - a + 128], xn[:, j], ident[:])
                    last.then_inc(xt_psum, 1)

            def project(weight, banks, done):
                for half in range(2):
                    cols = slice(HALF * half, HALF * half + HALF)
                    split_matmul(ps[:, banks + half, 0:HALF], wt1[:, weight], wt2[:, weight],
                                 xt1[:, cols], xt2[:, cols]).then_inc(done, 1)

            transpose_norm(0)
            pe.wait_ge(wt2_ok, 2)
            pe.wait_ge(xt2_ok, 2)
            project(SELF_W + 1, 0, k_psum)
            project(SELF_W, 4, q_psum)
            pe.wait_ge(bias_step, 2)
            for b in range(B):
                last = tr(ps[0:KT, (2, 3, 6, 7)[b // 4], 128 * (b % 4):128 * (b % 4) + KP],
                          bh32[:, b], ident[0:KP, 0:KP])
            last.then_inc(bt_psum, 1)

            pe.wait_ge(qs_ok, 12 * 16)
            pe.wait_ge(kself_ok, 12 * 16)
            def self_maxima(r):
                for k in range(2):
                    b = 2 * r + k
                    if not (isinstance(r, int) and r == 0):
                        pe.wait_ge(mself_ok, 2 * r)
                    for pair in range(8):
                        last = mm(mbank[k][0:112, S * pair:S * pair + S],
                                  qs[0:ROWS, bass.ds(b, 1), 2 * pair:2 * pair + 2, :].rearrange("p o h q -> p (o h q)"),
                                  kself[0:ROWS, pair // 2, bass.ds(S * b, S)], start=True, stop=True)
                    last.then_inc(mself_psum, 1)

            self_maxima(0)
            with pe.Fori(1, B // 2, 1) as r:
                self_maxima(r)
            pe.wait_ge(mself_ok, B)
            tr(ps[:, 0, 0:112], mself[:].rearrange("p b k -> p (b k)"), ident[0:112, 0:112]).then_inc(mselft_psum, 1)
            pe.wait_ge(mselfr_ok, 1)
            pe.wait_ge(mself_row, 16)

            def times_v(vt, pt, keys, first, last_):
                for quad in range(4):
                    mm(obank[32 * quad:32 * quad + 32, 0:168], vt[0:keys, 27 * quad:27 * quad + 32],
                       pt[0:keys, 168 * quad:168 * quad + 168], start=first, stop=last_, skip_group_check=True)
                for quad in range(4):
                    done = mm(obank[32 * quad:32 * quad + 32, 168:224], vt[0:keys, 108 + 9 * quad:140 + 9 * quad],
                              pt[0:keys, 672 + S * quad:672 + S * quad + S], start=False, stop=last_,
                              skip_group_check=True)
                done.then_inc(pv_done, 1)

            def pick_heads():
                for k in range(4):
                    last = mm(misc[0:S, 36 * k:36 * k + 36], osb[:, S * k:S * k + S],
                              pick[:, k % 3].rearrange("p a b -> p (a b)"), start=True, stop=True)
                last.then_inc(misc_done, 1)

            def self_step(r, c):
                j, k = 2 * r + c, c % 2
                if self_live(r, c):
                    tokens = bass.ds(S * j, S)
                    if not (isinstance(r, int) and j < 2):
                        pe.wait_ge(exp_done, j - 1)
                    for g in range(G):
                        last = mm(sbank[k][0:S, g // 2, 224 * (g % 2):224 * (g % 2) + 224],
                                  kself[0:ROWS, g, tokens],
                                  qs[0:ROWS, bass.ds(j, 1), HG * g:HG * g + HG, :].rearrange("p o h q -> p (o h q)"),
                                  start=True, stop=True)
                    last.then_inc(st_done, 1)
                    pe.wait_ge(misc_read, self_index(r, c, "V"))
                    mm(misc[0:S, 0:D], xt1[:, tokens], wt1[:, SELF_W + 2], start=True, stop=False)
                    mm(misc[0:S, 0:D], xt1[:, tokens], wt2[:, SELF_W + 2], start=False, stop=False)
                    mm(misc[0:S, 0:D], xt2[:, tokens], wt1[:, SELF_W + 2], start=False, stop=True
                       ).then_inc(misc_done, 1)
                if self_live(r, c - 3):
                    pe.wait_ge(misc_read, self_index(r, c, "tr"))
                    tr(misc[:, 0:128], tok[:], ident[:]).then_inc(misc_done, 1)
                if self_live(r, c - 2):
                    pe.wait_ge(misc_read, self_index(r, c, "sel"))
                    pe.wait_ge(o_read, j - 1)
                    pick_heads()
                if self_live(r, c - 1):
                    pe.wait_ge(misc_read, self_index(r, c - 1, "V") + 1)
                    pe.wait_ge(exp_done, j)
                    if not (isinstance(r, int) and j < 2):
                        pe.wait_ge(o_read, j - 1)
                    times_v(v[1 - k][:, 0], p[1 - k], KP, True, True)

            pe.wait_ge(brow_ok, 1)
            for c in (0, 1, 2):
                self_step(0, c)
            with pe.Fori(0, 6, 1) as r:
                for c in (3, 4):
                    self_step(r, c)
            for c in (3, 4, 5, 6):
                self_step(6, c)

            def out_project(n):
                for half, (a, z) in enumerate((XA, XB)):
                    for j in range(a // 128, z // 128):
                        last = mm(ps[:, half, 128 * j - a:128 * j - a + 128], attn[:, 128 * j:128 * j + 128],
                                  wt32[:, n], start=True, stop=True)
                    last.then_inc(o_psum, 1)

            pe.wait_ge(misc_read, SELF_MISC)
            out_project(0)

            transpose_norm(1)
            pe.wait_ge(xt2_ok, 4)
            project(CROSS_W, 4, q_psum)

            def misc_use(r, c, use):
                pe.wait_ge(misc_read, misc_index(r, c, use))

            def ctx_transpose(r, c, j):
                misc_use(r, c, f"T{j}")
                pe.wait_ge(ch_ok, 3 * r + c + 3)
                for part in range(2):
                    for t in range(4):
                        o = 512 * part + 128 * t
                        last = tr(misch[:, o:o + 128], ch[(c + 2) % 3][:, part, 4 * j + t], identh[:])
                last.then_inc(misc_done, 1)

            def key_project(r, c, j):
                misc_use(r, c, f"K{j}")
                pe.wait_ge(misc_read, misc_index(r, c, f"T{j}") + 1)
                c1, c2 = ct[:, 0, 4 * j:4 * j + 4, 0:KP], ct[:, 1, 4 * j:4 * j + 4, 0:KP]
                out = misc[:, 0:CH].rearrange("p (t k) -> p t k", t=4)
                split_matmul(out, wt1[:, CROSS_W + 1], wt2[:, CROSS_W + 1], c1, c2).then_inc(misc_done, 1)

            def value_project(r, c, j):
                misc_use(r, c, f"V{j}")
                for t in range(4):
                    last = split_matmul(misc[0:KP, 128 * t:128 * t + 128],
                                        ct[:, 0, 4 * j + t, 0:KP], ct[:, 1, 4 * j + t, 0:KP],
                                        wt1[:, CROSS_W + 2], wt2[:, CROSS_W + 2])
                last.then_inc(misc_done, 1)

            def max_chunk(r, c, off, k):
                b, n = 3 * r + c + off, (c + off) % 3
                pair, part = k // 3, k % 3
                if k == 0:
                    pe.wait_ge(first_ok[n], 16 * NFIRST * (r + (c + off) // 3 + 1))
                if k == 6:
                    pe.wait_ge(rest_ok[n], 16 * NREST * (r + (c + off) // 3 + 1))
                if not (isinstance(r, int) and NCH * b + k < 2):
                    pe.wait_ge(mx_read, NCH * b + k - 1)
                mm(mbank[k % 2][0:112, 0:CH], qsb[n][0:ROWS, 2 * pair:2 * pair + 2].rearrange("p h q -> p (h q)"),
                   ks[n][0:ROWS, pair // 2, CH * part:CH * part + CH], start=True, stop=True).then_inc(mx_psum, 1)

            def pv_tile(r, c, t):
                tile = B + KT * (3 * r + c) + t
                pe.wait_ge(exp_done, tile + 1)
                if t == 0:
                    pe.wait_ge(misc_read, misc_index(r, c - 2, "V2") + 1)
                    pe.wait_ge(o_read, B + 3 * r + c)
                times_v(v[c % 3][:, t], p[t % 2], KP, t == 0, t == KT - 1)

            def iteration(r, c):
                for s in range(KT):
                    if live(r, c):
                        if s == 0:
                            pe.wait_ge(mrow_in[c % 3], 16 * (r + c // 3 + 1))
                        pe.wait_ge(exp_done, B + KT * (3 * r + c) + s - 1)
                        for g in range(G):
                            last = mm(sbank[s % 2][0:KP, g // 2, 224 * (g % 2):224 * (g % 2) + 224],
                                      ks[c % 3][0:ROWS, g, KP * s:KP * s + KP],
                                      qsb[c % 3][0:ROWS, HG * g:HG * g + HG].rearrange("p h q -> p (h q)"),
                                      start=True, stop=True)
                        last.then_inc(st_done, 1)
                    if s == 0 and live(r, c - 1):
                        pv_tile(r, c - 1, KT - 1)
                    if s > 0 and live(r, c):
                        pv_tile(r, c, s - 1)
                    for off, k in chunks(s):
                        if live(r, c + off):
                            max_chunk(r, c, off, k)
                    for use in [MISC[s]]:
                        if not live(r, c + OFFSET[use[0]]):
                            continue
                        if use[0] == "T":
                            ctx_transpose(r, c, int(use[1]))
                        elif use[0] == "K":
                            key_project(r, c, int(use[1]))
                        elif use[0] == "V":
                            value_project(r, c, int(use[1]))
                        elif use == "sel":
                            misc_use(r, c, use)
                            pe.wait_ge(o_read, B + 3 * r + c)
                            pick_heads()
                        elif use == "tr":
                            misc_use(r, c, use)
                            tr(misc[:, 0:128], tok[:], ident[:]).then_inc(misc_done, 1)
                        else:
                            misc_use(r, c, use)
                            pe.wait_ge(mcol_ok, 3 * r + c + 2)
                            tr(misc[0:8, 0:112], mcol[:], ident[0:112, 0:112]).then_inc(misc_done, 1)

            for c in (-2, -1, 0):
                iteration(0, c)
            with pe.Fori(0, 4, 1) as r:
                for c in (1, 2, 3):
                    iteration(r, c)
            for c in (1, 2, 3, 4):
                iteration(4, c)

            pe.wait_ge(misc_read, misc_index(4, 4, "tr") + 1)
            out_project(1)

            transpose_norm(2)
            pe.wait_ge(xt1_ok, 6)
            for j in range(TT):
                last = mm(ps[:, 7, NE * j:NE * j + NE], xt32[:, 128 * j:128 * j + 128], wg_sb[:],
                          start=True, stop=True)
            last.then_inc(lg_psum, 1)

            hb = [[ps[:, 3 * n + k, 0:HALF] for k in range(3)] for n in range(2)]
            yb = [ps[:, 6, 0:HALF], ps[:, 7, 0:HALF]]

            def hidden(u, n, half, pr):
                step = 2 * u + half
                cols = slice(HALF * half, HALF * half + HALF)
                if not (isinstance(u, int) and u == 0):
                    pe.wait_ge(u_ok, step - 1)
                if half == 0:
                    pe.wait_ge(wh_ok, u + 1)
                for k in range(2):
                    last = split_matmul(hb[half][k], wh[n][:, k], wh[n][:, 2 + k], xt1[:, cols], xt2[:, cols])
                if pr is not None:
                    last = mm(hb[half][2], pairsel[:, bass.ds(pr, 1)].rearrange("p o e h -> p (o e h)"),
                              gt[:, cols], start=True, stop=True)
                last.then_inc(h_psum, 1)

            def down(u, n, half, first=False, final=False):
                pe.wait_ge(u_ok, 2 * u + half + 1)
                mm(yb[half], wf[n][:, 2], u_sb[half], start=first, stop=final,
                   skip_group_check=True).then_inc(y_done, 1)

            pe.wait_ge(xt2_ok, 6)
            hidden(0, 0, 0, None)
            hidden(0, 0, 1, None)
            pe.wait_ge(rt_step, 11)
            for j in range(TT):
                for k in range(j):
                    mm(ps[:, 2, NE * j:NE * j + NE], ones_h[:], chosen_h[:, k], start=(k == 0), stop=False)
                last = mm(ps[:, 2, NE * j:NE * j + NE], before[:], chosen_h[:, j], start=(j == 0), stop=True)
            last.then_inc(rank_psum, 1)
            down(0, 0, 0, first=True)
            down(0, 0, 1, first=True)
            pe.wait_ge(rt_step, 14)
            for j in range(TT):
                last = tr(ps[0:64, 5, :].bitcast(F16)[:, 128 * j:128 * j + 128], gpair[:, j], identh[:])
            last.then_inc(gt_psum, 1)
            pe.wait_ge(gt_ok, 1)
            hidden(1, 1, 0, 0)
            hidden(1, 1, 1, 0)
            with pe.Fori(1, NP // 2, 1) as r:
                for k in range(2):
                    u, n = 2 * r + k, k
                    down(u - 1, 1 - n, 0)
                    hidden(u, n, 0, u - 1)
                    down(u - 1, 1 - n, 1)
                    hidden(u, n, 1, u - 1)
            down(NP - 1, 1, 0)
            hidden(NP, 0, 0, NP - 1)
            down(NP - 1, 1, 1)
            hidden(NP, 0, 1, NP - 1)
            down(NP, 0, 0, final=True)
            down(NP, 0, 1, final=True)
            for half, (a, z) in enumerate((XA, XB)):
                pe.wait_ge(yt_ok, 2)
                for j in range(a // 128, z // 128):
                    last = tr(ps[:, half, 128 * j - a:128 * j - a + 128], yt[:, 128 * j:128 * j + 128], ident[:])
                last.then_inc(yt_psum, 1)

        @block.scalar
        def _(act):
            A = nc.scalar.activation
            for half in range(2):
                act.wait_ge(wt_psum, half + 1)
                src = ps[:, half, :].rearrange("p (n e) -> p n e", n=4)
                A(wt32[:, half], src[:, 3], ACT.Copy)
                A(wt1[:, 4 * half:4 * half + 4], src, ACT.Copy).then_inc(wt1_ok, 1)

            def norm_out(n):
                for half, (a, z) in enumerate((XA, XB)):
                    act.wait_ge(xt_psum, 2 * n + half + 1)
                    if n == 2:
                        A(xt32[:, a:z], ps[:, 2 + half, 0:z - a], ACT.Copy)
                    A(xt1[:, a:z], ps[:, 2 + half, 0:z - a], ACT.Copy).then_inc(xt1_ok, 1)

            def second_queries(n):
                act.wait_ge(q2_ok, 2 * n + 2)
                act.wait_ge(mask_ok, 1)
                act.wait_ge(qs_ok, 12 * 16 * n) if n else None
                for h in range(HG):
                    A(qd[1][:, :, h, :], q2[:].rearrange("p (b q) -> p b q", b=B), ACT.Copy,
                      scale=headmask[:, h:h + 1]).then_inc(qd_ok, 1)

            norm_out(0)
            act.wait_ge(w_loaded, 13 * 16)
            for half in range(2):
                act.wait_ge(k_psum, half + 1)
                A(k12[:, 0, HALF * half:HALF * half + HALF], ps[:, half, 0:HALF], ACT.Identity,
                  bias=bq[:, 1:2]).then_inc(ks1_ok, 1)
            for half in range(2):
                act.wait_ge(q_psum, half + 1)
                A(q1[:, HALF * half:HALF * half + HALF], ps[:, 4 + half, 0:HALF], ACT.Identity,
                  bias=bq[:, 0:1]).then_inc(q1_ok, 1)
            act.wait_ge(zero_ok, 2)
            second_queries(0)
            act.wait_ge(bt_psum, 1)
            for k, bank in enumerate((2, 3, 6, 7)):
                last = A(brow[:, 4 * k:4 * k + 4, :],
                         ps[0:KT, bank, :].rearrange("p (b k) -> p b k", b=4)[:, :, 0:KP], ACT.Copy)
            last.then_inc(brow_ok, 1)
            act.wait_ge(mselft_psum, 1)
            A(mrow_self[:], ps[:, 0, 0:112], ACT.Copy, scale=1.0 / BIG).then_inc(mselfr_ok, 1)

            def self_step(r, c):
                j, k = 2 * r + c, c % 2
                if self_live(r, c):
                    act.wait_ge(st_done, j + 1)
                    if not (isinstance(r, int) and j < 2):
                        act.wait_ge(pv_done, j - 1)
                    A(p[k][0:S].rearrange("p (a c) -> p a c", a=2), sbank[k][0:S, :, 0:448], ACT.Exp,
                      scale=SCALE).then_inc(exp_done, 1)
                if self_live(r, c - 3):
                    act.wait_ge(misc_done, self_index(r, c, "tr") + 1)
                    A(attn[:, bass.ds(S * (j - 3), S)], misc[:, 0:S], ACT.Copy).then_inc(misc_read, 1)
                if self_live(r, c - 1):
                    act.wait_ge(pv_done, j)
                    A(osb[:], obank[:, 0:224], ACT.Copy).then_inc(o_read, 1)

            for c in (0, 1, 2):
                self_step(0, c)
            with act.Fori(0, 6, 1) as r:
                for c in (3, 4):
                    self_step(r, c)
            for c in (3, 4, 5, 6):
                self_step(6, c)

            norm_out(1)
            for half in range(2):
                act.wait_ge(q_psum, 2 + half + 1)
                A(q1[:, HALF * half:HALF * half + HALF], ps[:, 4 + half, 0:HALF], ACT.Copy).then_inc(q1_ok, 1)
            second_queries(1)
            act.wait_ge(bias_step, 3)

            def iteration(r, c):
                i = 3 * r + c
                for s in range(KT):
                    if live(r, c):
                        tile = B + KT * i + s
                        act.wait_ge(st_done, tile + 1)
                        act.wait_ge(pv_done, tile - 1)
                        A(p[s % 2][0:KP].rearrange("p (a c) -> p a c", a=2), sbank[s % 2][0:KP, :, 0:448],
                          ACT.Exp, scale=SCALE,
                          bias=bres[:, bass.ds(i, 1), s:s + 1].rearrange("p o t -> p (o t)")).then_inc(exp_done, 1)
                    if s == 0 and live(r, c - 1):
                        act.wait_ge(pv_done, B + KT * i)
                        A(osb[:], obank[:, 0:224], ACT.Copy).then_inc(o_read, 1)
                    for use in [MISC[s]]:
                        if not live(r, c + OFFSET[use[0]]) or use[0] in "Ts" and use != "tr":
                            continue
                        act.wait_ge(misc_done, misc_index(r, c, use) + 1)
                        if use[0] == "K":
                            j = int(use[1])
                            if j == 0 and not (isinstance(r, int) and i == -2):
                                act.wait_ge(first_ok[(c + 1) % 3], 16 * NFIRST * (r + (c + 1) // 3 + 1))
                                act.wait_ge(rest_ok[(c + 1) % 3], 16 * NREST * (r + (c + 1) // 3 + 1))
                            A(k12[:, 0, CH * j:CH * j + CH], misc[:, 0:CH], ACT.Copy).then_inc(k1_ok, 1)
                        elif use[0] == "V":
                            j = int(use[1])
                            A(v[(c + 2) % 3][0:KP, 4 * j:4 * j + 4, 0:H * 9]
                              .rearrange("p t (h e) -> p t h e", h=H)[:, :, :, 0:HD],
                              misc[0:KP, :].rearrange("p (t h e) -> p t h e", t=4, h=H), ACT.Copy
                              ).then_inc(misc_read, 1)
                        elif use == "tr":
                            A(attn[:, bass.ds(S * (i - 1), S)], misc[:, 0:S], ACT.Copy).then_inc(misc_read, 1)
                        else:
                            A(mrow[:], misc[0:8, 0:112], ACT.Copy, scale=1.0 / BIG).then_inc(misc_read, 1)

            for c in (-2, -1, 0):
                iteration(0, c)
            with act.Fori(0, 4, 1) as r:
                for c in (1, 2, 3):
                    iteration(r, c)
            for c in (1, 2, 3, 4):
                iteration(4, c)

            norm_out(2)
            act.wait_ge(rt_step, 2)
            A(prob, logit, ACT.Exp).then_inc(rt_exp, 1)

            def silu(u, half):
                step = 2 * u + half
                act.wait_ge(h_psum, step + 1)
                if not (isinstance(u, int) and u == 0):
                    act.wait_ge(u_ok, step - 1)
                A(act_sb[half], ps[:, 3 * half, 0:HALF], ACT.Silu).then_inc(silu_ok, 1)

            silu(0, 0)
            silu(0, 1)
            with act.Fori(1, NP + 1, 1) as u:
                silu(u, 0)
                silu(u, 1)
            for half in range(2):
                act.wait_ge(y_done, 2 * NP + 1 + half)
                A(yt[:, HALF * half:HALF * half + HALF], ps[:, 6 + half, 0:HALF], ACT.Copy).then_inc(yt_ok, 1)

        @block.vector
        def _(dve):
            V = nc.vector

            def norm(n):
                for j in range(TT):
                    last = V.bn_stats(stats[:, j], xs[:, j])
                last.then_inc(ln_step, 1)
                dve.wait_ge(ln_step, 3 * n + 1)
                for j in range(TT):
                    last = V.bn_aggr(mv[:, j], stats[:, j])
                last.then_inc(ln_step, 1)
                dve.wait_ge(ln_step, 3 * n + 2)
                V.tensor_scalar_add(veps[:], mv[:, :, 1], EPS).then_inc(ln_step, 1)
                dve.wait_ge(rstd_ok, n + 1)
                for j in range(TT):
                    V.tensor_scalar(xn[:, j], xs[:, j], mv[:, j, 0:1], rstd[:, j:j + 1],
                                    ALU.subtract, ALU.mult).then_inc(xn_ok, 1)

            def norm_out(n):
                for half, (a, z) in enumerate((XA, XB)):
                    dve.wait_ge(xt1_ok, 2 * n + half + 1)
                    V.tensor_tensor(xt2[:, a:z], ps[:, 2 + half, 0:z - a], xt1[:, a:z], ALU.subtract
                                    ).then_inc(xt2_ok, 1)

            def first_queries(n):
                dve.wait_ge(q1_ok, 2 * n + 2)
                dve.wait_ge(mask_ok, 1)
                if n:
                    dve.wait_ge(qs_ok, 12 * 16)
                V.tensor_tensor(qd[0], q1[:].rearrange("p (b o q) -> p b o q", b=B, o=1).to_broadcast([128, B, HG, S]),
                                headmask[:].rearrange("p (a h b) -> p a h b", a=1, b=1).to_broadcast([128, B, HG, S]),
                                ALU.mult).then_inc(qd_ok, 1)

            V.memset(qs[96:ROWS], 0.0).then_inc(qs_rows, 1)
            dve.wait_ge(x_loaded, 16)
            norm(0)
            dve.wait_ge(const_ok, 1)
            V.tensor_reduce(headmask[:], grp[:].rearrange("p g h -> p h g"), axis=AX.X, op=ALU.add).then_inc(mask_ok, 1)
            for half in range(2):
                dve.wait_ge(wt1_ok, half + 1)
                V.tensor_tensor(wt2[:, 4 * half:4 * half + 4], ps[:, half, :].rearrange("p (n e) -> p n e", n=4),
                                wt1[:, 4 * half:4 * half + 4], ALU.subtract).then_inc(wt2_ok, 1)
            norm_out(0)
            dve.wait_ge(bias_loaded, 16)
            V.tensor_scalar(bh[:], bcol[:], SQ / BIG, None, ALU.mult).then_inc(bias_step, 1)
            dve.wait_ge(bias_step, 1)
            V.tensor_copy(bh32[:], bh[:]).then_inc(bias_step, 1)
            dve.wait_ge(bias_step, 2)
            V.scalar_tensor_tensor(bres[:].rearrange("p b t -> p (b t)"), bh32[:].rearrange("p b t -> p (b t)"),
                                   -BIG / SQ, bcol[:].rearrange("p b t -> p (b t)"), ALU.mult, ALU.add
                                   ).then_inc(bias_step, 1)
            dve.wait_ge(w_loaded, 13 * 16)
            for half in range(2):
                cols = slice(HALF * half, HALF * half + HALF)
                dve.wait_ge(ks1_ok, half + 1)
                V.scalar_tensor_tensor(k12[:, 1, cols], ps[:, half, 0:HALF], bq[:, 1:2], k12[:, 0, cols],
                                       ALU.add, ALU.subtract).then_inc(ks2_ok, 1)
            for half in range(2):
                cols = slice(HALF * half, HALF * half + HALF)
                dve.wait_ge(q1_ok, half + 1)
                V.scalar_tensor_tensor(q2[:, cols], ps[:, 4 + half, 0:HALF], bq[:, 0:1], q1[:, cols],
                                       ALU.add, ALU.subtract).then_inc(q2_ok, 1)
            first_queries(0)

            with dve.Fori(0, B // 2, 1) as r:
                for k in range(2):
                    b = 2 * r + k
                    dve.wait_ge(mself_psum, b + 1)
                    V.tensor_reduce(mself[:, bass.ds(b, 1), :].rearrange("p o k -> p (o k)"),
                                    mbank[k][0:112, 0:8 * S].rearrange("p (k s) -> p k s", k=8),
                                    axis=AX.X, op=ALU.max, negate=True).then_inc(mself_ok, 1)

            def normalize(batches):
                part = misc[0:S, 0:144].rearrange("p (k a e) -> p k a e", k=4, a=4)
                V.reciprocal(rec[:], part[:, :, :, HD]).then_inc(norm_step, 1)
                dve.wait_ge(norm_step, batches + 1)
                V.tensor_tensor(tok[0:S, 0:96].rearrange("p (a k e) -> p k a e", a=4, k=3), part[:, 0:3, :, 0:HD],
                                rec[:, 0:3, :].rearrange("p k (a o) -> p k a o", o=1).to_broadcast([S, 3, 4, HD]),
                                ALU.mult)
                V.tensor_tensor(tok[0:S, 96:128].rearrange("p (a e) -> p a e", a=4), part[:, 3, :, 0:HD],
                                rec[:, 3, :].rearrange("p (a o) -> p a o", o=1).to_broadcast([S, 4, HD]),
                                ALU.mult).then_inc(misc_read, 1)

            def self_step(r, c):
                j, k = 2 * r + c, c % 2
                if self_live(r, c):
                    dve.wait_ge(misc_done, self_index(r, c, "V") + 1)
                    if not (isinstance(r, int) and j < 2):
                        dve.wait_ge(pv_done, j - 1)
                    V.tensor_tensor(v[k][0:S, 0, 0:H * 9].rearrange("p (h e) -> p h e", h=H)[:, :, 0:HD],
                                    misc[0:S, 0:D].rearrange("p (h e) -> p h e", h=H),
                                    bv[:].rearrange("p (h e) -> p h e", h=H), ALU.add).then_inc(misc_read, 1)
                if self_live(r, c - 2):
                    dve.wait_ge(misc_done, self_index(r, c, "sel") + 1)
                    normalize(j - 2)

            dve.wait_ge(zero_ok, 2)
            for c in (0, 1, 2):
                self_step(0, c)
            with dve.Fori(0, 6, 1) as r:
                for c in (3, 4):
                    self_step(r, c)
            for c in (3, 4, 5, 6):
                self_step(6, c)

            def add_to_x(first_bank, source, before, done, start):
                for half, (a, z) in enumerate(((0, 4), (4, TT))):
                    dve.wait_ge(source, before + half + 1)
                    V.tensor_tensor(xs[:, a:z], xs[:, a:z],
                                    ps[:, half, 0:128 * (z - a)].rearrange("p (j d) -> p j d", d=D), ALU.add
                                    ).then_inc(done, 1)
                dve.wait_ge(done, start + 2)

            V.tensor_tensor(xs[:], xs[:], bp[:].rearrange("p (o d) -> p o d", o=1).to_broadcast([128, TT, D]),
                            ALU.add).then_inc(xb_ok, 1)
            dve.wait_ge(xb_ok, 1)
            dve.wait_ge(st_done, B)
            V.memset(qs[96:ROWS], 0.0).then_inc(xb_ok, 1)
            dve.wait_ge(xb_ok, 2)
            V.memset(qs[96:97], BIG).then_inc(qs_rows, 1)
            add_to_x(0, o_psum, 0, x_ok, 0)
            norm(1)
            norm_out(1)
            for half in range(2):
                cols = slice(HALF * half, HALF * half + HALF)
                dve.wait_ge(q1_ok, 2 + half + 1)
                V.tensor_tensor(q2[:, cols], ps[:, 4 + half, 0:HALF], q1[:, cols], ALU.subtract).then_inc(q2_ok, 1)
            first_queries(1)

            def iteration(r, c):
                i = 3 * r + c
                for s in range(KT):
                    for off, k in chunks(s):
                        if not live(r, c + off):
                            continue
                        b = i + off
                        dve.wait_ge(mx_psum, NCH * b + k + 1)
                        if k == 0 and not (isinstance(r, int) and b == 0):
                            dve.wait_ge(mcol_ok, b)
                        V.tensor_reduce(mx[:, k // 3, k % 3:k % 3 + 1], mbank[k % 2][0:112, 0:CH],
                                        axis=AX.X, op=ALU.max).then_inc(mx_read, 1)
                        if k == NCH - 1:
                            dve.wait_ge(mx_read, NCH * (b + 1))
                            V.tensor_reduce(mcol[:], mx[:], axis=AX.X, op=ALU.max, negate=True).then_inc(mcol_ok, 1)
                    for use in [MISC[s]]:
                        if not live(r, c + OFFSET[use[0]]) or use[0] in "Vm" or use == "tr":
                            continue
                        n = misc_index(r, c, use)
                        dve.wait_ge(misc_done, n + 1)
                        if use == "sel":
                            normalize(B + i - 1)
                            continue
                        j = int(use[1])
                        if use[0] == "T":
                            V.tensor_copy(ct[:, :, 4 * j:4 * j + 4, :],
                                          misch[:, :].rearrange("p (a t k) -> p a t k", a=2, t=4)).then_inc(misc_read, 1)
                        else:
                            dve.wait_ge(k1_ok, 3 * (i + 2) + j + 1)
                            V.tensor_tensor(k12[:, 1, CH * j:CH * j + CH], misc[:, 0:CH],
                                            k12[:, 0, CH * j:CH * j + CH], ALU.subtract).then_inc(misc_read, 1)

            for c in (-2, -1, 0):
                iteration(0, c)
            with dve.Fori(0, 4, 1) as r:
                for c in (1, 2, 3):
                    iteration(r, c)
            for c in (1, 2, 3, 4):
                iteration(4, c)

            add_to_x(1, o_psum, 2, x_ok, 2)
            norm(2)
            norm_out(2)
            steps = [0]

            def step(ins):
                steps[0] += 1
                ins.then_inc(rt_step, 1)
                dve.wait_ge(rt_step, steps[0])

            wide = lambda a: a.rearrange("p (j o) -> p j o", o=1).to_broadcast([128, TT, NE])
            lg = ps[:, 7, 0:TT * NE].rearrange("p (j e) -> p j e", e=NE)
            dve.wait_ge(lg_psum, 1)
            step(V.tensor_reduce(rmax, lg, axis=AX.X, op=ALU.max))
            step(V.tensor_tensor(logit, lg, wide(rmax), ALU.subtract))
            dve.wait_ge(rt_exp, 1)
            step(V.tensor_reduce(rsum, prob, axis=AX.X, op=ALU.add))
            step(V.reciprocal(rrec, rsum))
            step(V.tensor_tensor(prob, prob, wide(rrec), ALU.mult))
            for j in range(TT):
                last = V.max(top8[:, j], prob[:, j])
            step(last)
            for j in range(TT):
                last = V.max_index(idx8[:, j], top8[:, j], prob[:, j])
            step(last)
            step(V.tensor_copy(idxf, idx8))
            step(V.tensor_tensor(eq, idxf[:, :, 0:TOPK].rearrange("p j (k o) -> p j k o", o=1).to_broadcast([128, TT, TOPK, NE]),
                                 expert_no[:].rearrange("p (a b e) -> p a b e", a=1, b=1).to_broadcast([128, TT, TOPK, NE]),
                                 ALU.is_equal))
            step(V.tensor_reduce(chosen, eq.rearrange("p j k e -> p j e k"), axis=AX.X, op=ALU.add))
            V.tensor_copy(chosen_h, chosen)
            step(V.tensor_tensor(gate, prob, chosen, ALU.mult))

            def shared(half):
                dve.wait_ge(silu_ok, half + 1)
                V.tensor_tensor(u_sb[half], ps[:, 3 * half + 1, 0:HALF], act_sb[half], ALU.mult).then_inc(u_ok, 1)

            shared(0)
            shared(1)
            dve.wait_ge(rank_psum, 1)
            step(V.scalar_tensor_tensor(gate, ps[:, 2, 0:TT * NE].rearrange("p (j e) -> p j e", e=NE), float(CAP),
                                        gate, ALU.is_lt, ALU.mult))
            step(V.tensor_copy(gpair[:, :, 0:NE], gate))
            step(V.tensor_tensor(gpair[:, :, NE:64], gate, gpair[:, :, 0:NE], ALU.subtract))
            dve.wait_ge(gt_psum, 1)
            V.tensor_copy(gt, ps[0:64, 5, :].bitcast(F16)[:, 0:T]).then_inc(gt_ok, 1)

            def gated(u, half):
                step = 2 * u + half
                dve.wait_ge(silu_ok, step + 1)
                V.tensor_tensor(mid_sb[half], ps[:, 3 * half + 1, 0:HALF], act_sb[half], ALU.mult).then_inc(mid_ok, 1)
                dve.wait_ge(mid_ok, step - 1)
                dve.wait_ge(y_done, step - 1)
                V.tensor_tensor(u_sb[half], ps[:, 3 * half + 2, 0:HALF], mid_sb[half], ALU.mult).then_inc(u_ok, 1)

            with dve.Fori(1, NP + 1, 1) as u:
                gated(u, 0)
                gated(u, 1)
            add_to_x(0, yt_psum, 0, res_ok, 0)


_INS = ["x", "ctx_1024", "fside_BxS2_0", "L0_attn_qkv_w", "L0_attn_qkv_b", "L0_attn_proj_w", "L0_attn_proj_b",
        "L0_xattn_Wq", "L0_xattn_Wk", "L0_xattn_Wv", "L0_xattn_Wo", "L0_ffn_Wg", "L0_ffn_W1", "L0_ffn_W2",
        "L0_ffn_W3", "L0_ffn_Ws1", "L0_ffn_Ws2", "L0_ffn_Ws3"]


def kernel(**inputs):
    import numpy as _np
    import concourse.bacc as _bacc
    from concourse import mybir as _mybir
    from concourse.bass_utils import run_bass_kernel_spmd as _run

    nc = _bacc.Bacc("TRN2", target_bir_lowering=False, num_devices=1)
    arrays, args = {}, []
    for name in _INS:
        a = _np.ascontiguousarray(inputs[name])
        arrays[f"in_{name}"] = a
        args.append(nc.dram_tensor(f"in_{name}", a.shape, _mybir.dt.from_np(a.dtype), kind="ExternalInput").ap())
    out = nc.dram_tensor("out", (B, S, D), _mybir.dt.float32, kind="ExternalOutput").ap()
    (x, ctx, bias, qkv_w, qkv_b, proj_w, proj_b, wq, wk, wv, wo, wg, w1, w2, w3, ws1, ws2, ws3) = args
    build(nc, x, ctx, bias, qkv_w, qkv_b, proj_w, proj_b, wq, wk, wv, wo, wg, w1, w2, w3, ws1, ws2, ws3, out)
    r = _run(nc, [arrays], core_ids=[0])
    return r.results[0]["out"]
```

```python
from contextlib import ExitStack

import numpy as np
import concourse.bass as bass
from concourse import mybir
from concourse.alu_op_type import AluOpType as ALU

F32 = mybir.dt.float32
F16 = mybir.dt.float16
U32 = mybir.dt.uint32
ACT = mybir.ActivationFunctionType
AX = mybir.AxisListType

B, S, D, H = 16, 56, 128, 16
HD = D // H
NKEY, KT = 1500, 12
KP = NKEY // KT
T = B * S
TT = T // 128
G = 4
HG = H // G
ROWS = 98
BIG = 32768.0
TWO_BIGS = float(np.array([BIG, BIG], np.float16).view(np.float32)[0])
SQ = float(HD) ** 0.5
SCALE = 1.0 / SQ
VW = H * (HD + 1)
NE, TOPK, HE = 32, 4, 64
CAP = 4 * T * TOPK // NE
NP = NE // 2
NW = 4
CH = NKEY // 3
NCH = 24
EPS = 1e-5
HALF = T // 2
NFIRST, NREST = 4, 4 * (G - 1)
QCUT = 4
SELF_ROWS = 97

EARLY = 2
PREP = ["T0", "T1", "T2", "K0", "K1", "K2", "V0", "V1", "V2"]
MISC = ["T0", "K0", "T1", "K1", "T2", "K2", "sel", "V0", "V1", "V2", "mt", "tr"]
OFFSET = {"T": 2, "K": 2, "V": 2, "s": -1, "t": -1, "m": 1}
BEFORE_LOOP = 2 * B


def live(r, c):
    return not isinstance(r, int) or 0 <= 3 * r + c < B


def prep_live(r, c):
    return not isinstance(r, int) or EARLY <= 3 * r + c < B


def used(r, c, use):
    return (prep_live if use[0] in "TKV" else live)(r, c + OFFSET[use[0]])


def misc_index(r, c, use):
    i = 3 * r + c if isinstance(r, int) else c
    n = BEFORE_LOOP + sum(used(0, j, u) for j in range(-2, i) for u in MISC)
    n += [u for u in MISC if used(0, i, u)].index(use)
    return n if isinstance(r, int) else n + 3 * len(MISC) * r


def batch_index(r, c, use):
    return misc_index(r, c - 2, use)


def early(r, c):
    return isinstance(r, int) and 3 * r + c < EARLY


def self_uses(j):
    return [u for u, lag in (("tr", 3), ("sel", 2)) if 0 <= j - lag < B]


def self_index(r, c, use):
    j = 2 * r + c if isinstance(r, int) else c
    n = sum(len(self_uses(k)) for k in range(j)) + self_uses(j).index(use)
    return n if isinstance(r, int) else n + 2 * 2 * r


def self_live(r, c):
    return not isinstance(r, int) or 0 <= 2 * r + c < B


def chunks(s):
    return [(1, 6 + 2 * s + j) if s < 9 else (2, 2 * (s - 9) + j) for j in range(2)]


def build(nc, x_d, ctx_d, bias_d, qkv_w, qkv_b, proj_w, proj_b, wq, wk, wv, wo,
          wg, w1, w2, w3, ws1, ws2, ws3, out_d):
    with ExitStack() as stack:
        sb = lambda n, s, d: stack.enter_context(nc.sbuf_tensor(n, s, d))
        sem = lambda n: stack.enter_context(nc.semaphore(n))

        ident = sb("ident", [128, 128], F32)
        identh = sb("identh", [128, 128], F16)
        grp = sb("grp", [128, G, HG], F32)
        headmask = sb("headmask", [128, HG], F32)
        pick = sb("pick", [128, 3, 4, 9], F32)
        mhalf = sb("mhalf", [128, TT], F32)
        zero = sb("zero", [128, 1, 1], F32)
        ones_h = sb("ones_h", [128, 128], F16)
        before = sb("before", [128, 128], F16)
        pairsel = sb("pairsel", [64, NP, 2, HE], F16)
        expert_no = sb("expert_no", [128, NE], F32)
        wnat = sb("wnat", [128, 8, 128], F32)
        wt32 = sb("wt32", [128, 2, 128], F32)
        wt1 = sb("wt1", [128, 8, 128], F16)
        wt2 = sb("wt2", [128, 8, 128], F16)
        wg_sb = sb("wg_sb", [128, NE], F32)
        bq = sb("bq", [128, 2], F32)
        bv = sb("bv", [S, D], F32)
        bp = sb("bp", [128, D], F32)
        xs = sb("xs", [128, TT, D], F32)
        xn = sb("xn", [128, TT, D], F32)
        stats = sb("stats", [128, TT, 6], F32)
        mv = sb("mv", [128, TT, 2], F32)
        veps = sb("veps", [128, TT], F32)
        rstd = sb("rstd", [128, TT], F32)
        xt1 = sb("xt1", [128, T], F16)
        xt2 = sb("xt2", [128, T], F16)
        q1 = sb("q1", [128, T], F16)
        q2 = sb("q2", [128, T], F16)
        attn = sb("attn", [128, T], F32)
        qs = sb("qs", [SELF_ROWS, B, H, S], F16)
        late = sb("late", [128, 2, T], F32)
        qd = [late[:].rearrange("p a t -> p (a t)").bitcast(F16).rearrange("p (b h q) -> p b h q", b=B, h=HG),
              sb("qd2", [128, B, HG, S], F16)[:]]
        xt32, yt = late[:, 0], late[:, 1]
        qsb = [sb(f"qsb{n}", [128, H, S], F16) for n in range(3)]
        ks = [sb(f"ks{n}", [128, G, NKEY], F16) for n in range(3)]
        kself = ks[2][:, :, 0:T]
        ctx = [sb(f"ctx{n}", [128, KT, D], F32) for n in range(3)]
        ch = [sb(f"ch{n}", [128, 2, KT, D], F16) for n in range(3)]
        ct = sb("ct", [128, 2, KT, 128], F16)
        k12 = sb("k12", [128, 2, NKEY], F16)
        v = [sb(f"v{n}", [128, KT, VW], F32) for n in range(3)]
        bcol = sb("bcol", [KP, B, KT], F32)
        bh = sb("bh", [KP, B, KT], F16)
        bh32 = sb("bh32", [KP, B, KT], F32)
        bres = sb("bres", [KP, B, KT], F32)
        brow = sb("brow", [KT, B, KP], F16)
        p = [sb(f"p{n}", [128, H * S], F32) for n in range(2)]
        mx = sb("mx", [112, 8, 3], F32)
        mcol = sb("mcol", [112, 8], F32)
        mrow = sb("mrow", [8, 112], F16)
        mself = sb("mself", [112, B, 8], F32)
        mrow_self = sb("mrow_self", [128, 112], F16)
        osb = sb("osb", [128, 224], F32)
        rec = sb("rec", [S, 4, 4], F32)
        tok = sb("tok", [128, D], F32)

        flat = lambda t, d, n, o=0: t[:].rearrange("p a b -> p (a b)").bitcast(d)[:, o:o + n]
        wf = [flat(ks[1], F32, 384, 384 * n).rearrange("p (a b) -> p a b", a=3) for n in range(NW)]
        wh = [flat(ks[1], F16, 512, 768 * NW + 512 * n).rearrange("p (a b) -> p a b", a=4) for n in range(NW)]
        act_sb = [flat(v[0], F32, HALF, HALF * n) for n in range(2)]
        mid_sb = [flat(v[1], F32, HALF, HALF * n) for n in range(2)]
        u_sb = [flat(v[2], F32, HALF, HALF * n) for n in range(2)]
        logit = flat(ctx[1], F32, 224).rearrange("p (j e) -> p j e", e=NE)
        prob = flat(ctx[1], F32, 224, 224).rearrange("p (j e) -> p j e", e=NE)
        chosen = flat(ctx[1], F32, 224, 448).rearrange("p (j e) -> p j e", e=NE)
        gate = flat(ctx[1], F32, 224, 672).rearrange("p (j e) -> p j e", e=NE)
        eq = flat(ctx[2], F32, 896).rearrange("p (j k e) -> p j k e", j=TT, k=TOPK)
        top8 = flat(ctx[2], F32, 56, 896).rearrange("p (j k) -> p j k", k=8)
        idx8 = flat(ctx[2], U32, 56, 960).rearrange("p (j k) -> p j k", k=8)
        idxf = flat(ctx[2], F32, 56, 1024).rearrange("p (j k) -> p j k", k=8)
        rmax = flat(ctx[2], F32, TT, 1088)
        rsum = flat(ctx[2], F32, TT, 1096)
        rrec = flat(ctx[2], F32, TT, 1104)
        chosen_h = flat(ks[2], F16, 224).rearrange("p (j e) -> p j e", e=NE)
        gpair = flat(ks[2], F16, 448, 256).rearrange("p (j e) -> p j e", e=64)
        gt = flat(ks[2], F16, T, 1024)[0:64]

        ps = stack.enter_context(nc.psum_tensor("ps", [128, 8, 512], F32))
        sbank = [ps[:, 0:2, :], ps[:, 2:4, :]]
        mbank = [ps[:, 4, :], ps[:, 5, :]]
        misc = ps[:, 6, :]
        obank = ps[:, 7, :]

        ident_ok = sem("ident_ok")
        grp_ok = sem("grp_ok")
        const_ok = sem("const_ok")
        big_ok = sem("big_ok")
        const_step = sem("const_step")
        mask_ok = sem("mask_ok")
        w_loaded = sem("w_loaded")
        b_loaded = sem("b_loaded")
        x_loaded = sem("x_loaded")
        bias_loaded = sem("bias_loaded")
        wt_psum = sem("wt_psum")
        wt1_ok = sem("wt1_ok")
        wt2_ok = sem("wt2_ok")
        ln_step = sem("ln_step")
        rstd_ok = sem("rstd_ok")
        xn_ok = sem("xn_ok")
        xt_psum = sem("xt_psum")
        xt1_ok = sem("xt1_ok")
        xt2_ok = sem("xt2_ok")
        q_psum = sem("q_psum")
        k_psum = sem("k_psum")
        q1_ok = sem("q1_ok")
        q2_ok = sem("q2_ok")
        ks1_ok = sem("ks1_ok")
        ks2_ok = sem("ks2_ok")
        qd_ok = [sem(f"qd_ok{n}") for n in range(2)]
        qs_ok = [sem(f"qs_ok{n}") for n in range(2)]
        qsb_ok = [sem(f"qsb_ok{n}") for n in range(3)]
        vself_psum = sem("vself_psum")
        vself_ok = sem("vself_ok")
        kself_ok = sem("kself_ok")
        mself_psum = sem("mself_psum")
        mself_ok = sem("mself_ok")
        mselft_psum = sem("mselft_psum")
        mselfr_ok = sem("mselfr_ok")
        mself_row = sem("mself_row")
        st_done = sem("st_done")
        exp_done = sem("exp_done")
        pv_done = sem("pv_done")
        o_read = sem("o_read")
        prep_psum = sem("prep_psum")
        prep_read = {u: sem(f"prep_read{u}") for u in "TKV"}
        misc_done = sem("misc_done")
        misc_read = sem("misc_read")
        norm_step = sem("norm_step")
        o_psum = sem("o_psum")
        xb_ok = sem("xb_ok")
        x_ok = sem("x_ok")
        bias_step = sem("bias_step")
        bt_psum = sem("bt_psum")
        brow_ok = sem("brow_ok")
        ctx_loaded = [sem(f"ctx_loaded{n}") for n in range(3)]
        ch_step = sem("ch_step")
        ch_ok = sem("ch_ok")
        k1_ok = sem("k1_ok")
        first_ok = [sem(f"first_ok{n}") for n in range(3)]
        rest_ok = [sem(f"rest_ok{n}") for n in range(3)]
        mrow_in = [sem(f"mrow_in{n}") for n in range(3)]
        mx_psum = sem("mx_psum")
        mx_read = sem("mx_read")
        mcol_ok = sem("mcol_ok")
        ctx_clear = sem("ctx_clear")
        ones_ok = sem("ones_ok")
        o_clear = sem("o_clear")
        clear_ok = sem("clear_ok")

        we_loaded = [sem(f"we_loaded{n}") for n in range(NW)]
        wh_step = sem("wh_step")
        wh_ok = sem("wh_ok")
        lg_psum = sem("lg_psum")
        rt_step = sem("rt_step")
        rt_exp = sem("rt_exp")
        rank_psum = sem("rank_psum")
        gt_psum = sem("gt_psum")
        gt_ok = sem("gt_ok")
        h_psum = sem("h_psum")
        silu_ok = sem("silu_ok")
        mid_ok = sem("mid_ok")
        u_ok = sem("u_ok")
        y_done = sem("y_done")
        yt_ok = sem("yt_ok")
        yt_psum = sem("yt_psum")
        res_ok = sem("res_ok")
        out_ok = sem("out_ok")

        XA, XB = (0, 512), (512, T)
        SELF_W, CROSS_W = 0, 4

        def split_matmul(out, a1, a2, b1, b2):
            nc.tensor.matmul(out, a1, b1, start=True, stop=False)
            nc.tensor.matmul(out, a1, b2, start=False, stop=False)
            return nc.tensor.matmul(out, a2, b1, start=False, stop=True)

        def use_filled(r, c, use):
            if early(r, c):
                return prep_psum, len(PREP) * (3 * r + c) + PREP.index(use) + 1
            return misc_done, batch_index(r, c, use) + 1

        def use_read(r, c, use):
            if early(r, c):
                return prep_read[use[0]], 3 * (3 * r + c) + int(use[1]) + 1
            return misc_read, batch_index(r, c, use) + 1

        def use_bank(r, c, j):
            return ps[:, (6, 4, 5)[j], :] if early(r, c) else misc

        block = stack.enter_context(nc.Block())

        @block.sync
        def _(sp):
            sp.dma_start(xs[:], x_d.rearrange("b s d -> (b s) d").rearrange("(j p) d -> p j d", p=128)
                         ).then_inc(x_loaded, 16)
            sp.dma_start(wnat[:, 0:3, :], qkv_w.rearrange("(n p) d -> p n d", n=3)).then_inc(w_loaded, 16)
            for n, w in enumerate((proj_w, wq, wk, wv, wo)):
                sp.dma_start(wnat[:, 3 + n, :], w).then_inc(w_loaded, 16)
            qb = qkv_b.rearrange("(n p a) -> n p a", n=3, a=1)
            for n in range(2):
                sp.dma_start(bq[:, n:n + 1], qb[n]).then_inc(b_loaded, 16)
            row = lambda a: a.rearrange("(o n) -> o n", o=1)
            sp.dma_start(bv[:], row(qkv_b[256:384]).to_broadcast([S, D])).then_inc(b_loaded, 16)
            sp.dma_start(bp[:], row(proj_b).to_broadcast([128, D])).then_inc(b_loaded, 16)
            sp.dma_start(wg_sb[:], wg).then_inc(b_loaded, 16)
            sp.dma_start(bcol[:], bias_d.rearrange("b (p t) -> p b t", t=KT)).then_inc(bias_loaded, 16)

            def load_ctx(r, c):
                if not live(r, c):
                    return
                if not isinstance(r, int) or 3 * r + c >= 3:
                    sp.wait_ge(ch_ok, 3 * r + c - 2)
                else:
                    sp.wait_ge(ctx_clear, 1)
                sp.dma_start(ctx[c % 3][0:KP], ctx_d[3 * r + c].rearrange("(p t) d -> p t d", t=KT)
                             ).then_inc(ctx_loaded[c % 3], 16)

            for c in range(3):
                load_ctx(0, c)

            def query_stacks(n, k):
                a, z = ((0, QCUT), (QCUT, B))[k]
                sp.wait_ge(qd_ok[k], 5 * n + 5)
                for g in range(G):
                    for row0, part in ((0, 0), (32, 0), (64, 1)):
                        sp.dma_start(qs[row0:row0 + 32, a:z, HG * g:HG * g + HG, :],
                                     qd[part][32 * g:32 * g + 32, a:z]).then_inc(qs_ok[k], 16)

            def key_stacks(r, c):
                n, b = c % 3, 3 * r + c
                for g in range(G):
                    sp.dma_start(ks[n][96:97, g, :].rearrange("o (t k) -> o t k", t=KT),
                                 brow[:, bass.ds(b, 1), :]).then_inc((rest_ok if g else first_ok)[n], 16)
                sp.wait_ge(*use_read(r, c, "K2"))
                for g in range(G):
                    for row0, part in ((0, 0), (32, 1), (64, 0)):
                        sp.dma_start(ks[n][row0:row0 + 32, g, :], k12[32 * g:32 * g + 32, part, :]
                                     ).then_inc((rest_ok if g else first_ok)[n], 16)

            sp.wait_ge(ks2_ok, 2)
            for g in range(G):
                for row0, part in ((0, 0), (32, 1), (64, 0)):
                    sp.dma_start(kself[row0:row0 + 32, g, :], k12[32 * g:32 * g + 32, part, 0:T]
                                 ).then_inc(kself_ok, 16)
            query_stacks(0, 0)
            query_stacks(0, 1)
            sp.wait_ge(brow_ok, 1)
            sp.wait_ge(big_ok, 1)
            for c in range(EARLY):
                key_stacks(0, c)
            sp.wait_ge(mselfr_ok, 1)
            sp.dma_start(qs[96:97].rearrange("o b (k h) q -> o (b k) (h q)", k=8), mrow_self[:]
                         ).then_inc(mself_row, 16)

            sp.wait_ge(st_done, B)
            query_stacks(1, 0)

            def iteration(r, c):
                if prep_live(r, c + 3) and (not isinstance(r, int) or 3 * r + c >= 0):
                    load_ctx(r, c + 3)
                n, b = (c + 2) % 3, 3 * r + c + 2
                if live(r, c + 2):
                    sp.wait_ge(qs_ok[0 if isinstance(r, int) and b < QCUT else 1], 2 * 12 * 16)
                    if prep_live(r, c + 2):
                        sp.wait_ge(st_done, B + KT * (b - 2))
                    sp.dma_start(qsb[n][0:96], qs[0:96, bass.ds(b, 1)].rearrange("p o h q -> p (o h) q")
                                 ).then_inc(qsb_ok[n], 16)
                if prep_live(r, c + 2):
                    key_stacks(r, c + 2)
                if live(r, c + 1):
                    sp.wait_ge(misc_read, misc_index(r, c, "mt") + 1)
                    sp.dma_start(qsb[(c + 1) % 3][97:98].rearrange("o (k h) q -> o k (h q)", k=8), mrow[:]
                                 ).then_inc(mrow_in[(c + 1) % 3], 16)

            for c in (-2, -1):
                iteration(0, c)
            query_stacks(1, 1)
            iteration(0, 0)
            with sp.Fori(0, 4, 1) as r:
                for c in (1, 2, 3):
                    iteration(r, c)
            for c in (1, 2, 3, 4):
                iteration(4, c)

            def load_experts(n, a, b_, c_):
                for k, w in enumerate((a, b_, c_)):
                    dst = wf[n][:, k, :]
                    sp.dma_start(dst.rearrange("p (e h) -> p e h", e=2) if k < 2 and len(w.shape) == 3 else dst, w
                                 ).then_inc(we_loaded[n], 16)

            sp.wait_ge(st_done, B + KT * (B - 2))
            load_experts(0, ws1, ws3, ws2)
            w1v = w1.rearrange("(n e) d h -> n d e h", e=2)
            w3v = w3.rearrange("(n e) d h -> n d e h", e=2)
            w2v = w2.rearrange("(n e) h d -> n (e h) d", e=2)

            def load_pair(u, n):
                if not isinstance(u, int) or u >= NW:
                    sp.wait_ge(y_done, 2 * (u - NW) + 2)
                load_experts(n, w1v[u - 1], w3v[u - 1], w2v[u - 1])

            for u in range(1, NW):
                load_pair(u, u)
            with sp.Fori(1, NP // NW, 1) as r:
                for n in range(NW):
                    load_pair(NW * r + n, n)
            load_pair(NP, 0)

            outv = out_d.rearrange("b s d -> (b s) d").rearrange("(j p) d -> p j d", p=128)
            sp.wait_ge(res_ok, 1)
            sp.dma_start(outv[:, 0:4], xs[:, 0:4]).then_inc(out_ok, 16)
            sp.wait_ge(res_ok, 2)
            sp.dma_start(outv[:, 4:7], xs[:, 4:7]).then_inc(out_ok, 16)
            sp.wait_ge(out_ok, 32)

        @block.gpsimd
        def _(pool):
            steps = [0]

            def step(ins):
                steps[0] += 1
                ins.then_inc(const_step, 1)
                pool.wait_ge(const_step, steps[0])

            memset, select = nc.gpsimd.memset, nc.gpsimd.affine_select
            memset(mhalf[:], -0.5)
            memset(zero[:], 0.0)
            memset(grp[:], 1.0)
            step(memset(ident[:], 0.0))
            step(select(out=ident[:], in_=ident[:], compare_op=ALU.not_equal, fill=1.0, base=0,
                        pattern=[[-1, 128]], channel_multiplier=1))
            nc.gpsimd.tensor_copy(identh[:], ident[:]).then_inc(ident_ok, 1)
            step(select(out=grp[:], in_=grp[:], compare_op=ALU.is_ge, fill=0.0, base=0,
                        pattern=[[-32, G], [-HD, HG]], channel_multiplier=1))
            select(out=grp[:], in_=grp[:], compare_op=ALU.is_ge, fill=0.0, base=HD - 1,
                   pattern=[[32, G], [HD, HG]], channel_multiplier=-1).then_inc(grp_ok, 1)
            pool.wait_ge(grp_ok, 1)
            for n in range(3):
                last = memset(ctx[n][96:128], 0.0)
            last.then_inc(ctx_clear, 1)
            pool.wait_ge(ctx_clear, 1)

            def rstd_of(n):
                pool.wait_ge(ln_step, 3 * n + 3)
                nc.gpsimd.tensor_tensor(rstd[:], veps[:], mhalf[:], ALU.pow).then_inc(rstd_ok, 1)

            def split_ctx(r, c):
                if not live(r, c):
                    return
                n, b = c % 3, 3 * r + c
                pool.wait_ge(ctx_loaded[n], 16 * (r + c // 3 + 1))
                if not isinstance(r, int) or b >= 3:
                    if isinstance(r, int):
                        pool.wait_ge(*use_filled(r, c - 3, "T2"))
                    else:
                        pool.wait_ge(misc_done, misc_index(r, c - 4, "T0"))
                nc.gpsimd.tensor_tensor(ch[n][:, 0], ctx[n][:], zero[:].to_broadcast([128, KT, D]), ALU.add
                                        ).then_inc(ch_step, 1)
                pool.wait_ge(ch_step, b + 1)
                nc.gpsimd.tensor_tensor(ch[n][:, 1], ctx[n][:], ch[n][:, 0], ALU.subtract).then_inc(ch_ok, 1)

            rstd_of(0)
            pool.wait_ge(rstd_ok, 1)
            step(memset(ks[2][96:ROWS].rearrange("p g k -> p (g k)").bitcast(F32), TWO_BIGS))
            split_ctx(0, 0)
            pool.wait_ge(ch_ok, 1)
            for n in range(2):
                memset(ks[n][96:ROWS].rearrange("p g k -> p (g k)").bitcast(F32), TWO_BIGS)
            for n in range(3):
                last = memset(qsb[n][96:97], BIG)
            last.then_inc(big_ok, 1)
            pool.wait_ge(big_ok, 1)
            for n in range(3):
                last = memset(v[n][:], 1.0)
            last.then_inc(ones_ok, 1)
            split_ctx(0, 1)
            step(memset(pick[:], 0.0))
            memset(ones_h[:], 1.0)
            memset(before[:], 1.0)
            memset(pairsel[:], 0.0)
            nc.gpsimd.iota(expert_no[:], pattern=[[1, NE]], base=0, channel_multiplier=0,
                           allow_small_or_imprecise_dtypes=True)
            step(select(out=pick[:], in_=pick[:], compare_op=ALU.not_equal, fill=1.0, base=0,
                        pattern=[[-9, 3], [-32, 4], [-1, 9]], channel_multiplier=1))
            select(out=before[:], in_=before[:], compare_op=ALU.is_gt, fill=0.0, base=0,
                   pattern=[[1, 128]], channel_multiplier=-1)
            for row0 in (0, 32):
                last = select(out=pairsel[:], in_=pairsel[:], compare_op=ALU.not_equal, fill=1.0, base=-row0,
                              pattern=[[-2, NP], [-1, 2], [0, HE]], channel_multiplier=1)
                if row0 == 0:
                    step(last)
            last.then_inc(const_ok, 1)
            rstd_of(1)
            for c in (-1, 0):
                split_ctx(0, c + 3)
            with pool.Fori(0, 4, 1) as r:
                for c in (1, 2, 3):
                    split_ctx(r, c + 3)
            for c in (1, 2, 3, 4):
                split_ctx(4, c + 3)
            def split_experts(u, n, it):
                pool.wait_ge(we_loaded[n], 48 * (it + 1))
                if not isinstance(u, int) or u >= NW:
                    pool.wait_ge(h_psum, 2 * (u - NW) + 2)
                nc.gpsimd.tensor_tensor(wh[n][:, 0:2], wf[n][:, 0:2], zero[:].to_broadcast([128, 2, 128]), ALU.add
                                        ).then_inc(wh_step, 1)
                pool.wait_ge(wh_step, u + 1)
                nc.gpsimd.tensor_tensor(wh[n][:, 2:4], wf[n][:, 0:2], wh[n][:, 0:2], ALU.subtract
                                        ).then_inc(wh_ok, 1)

            for u in range(NW):
                split_experts(u, u, 0)
            rstd_of(2)
            with pool.Fori(1, NP // NW, 1) as r:
                for n in range(NW):
                    split_experts(NW * r + n, n, r)
            split_experts(NP, 0, NP // NW)

        @block.tensor
        def _(pe):
            mm, tr = nc.tensor.matmul, nc.tensor.transpose

            pe.wait_ge(ident_ok, 1)
            pe.wait_ge(w_loaded, 6 * 16)
            for half in range(2):
                for n in range(4):
                    last = tr(ps[:, half, 128 * n:128 * n + 128], wnat[:, 4 * half + n], ident[:])
                last.then_inc(wt_psum, 1)

            def transpose_norm(n):
                for half, (a, z) in enumerate((XA, XB)):
                    pe.wait_ge(xn_ok, TT * n + z // 128)
                    for j in range(a // 128, z // 128):
                        last = tr(ps[:, 2 + half, 128 * j - a:128 * j - a + 128], xn[:, j], ident[:])
                    last.then_inc(xt_psum, 1)

            def project(weight, banks, done):
                for half in range(2):
                    cols = slice(HALF * half, HALF * half + HALF)
                    split_matmul(ps[:, banks + half, 0:HALF], wt1[:, weight], wt2[:, weight],
                                 xt1[:, cols], xt2[:, cols]).then_inc(done, 1)

            def ctx_transpose(r, c, j):
                if not early(r, c):
                    pe.wait_ge(misc_read, batch_index(r, c, f"T{j}"))
                elif 3 * r + c:
                    pe.wait_ge(*use_read(r, c - 1, f"V{j}"))
                pe.wait_ge(ch_ok, 3 * r + c + 1)
                bank = use_bank(r, c, j).bitcast(F16)
                for part in range(2):
                    for t in range(4):
                        o = 512 * part + 128 * t
                        last = tr(bank[:, o:o + 128], ch[c % 3][:, part, 4 * j + t], identh[:])
                last.then_inc(use_filled(r, c, "T0")[0], 1)

            def key_project(r, c, j):
                if early(r, c):
                    pe.wait_ge(*use_read(r, c, f"T{j}"))
                else:
                    pe.wait_ge(misc_read, batch_index(r, c, f"K{j}"))
                c1, c2 = ct[:, 0, 4 * j:4 * j + 4, 0:KP], ct[:, 1, 4 * j:4 * j + 4, 0:KP]
                out = use_bank(r, c, j)[:, 0:CH].rearrange("p (t k) -> p t k", t=4)
                split_matmul(out, wt1[:, CROSS_W + 1], wt2[:, CROSS_W + 1], c1, c2
                             ).then_inc(use_filled(r, c, "K0")[0], 1)

            def value_project(r, c, j):
                if early(r, c):
                    pe.wait_ge(*use_read(r, c, f"K{j}"))
                else:
                    pe.wait_ge(misc_read, batch_index(r, c, f"V{j}"))
                for t in range(4):
                    last = split_matmul(use_bank(r, c, j)[0:KP, 128 * t:128 * t + 128],
                                        ct[:, 0, 4 * j + t, 0:KP], ct[:, 1, 4 * j + t, 0:KP],
                                        wt1[:, CROSS_W + 2], wt2[:, CROSS_W + 2])
                last.then_inc(use_filled(r, c, "V0")[0], 1)

            prepare = {"T": ctx_transpose, "K": key_project, "V": value_project}

            transpose_norm(0)
            pe.wait_ge(wt2_ok, 2)
            pe.wait_ge(xt2_ok, 2)
            project(SELF_W + 1, 0, k_psum)
            project(SELF_W, 4, q_psum)
            def self_maxima(r):
                for k in range(4):
                    b = 4 * r + k
                    if not (isinstance(r, int) and r == 0):
                        pe.wait_ge(mself_ok, b - 3)
                    for pair in range(8):
                        last = mm(ps[0:112, k, S * pair:S * pair + S],
                                  qs[0:96, bass.ds(b, 1), 2 * pair:2 * pair + 2, :].rearrange("p o h q -> p (o h q)"),
                                  kself[0:96, pair // 2, bass.ds(S * b, S)], start=True, stop=True)
                    last.then_inc(mself_psum, 1)

            pe.wait_ge(q2_ok, 2)
            for use in PREP[0:6]:
                prepare[use[0]](0, 0, int(use[1]))
            pe.wait_ge(bias_step, 2)
            for b in range(B):
                last = tr(ps[0:KT, (2, 3, 0, 7)[b // 4], 128 * (b % 4):128 * (b % 4) + KP],
                          bh32[:, b], ident[0:KP, 0:KP])
            last.then_inc(bt_psum, 1)
            for use in PREP[6:]:
                prepare[use[0]](0, 0, int(use[1]))
            pe.wait_ge(brow_ok, 1)
            pe.wait_ge(kself_ok, 12 * 16)
            pe.wait_ge(qs_ok[0], 12 * 16)
            self_maxima(0)
            for use in PREP[0:3]:
                prepare[use[0]](0, 1, int(use[1]))
            pe.wait_ge(qs_ok[1], 12 * 16)
            with pe.Fori(1, B // 4, 1) as r:
                self_maxima(r)
            for use in PREP[3:]:
                prepare[use[0]](0, 1, int(use[1]))
            pe.wait_ge(mself_ok, B)
            tr(ps[:, 0, 0:112], mself[:].rearrange("p b k -> p (b k)"), ident[0:112, 0:112]).then_inc(mselft_psum, 1)
            pe.wait_ge(mselfr_ok, 1)
            pe.wait_ge(mself_row, 16)

            def times_v(vt, pt, keys, first, last_):
                for quad in range(4):
                    mm(obank[32 * quad:32 * quad + 27, 0:168], vt[0:keys, 27 * quad:27 * quad + 27],
                       pt[0:keys, 168 * quad:168 * quad + 168], start=first, stop=last_, skip_group_check=True)
                for quad in range(4):
                    done = mm(obank[32 * quad:32 * quad + 9, 168:224], vt[0:keys, 108 + 9 * quad:117 + 9 * quad],
                              pt[0:keys, 672 + S * quad:672 + S * quad + S], start=False, stop=last_,
                              skip_group_check=True)
                done.then_inc(pv_done, 1)

            def pick_heads():
                for k in range(4):
                    last = mm(misc[0:S, 36 * k:36 * k + 36], osb[:, S * k:S * k + S],
                              pick[:, k % 3].rearrange("p a b -> p (a b)"), start=True, stop=True)
                last.then_inc(misc_done, 1)

            def self_step(r, c):
                j, k = 2 * r + c, c % 2
                if self_live(r, c):
                    tokens = bass.ds(S * j, S)
                    if not (isinstance(r, int) and j < 2):
                        pe.wait_ge(exp_done, j - 1)
                    for g in range(G):
                        last = mm(sbank[k][0:S, g // 2, 224 * (g % 2):224 * (g % 2) + 224],
                                  kself[0:SELF_ROWS, g, tokens],
                                  qs[0:SELF_ROWS, bass.ds(j, 1), HG * g:HG * g + HG, :].rearrange("p o h q -> p (o h q)"),
                                  start=True, stop=True)
                    last.then_inc(st_done, 1)
                    if not (isinstance(r, int) and j < 2):
                        pe.wait_ge(vself_ok, j - 1)
                    mm(mbank[k][0:S, 0:D], xt1[:, tokens], wt1[:, SELF_W + 2], start=True, stop=False)
                    mm(mbank[k][0:S, 0:D], xt1[:, tokens], wt2[:, SELF_W + 2], start=False, stop=False)
                    mm(mbank[k][0:S, 0:D], xt2[:, tokens], wt1[:, SELF_W + 2], start=False, stop=True
                       ).then_inc(vself_psum, 1)
                if self_live(r, c - 3):
                    pe.wait_ge(misc_read, self_index(r, c, "tr"))
                    tr(misc[:, 0:128], tok[:], ident[:]).then_inc(misc_done, 1)
                if self_live(r, c - 1):
                    pe.wait_ge(vself_ok, j)
                    pe.wait_ge(exp_done, j)
                    if not (isinstance(r, int) and j < 2):
                        pe.wait_ge(o_read, j - 1)
                    times_v(v[2][:, 1 - k], p[1 - k], KP, True, True)
                if self_live(r, c - 2):
                    pe.wait_ge(misc_read, self_index(r, c, "sel"))
                    pe.wait_ge(o_read, j - 1)
                    pick_heads()

            pe.wait_ge(const_ok, 1)
            pe.wait_ge(o_clear, 1)
            for c in (0, 1, 2):
                self_step(0, c)
            with pe.Fori(0, 6, 1) as r:
                for c in (3, 4):
                    self_step(r, c)
            for c in (3, 4, 5, 6):
                self_step(6, c)

            def out_project(n):
                for half, (a, z) in enumerate((XA, XB)):
                    for j in range(a // 128, z // 128):
                        last = mm(ps[:, half, 128 * j - a:128 * j - a + 128], attn[:, 128 * j:128 * j + 128],
                                  wt32[:, n], start=True, stop=True)
                    last.then_inc(o_psum, 1)

            pe.wait_ge(misc_read, BEFORE_LOOP)
            out_project(0)

            transpose_norm(1)
            pe.wait_ge(xt2_ok, 4)
            project(CROSS_W, 4, q_psum)

            def max_chunk(r, c, off, k):
                b, n = 3 * r + c + off, (c + off) % 3
                pair, part = k // 3, k % 3
                if k == 0:
                    pe.wait_ge(qsb_ok[n], 16 * (r + (c + off) // 3 + 1))
                    pe.wait_ge(first_ok[n], 16 * NFIRST * (r + (c + off) // 3 + 1))
                if k == 6:
                    pe.wait_ge(rest_ok[n], 16 * NREST * (r + (c + off) // 3 + 1))
                if not (isinstance(r, int) and NCH * b + k < 2):
                    pe.wait_ge(mx_read, NCH * b + k - 1)
                mm(mbank[k % 2][0:112, 0:CH], qsb[n][0:ROWS - 1, 2 * pair:2 * pair + 2].rearrange("p h q -> p (h q)"),
                   ks[n][0:ROWS - 1, pair // 2, CH * part:CH * part + CH], start=True, stop=True).then_inc(mx_psum, 1)

            def pv_tile(r, c, t):
                tile = B + KT * (3 * r + c) + t
                pe.wait_ge(exp_done, tile + 1)
                if t == 0:
                    if isinstance(r, int):
                        pe.wait_ge(*use_read(r, c, "V2"))
                    else:
                        pe.wait_ge(misc_read, misc_index(r, c, "T0"))
                    pe.wait_ge(o_read, B + 3 * r + c)
                times_v(v[c % 3][:, t], p[t % 2], KP, t == 0, t == KT - 1)

            def iteration(r, c):
                for s in range(KT):
                    use = MISC[s]
                    if used(r, c, use):
                        if use[0] in "TKV":
                            prepare[use[0]](r, c + 2, int(use[1]))
                        else:
                            pe.wait_ge(misc_read, misc_index(r, c, use))
                        if use == "sel":
                            pe.wait_ge(o_read, B + 3 * r + c)
                            pick_heads()
                        elif use == "tr":
                            tr(misc[:, 0:128], tok[:], ident[:]).then_inc(misc_done, 1)
                        elif use == "mt":
                            pe.wait_ge(mcol_ok, 3 * r + c + 2)
                            tr(misc[0:8, 0:112], mcol[:], ident[0:112, 0:112]).then_inc(misc_done, 1)
                    if live(r, c):
                        if s == 0:
                            pe.wait_ge(mrow_in[c % 3], 16 * (r + c // 3 + 1))
                        pe.wait_ge(exp_done, B + KT * (3 * r + c) + s - 1)
                        for g in range(G):
                            last = mm(sbank[s % 2][0:KP, g // 2, 224 * (g % 2):224 * (g % 2) + 224],
                                      ks[c % 3][0:ROWS, g, KP * s:KP * s + KP],
                                      qsb[c % 3][0:ROWS, HG * g:HG * g + HG].rearrange("p h q -> p (h q)"),
                                      start=True, stop=True)
                        last.then_inc(st_done, 1)
                    if s == 0 and live(r, c - 1):
                        pv_tile(r, c - 1, KT - 1)
                    if s > 0 and live(r, c):
                        pv_tile(r, c, s - 1)
                    for off, k in chunks(s):
                        if live(r, c + off):
                            max_chunk(r, c, off, k)

            for c in (-2, -1, 0):
                iteration(0, c)
            with pe.Fori(0, 4, 1) as r:
                for c in (1, 2, 3):
                    iteration(r, c)
            for c in (1, 2, 3, 4):
                iteration(4, c)

            pe.wait_ge(misc_read, misc_index(4, 4, "tr") + 1)
            out_project(1)

            transpose_norm(2)
            pe.wait_ge(xt1_ok, 6)
            for j in range(TT):
                last = mm(ps[:, 7, NE * j:NE * j + NE], xt32[:, 128 * j:128 * j + 128], wg_sb[:],
                          start=True, stop=True)
            last.then_inc(lg_psum, 1)

            hb = [[ps[:, 3 * n + k, 0:HALF] for k in range(3)] for n in range(2)]
            yb = [ps[:, 6, 0:HALF], ps[:, 7, 0:HALF]]

            def hidden(u, n, half, pr):
                step = 2 * u + half
                cols = slice(HALF * half, HALF * half + HALF)
                if not (isinstance(u, int) and u == 0):
                    pe.wait_ge(u_ok, step - 1)
                if half == 0:
                    pe.wait_ge(wh_ok, u + 1)
                for k in range(2):
                    last = split_matmul(hb[half][k], wh[n][:, k], wh[n][:, 2 + k], xt1[:, cols], xt2[:, cols])
                if pr is not None:
                    last = mm(hb[half][2], pairsel[:, bass.ds(pr, 1)].rearrange("p o e h -> p (o e h)"),
                              gt[:, cols], start=True, stop=True)
                last.then_inc(h_psum, 1)

            def down(u, n, half, first=False, final=False):
                pe.wait_ge(u_ok, 2 * u + half + 1)
                mm(yb[half], wf[n][:, 2], u_sb[half], start=first, stop=final,
                   skip_group_check=True).then_inc(y_done, 1)

            pe.wait_ge(xt2_ok, 6)
            hidden(0, 0, 0, None)
            hidden(0, 0, 1, None)
            pe.wait_ge(rt_step, 11)
            for j in range(TT):
                for k in range(j):
                    mm(ps[:, 2, NE * j:NE * j + NE], ones_h[:], chosen_h[:, k], start=(k == 0), stop=False)
                last = mm(ps[:, 2, NE * j:NE * j + NE], before[:], chosen_h[:, j], start=(j == 0), stop=True)
            last.then_inc(rank_psum, 1)
            down(0, 0, 0, first=True)
            down(0, 0, 1, first=True)
            pe.wait_ge(rt_step, 14)
            for j in range(TT):
                last = tr(ps[0:64, 5, :].bitcast(F16)[:, 128 * j:128 * j + 128], gpair[:, j], identh[:])
            last.then_inc(gt_psum, 1)
            pe.wait_ge(gt_ok, 1)
            hidden(1, 1, 0, 0)
            hidden(1, 1, 1, 0)

            def unit(u, n):
                down(u - 1, (n - 1) % NW, 0)
                hidden(u, n, 0, u - 1)
                down(u - 1, (n - 1) % NW, 1)
                hidden(u, n, 1, u - 1)

            for u in range(2, NW):
                unit(u, u)
            with pe.Fori(1, NP // NW, 1) as r:
                for n in range(NW):
                    unit(NW * r + n, n)
            unit(NP, 0)
            down(NP, 0, 0, final=True)
            down(NP, 0, 1, final=True)
            for half, (a, z) in enumerate((XA, XB)):
                pe.wait_ge(yt_ok, 2)
                for j in range(a // 128, z // 128):
                    last = tr(ps[:, half, 128 * j - a:128 * j - a + 128], yt[:, 128 * j:128 * j + 128], ident[:])
                last.then_inc(yt_psum, 1)

        @block.scalar
        def _(act):
            A = nc.scalar.activation
            for half in range(2):
                act.wait_ge(wt_psum, half + 1)
                src = ps[:, half, :].rearrange("p (n e) -> p n e", n=4)
                A(wt32[:, half], src[:, 3], ACT.Copy)
                A(wt1[:, 4 * half:4 * half + 4], src, ACT.Copy).then_inc(wt1_ok, 1)

            def norm_out(n):
                for half, (a, z) in enumerate((XA, XB)):
                    act.wait_ge(xt_psum, 2 * n + half + 1)
                    if n == 2:
                        A(xt32[:, a:z], ps[:, 2 + half, 0:z - a], ACT.Copy)
                    A(xt1[:, a:z], ps[:, 2 + half, 0:z - a], ACT.Copy).then_inc(xt1_ok, 1)

            def second_queries(n):
                act.wait_ge(q2_ok, 2 * n + 2)
                act.wait_ge(mask_ok, 1)
                if n:
                    for k in range(2):
                        act.wait_ge(qs_ok[k], 12 * 16)
                for k, (a, z) in enumerate(((0, QCUT), (QCUT, B))):
                    for h in range(HG):
                        A(qd[1][:, a:z, h, :], q2[:].rearrange("p (b q) -> p b q", b=B)[:, a:z], ACT.Copy,
                          scale=headmask[:, h:h + 1]).then_inc(qd_ok[k], 1)

            norm_out(0)
            act.wait_ge(b_loaded, 5 * 16)
            for half in range(2):
                act.wait_ge(k_psum, half + 1)
                A(k12[:, 0, HALF * half:HALF * half + HALF], ps[:, half, 0:HALF], ACT.Identity,
                  bias=bq[:, 1:2]).then_inc(ks1_ok, 1)
            for half in range(2):
                act.wait_ge(q_psum, half + 1)
                A(q1[:, HALF * half:HALF * half + HALF], ps[:, 4 + half, 0:HALF], ACT.Identity,
                  bias=bq[:, 0:1]).then_inc(q1_ok, 1)
            second_queries(0)
            def take_keys(r, c, j):
                act.wait_ge(*use_filled(r, c, f"K{j}"))
                if j == 0:
                    if isinstance(r, int) and 3 * r + c == 0:
                        act.wait_ge(kself_ok, 12 * 16)
                    else:
                        act.wait_ge(first_ok[(c - 1) % 3], 16 * NFIRST * (r + (c - 1) // 3 + 1))
                        act.wait_ge(rest_ok[(c - 1) % 3], 16 * NREST * (r + (c - 1) // 3 + 1))
                A(k12[:, 0, CH * j:CH * j + CH], use_bank(r, c, j)[:, 0:CH], ACT.Copy).then_inc(k1_ok, 1)

            def take_values(r, c, j):
                act.wait_ge(*use_filled(r, c, f"V{j}"))
                A(v[c % 3][0:KP, 4 * j:4 * j + 4, :].rearrange("p t (h e) -> p t h e", h=H)[:, :, :, 0:HD],
                  use_bank(r, c, j)[0:KP, :].rearrange("p (t h e) -> p t h e", t=4, h=H), ACT.Copy
                  ).then_inc(use_read(r, c, "V0")[0], 1)

            take = {"K": take_keys, "V": take_values}
            for use in PREP[3:6]:
                take[use[0]](0, 0, int(use[1]))
            act.wait_ge(bt_psum, 1)
            for k, bank in enumerate((2, 3, 0, 7)):
                last = A(brow[:, 4 * k:4 * k + 4, :],
                         ps[0:KT, bank, :].rearrange("p (b k) -> p b k", b=4)[:, :, 0:KP], ACT.Copy)
            last.then_inc(brow_ok, 1)

            act.wait_ge(ones_ok, 1)
            for use in PREP[6:]:
                take[use[0]](0, 0, int(use[1]))
            for use in PREP[3:]:
                take[use[0]](0, 1, int(use[1]))
            act.wait_ge(mselft_psum, 1)
            A(mrow_self[:], ps[:, 0, 0:112], ACT.Copy, scale=1.0 / BIG).then_inc(mselfr_ok, 1)

            def self_step(r, c):
                j, k = 2 * r + c, c % 2
                if self_live(r, c):
                    act.wait_ge(st_done, j + 1)
                    if not (isinstance(r, int) and j < 2):
                        act.wait_ge(pv_done, j - 1)
                    A(p[k][0:S].rearrange("p (a c) -> p a c", a=2), sbank[k][0:S, :, 0:448], ACT.Exp,
                      scale=SCALE).then_inc(exp_done, 1)
                if self_live(r, c - 3):
                    act.wait_ge(misc_done, self_index(r, c, "tr") + 1)
                    A(attn[:, bass.ds(S * (j - 3), S)], misc[:, 0:S], ACT.Copy).then_inc(misc_read, 1)
                if self_live(r, c - 1):
                    act.wait_ge(pv_done, j)
                    if self_live(r, c - 2):
                        act.wait_ge(misc_done, self_index(r, c, "sel") + 1)
                    A(osb[:], obank[:, 0:224], ACT.Copy).then_inc(o_read, 1)

            act.wait_ge(clear_ok, 1)
            for c in (0, 1, 2):
                self_step(0, c)
            with act.Fori(0, 6, 1) as r:
                for c in (3, 4):
                    self_step(r, c)
            for c in (3, 4, 5, 6):
                self_step(6, c)

            norm_out(1)
            for half in range(2):
                act.wait_ge(q_psum, 2 + half + 1)
                A(q1[:, HALF * half:HALF * half + HALF], ps[:, 4 + half, 0:HALF], ACT.Copy).then_inc(q1_ok, 1)
            second_queries(1)
            act.wait_ge(bias_step, 3)

            def iteration(r, c):
                i = 3 * r + c
                for s in range(KT):
                    use = MISC[s]
                    if used(r, c, use):
                        if use[0] in "KV":
                            take[use[0]](r, c + 2, int(use[1]))
                        elif use == "tr":
                            act.wait_ge(misc_done, misc_index(r, c, use) + 1)
                            A(attn[:, bass.ds(S * (i - 1), S)], misc[:, 0:S], ACT.Copy).then_inc(misc_read, 1)
                        elif use == "mt":
                            act.wait_ge(misc_done, misc_index(r, c, use) + 1)
                            A(mrow[:], misc[0:8, 0:112], ACT.Copy, scale=1.0 / BIG).then_inc(misc_read, 1)
                    if live(r, c):
                        tile = B + KT * i + s
                        act.wait_ge(st_done, tile + 1)
                        act.wait_ge(pv_done, tile - 1)
                        A(p[s % 2][0:KP].rearrange("p (a c) -> p a c", a=2), sbank[s % 2][0:KP, :, 0:448],
                          ACT.Exp, scale=SCALE,
                          bias=bres[:, bass.ds(i, 1), s:s + 1].rearrange("p o t -> p (o t)")).then_inc(exp_done, 1)
                    if s == 0 and live(r, c - 1):
                        act.wait_ge(pv_done, B + KT * i)
                        A(osb[:], obank[:, 0:224], ACT.Copy).then_inc(o_read, 1)

            for c in (-2, -1, 0):
                iteration(0, c)
            with act.Fori(0, 4, 1) as r:
                for c in (1, 2, 3):
                    iteration(r, c)
            for c in (1, 2, 3, 4):
                iteration(4, c)

            norm_out(2)
            act.wait_ge(rt_step, 2)
            A(prob, logit, ACT.Exp).then_inc(rt_exp, 1)

            def silu(u, half):
                step = 2 * u + half
                act.wait_ge(h_psum, step + 1)
                if not (isinstance(u, int) and u == 0):
                    act.wait_ge(u_ok, step - 1)
                A(act_sb[half], ps[:, 3 * half, 0:HALF], ACT.Silu).then_inc(silu_ok, 1)

            silu(0, 0)
            silu(0, 1)
            with act.Fori(1, NP + 1, 1) as u:
                silu(u, 0)
                silu(u, 1)
            for half in range(2):
                act.wait_ge(y_done, 2 * NP + 1 + half)
                A(yt[:, HALF * half:HALF * half + HALF], ps[:, 6 + half, 0:HALF], ACT.Copy).then_inc(yt_ok, 1)

        @block.vector
        def _(dve):
            V = nc.vector

            def norm(n):
                for j in range(TT):
                    last = V.bn_stats(stats[:, j], xs[:, j])
                last.then_inc(ln_step, 1)
                dve.wait_ge(ln_step, 3 * n + 1)
                for j in range(TT):
                    last = V.bn_aggr(mv[:, j], stats[:, j])
                last.then_inc(ln_step, 1)
                dve.wait_ge(ln_step, 3 * n + 2)
                V.tensor_scalar_add(veps[:], mv[:, :, 1], EPS).then_inc(ln_step, 1)
                dve.wait_ge(rstd_ok, n + 1)
                for j in range(TT):
                    V.tensor_scalar(xn[:, j], xs[:, j], mv[:, j, 0:1], rstd[:, j:j + 1],
                                    ALU.subtract, ALU.mult).then_inc(xn_ok, 1)

            def norm_out(n):
                for half, (a, z) in enumerate((XA, XB)):
                    dve.wait_ge(xt1_ok, 2 * n + half + 1)
                    V.tensor_tensor(xt2[:, a:z], ps[:, 2 + half, 0:z - a], xt1[:, a:z], ALU.subtract
                                    ).then_inc(xt2_ok, 1)

            def first_queries(n):
                dve.wait_ge(q1_ok, 2 * n + 2)
                dve.wait_ge(mask_ok, 1)
                if n:
                    for k in range(2):
                        dve.wait_ge(qs_ok[k], 12 * 16)
                for k, (a, z) in enumerate(((0, QCUT), (QCUT, B))):
                    shape = [128, z - a, HG, S]
                    V.tensor_tensor(qd[0][:, a:z],
                                    q1[:].rearrange("p (b o q) -> p b o q", b=B, o=1)[:, a:z].to_broadcast(shape),
                                    headmask[:].rearrange("p (a h b) -> p a h b", a=1, b=1).to_broadcast(shape),
                                    ALU.mult).then_inc(qd_ok[k], 1)

            dve.wait_ge(x_loaded, 16)
            norm(0)
            dve.wait_ge(grp_ok, 1)
            V.tensor_reduce(headmask[:], grp[:].rearrange("p g h -> p h g"), axis=AX.X, op=ALU.add).then_inc(mask_ok, 1)
            for half in range(2):
                dve.wait_ge(wt1_ok, half + 1)
                V.tensor_tensor(wt2[:, 4 * half:4 * half + 4], ps[:, half, :].rearrange("p (n e) -> p n e", n=4),
                                wt1[:, 4 * half:4 * half + 4], ALU.subtract).then_inc(wt2_ok, 1)
            norm_out(0)
            dve.wait_ge(bias_loaded, 16)
            V.tensor_scalar(bh[:], bcol[:], SQ / BIG, None, ALU.mult).then_inc(bias_step, 1)
            dve.wait_ge(bias_step, 1)
            V.tensor_copy(bh32[:], bh[:]).then_inc(bias_step, 1)
            dve.wait_ge(bias_step, 2)
            V.scalar_tensor_tensor(bres[:].rearrange("p b t -> p (b t)"), bh32[:].rearrange("p b t -> p (b t)"),
                                   -BIG / SQ, bcol[:].rearrange("p b t -> p (b t)"), ALU.mult, ALU.add
                                   ).then_inc(bias_step, 1)
            dve.wait_ge(b_loaded, 5 * 16)
            for half in range(2):
                cols = slice(HALF * half, HALF * half + HALF)
                dve.wait_ge(ks1_ok, half + 1)
                V.scalar_tensor_tensor(k12[:, 1, cols], ps[:, half, 0:HALF], bq[:, 1:2], k12[:, 0, cols],
                                       ALU.add, ALU.subtract).then_inc(ks2_ok, 1)
            for half in range(2):
                cols = slice(HALF * half, HALF * half + HALF)
                dve.wait_ge(q1_ok, half + 1)
                V.scalar_tensor_tensor(q2[:, cols], ps[:, 4 + half, 0:HALF], bq[:, 0:1], q1[:, cols],
                                       ALU.add, ALU.subtract).then_inc(q2_ok, 1)
            first_queries(0)

            def take_ctx(r, c, j):
                dve.wait_ge(*use_filled(r, c, f"T{j}"))
                V.tensor_copy(ct[:, :, 4 * j:4 * j + 4, :],
                              use_bank(r, c, j).bitcast(F16).rearrange("p (a t k) -> p a t k", a=2, t=4)
                              ).then_inc(use_read(r, c, "T0")[0], 1)

            def take_keys(r, c, j):
                dve.wait_ge(k1_ok, 3 * (3 * r + c) + j + 1)
                V.tensor_tensor(k12[:, 1, CH * j:CH * j + CH], use_bank(r, c, j)[:, 0:CH],
                                k12[:, 0, CH * j:CH * j + CH], ALU.subtract).then_inc(use_read(r, c, "K0")[0], 1)

            take = {"T": take_ctx, "K": take_keys}

            def self_maxima(r):
                for k in range(4):
                    b = 4 * r + k
                    dve.wait_ge(mself_psum, b + 1)
                    V.tensor_reduce(mself[:, bass.ds(b, 1), :].rearrange("p o k -> p (o k)"),
                                    ps[0:112, k, 0:8 * S].rearrange("p (k s) -> p k s", k=8),
                                    axis=AX.X, op=ALU.max, negate=True).then_inc(mself_ok, 1)

            for n in range(2):
                V.memset(p[n][:], 0.0)
            V.memset(tok[:], 0.0).then_inc(clear_ok, 1)
            for use in PREP[0:6]:
                take[use[0]](0, 0, int(use[1]))
            self_maxima(0)
            for use in PREP[0:3]:
                take[use[0]](0, 1, int(use[1]))
            with dve.Fori(1, B // 4, 1) as r:
                self_maxima(r)
            for use in PREP[3:6]:
                take[use[0]](0, 1, int(use[1]))
            V.tensor_tensor(xs[:], xs[:], bp[:].rearrange("p (o d) -> p o d", o=1).to_broadcast([128, TT, D]),
                            ALU.add).then_inc(xb_ok, 1)

            def normalize(batches):
                part = misc[0:S, 0:144].rearrange("p (k a e) -> p k a e", k=4, a=4)
                V.reciprocal(rec[:], part[:, :, :, HD]).then_inc(norm_step, 1)
                dve.wait_ge(norm_step, batches + 1)
                V.tensor_tensor(tok[0:S, 0:96].rearrange("p (a k e) -> p k a e", a=4, k=3), part[:, 0:3, :, 0:HD],
                                rec[:, 0:3, :].rearrange("p k (a o) -> p k a o", o=1).to_broadcast([S, 3, 4, HD]),
                                ALU.mult)
                V.tensor_tensor(tok[0:S, 96:128].rearrange("p (a e) -> p a e", a=4), part[:, 3, :, 0:HD],
                                rec[:, 3, :].rearrange("p (a o) -> p a o", o=1).to_broadcast([S, 4, HD]),
                                ALU.mult).then_inc(misc_read, 1)

            def self_step(r, c):
                j, k = 2 * r + c, c % 2
                if self_live(r, c):
                    dve.wait_ge(vself_psum, j + 1)
                    if not (isinstance(r, int) and j < 2):
                        dve.wait_ge(pv_done, j - 1)
                    V.tensor_tensor(v[2][0:S, k].rearrange("p (h e) -> p h e", h=H)[:, :, 0:HD],
                                    mbank[k][0:S, 0:D].rearrange("p (h e) -> p h e", h=H),
                                    bv[:].rearrange("p (h e) -> p h e", h=H), ALU.add).then_inc(vself_ok, 1)
                if self_live(r, c - 2):
                    dve.wait_ge(misc_done, self_index(r, c, "sel") + 1)
                    normalize(j - 2)

            dve.wait_ge(ones_ok, 1)
            dve.wait_ge(brow_ok, 1)
            V.memset(obank[:, 0:224], 0.0).then_inc(o_clear, 1)
            for c in (0, 1, 2):
                self_step(0, c)
            with dve.Fori(0, 6, 1) as r:
                for c in (3, 4):
                    self_step(r, c)
            for c in (3, 4, 5, 6):
                self_step(6, c)

            def add_to_x(first_bank, source, before, done, start):
                for half, (a, z) in enumerate(((0, 4), (4, TT))):
                    dve.wait_ge(source, before + half + 1)
                    V.tensor_tensor(xs[:, a:z], xs[:, a:z],
                                    ps[:, half, 0:128 * (z - a)].rearrange("p (j d) -> p j d", d=D), ALU.add
                                    ).then_inc(done, 1)
                dve.wait_ge(done, start + 2)

            dve.wait_ge(xb_ok, 1)
            add_to_x(0, o_psum, 0, x_ok, 0)
            norm(1)
            norm_out(1)
            for half in range(2):
                cols = slice(HALF * half, HALF * half + HALF)
                dve.wait_ge(q1_ok, 2 + half + 1)
                V.tensor_tensor(q2[:, cols], ps[:, 4 + half, 0:HALF], q1[:, cols], ALU.subtract).then_inc(q2_ok, 1)
            first_queries(1)

            def iteration(r, c):
                i = 3 * r + c
                for s in range(KT):
                    use = MISC[s]
                    if used(r, c, use):
                        if use[0] in "TK":
                            take[use[0]](r, c + 2, int(use[1]))
                        elif use == "sel":
                            dve.wait_ge(misc_done, misc_index(r, c, use) + 1)
                            normalize(B + i - 1)
                    for off, k in chunks(s):
                        if not live(r, c + off):
                            continue
                        b = i + off
                        dve.wait_ge(mx_psum, NCH * b + k + 1)
                        if k == 0 and not (isinstance(r, int) and b == 0):
                            dve.wait_ge(mcol_ok, b)
                        V.tensor_reduce(mx[:, k // 3, k % 3:k % 3 + 1], mbank[k % 2][0:112, 0:CH],
                                        axis=AX.X, op=ALU.max).then_inc(mx_read, 1)
                        if k == NCH - 1:
                            dve.wait_ge(mx_read, NCH * (b + 1))
                            V.tensor_reduce(mcol[:], mx[:], axis=AX.X, op=ALU.max, negate=True).then_inc(mcol_ok, 1)

            for c in (-2, -1, 0):
                iteration(0, c)
            with dve.Fori(0, 4, 1) as r:
                for c in (1, 2, 3):
                    iteration(r, c)
            for c in (1, 2, 3, 4):
                iteration(4, c)

            add_to_x(1, o_psum, 2, x_ok, 2)
            norm(2)
            norm_out(2)
            steps = [0]

            def step(ins):
                steps[0] += 1
                ins.then_inc(rt_step, 1)
                dve.wait_ge(rt_step, steps[0])

            wide = lambda a: a.rearrange("p (j o) -> p j o", o=1).to_broadcast([128, TT, NE])
            lg = ps[:, 7, 0:TT * NE].rearrange("p (j e) -> p j e", e=NE)
            dve.wait_ge(lg_psum, 1)
            step(V.tensor_reduce(rmax, lg, axis=AX.X, op=ALU.max))
            step(V.tensor_tensor(logit, lg, wide(rmax), ALU.subtract))
            dve.wait_ge(rt_exp, 1)
            step(V.tensor_reduce(rsum, prob, axis=AX.X, op=ALU.add))
            step(V.reciprocal(rrec, rsum))
            step(V.tensor_tensor(prob, prob, wide(rrec), ALU.mult))
            for j in range(TT):
                last = V.max(top8[:, j], prob[:, j])
            step(last)
            for j in range(TT):
                last = V.max_index(idx8[:, j], top8[:, j], prob[:, j])
            step(last)
            step(V.tensor_copy(idxf, idx8))
            step(V.tensor_tensor(eq, idxf[:, :, 0:TOPK].rearrange("p j (k o) -> p j k o", o=1).to_broadcast([128, TT, TOPK, NE]),
                                 expert_no[:].rearrange("p (a b e) -> p a b e", a=1, b=1).to_broadcast([128, TT, TOPK, NE]),
                                 ALU.is_equal))
            step(V.tensor_reduce(chosen, eq.rearrange("p j k e -> p j e k"), axis=AX.X, op=ALU.add))
            V.tensor_copy(chosen_h, chosen)
            step(V.tensor_tensor(gate, prob, chosen, ALU.mult))

            def shared(half):
                dve.wait_ge(silu_ok, half + 1)
                V.tensor_tensor(u_sb[half], ps[:, 3 * half + 1, 0:HALF], act_sb[half], ALU.mult).then_inc(u_ok, 1)

            shared(0)
            shared(1)
            dve.wait_ge(rank_psum, 1)
            step(V.scalar_tensor_tensor(gate, ps[:, 2, 0:TT * NE].rearrange("p (j e) -> p j e", e=NE), float(CAP),
                                        gate, ALU.is_lt, ALU.mult))
            step(V.tensor_copy(gpair[:, :, 0:NE], gate))
            step(V.tensor_tensor(gpair[:, :, NE:64], gate, gpair[:, :, 0:NE], ALU.subtract))
            dve.wait_ge(gt_psum, 1)
            V.tensor_copy(gt, ps[0:64, 5, :].bitcast(F16)[:, 0:T]).then_inc(gt_ok, 1)

            def gated(u, half):
                step = 2 * u + half
                dve.wait_ge(silu_ok, step + 1)
                V.tensor_tensor(mid_sb[half], ps[:, 3 * half + 1, 0:HALF], act_sb[half], ALU.mult).then_inc(mid_ok, 1)
                dve.wait_ge(mid_ok, step - 1)
                dve.wait_ge(y_done, step - 1)
                V.tensor_tensor(u_sb[half], ps[:, 3 * half + 2, 0:HALF], mid_sb[half], ALU.mult).then_inc(u_ok, 1)

            with dve.Fori(1, NP + 1, 1) as u:
                gated(u, 0)
                gated(u, 1)
            add_to_x(0, yt_psum, 0, res_ok, 0)


_INS = ["x", "ctx_1024", "fside_BxS2_0", "L0_attn_qkv_w", "L0_attn_qkv_b", "L0_attn_proj_w", "L0_attn_proj_b",
        "L0_xattn_Wq", "L0_xattn_Wk", "L0_xattn_Wv", "L0_xattn_Wo", "L0_ffn_Wg", "L0_ffn_W1", "L0_ffn_W2",
        "L0_ffn_W3", "L0_ffn_Ws1", "L0_ffn_Ws2", "L0_ffn_Ws3"]


def kernel(**inputs):
    import numpy as _np
    import concourse.bacc as _bacc
    from concourse import mybir as _mybir
    from concourse.bass_utils import run_bass_kernel_spmd as _run

    nc = _bacc.Bacc("TRN2", target_bir_lowering=False, num_devices=1)
    arrays, args = {}, []
    for name in _INS:
        a = _np.ascontiguousarray(inputs[name])
        arrays[f"in_{name}"] = a
        args.append(nc.dram_tensor(f"in_{name}", a.shape, _mybir.dt.from_np(a.dtype), kind="ExternalInput").ap())
    out = nc.dram_tensor("out", (B, S, D), _mybir.dt.float32, kind="ExternalOutput").ap()
    (x, ctx, bias, qkv_w, qkv_b, proj_w, proj_b, wq, wk, wv, wo, wg, w1, w2, w3, ws1, ws2, ws3) = args
    build(nc, x, ctx, bias, qkv_w, qkv_b, proj_w, proj_b, wq, wk, wv, wo, wg, w1, w2, w3, ws1, ws2, ws3, out)
    r = _run(nc, [arrays], core_ids=[0])
    return r.results[0]["out"]
```

```python
from contextlib import ExitStack

import numpy as np
import concourse.bass as bass
from concourse import mybir
from concourse.alu_op_type import AluOpType as ALU

F32 = mybir.dt.float32
F16 = mybir.dt.float16
U32 = mybir.dt.uint32
ACT = mybir.ActivationFunctionType
AX = mybir.AxisListType

B, S, D, H = 16, 56, 128, 16
HD = D // H
NKEY, KT = 1500, 12
KP = NKEY // KT
T = B * S
TT = T // 128
G = 4
HG = H // G
ROWS = 98
BIG = 32768.0
TWO_BIGS = float(np.array([BIG, BIG], np.float16).view(np.float32)[0])
SQ = float(HD) ** 0.5
SCALE = 1.0 / SQ
VW = H * (HD + 1)
NE, TOPK, HE = 32, 4, 64
CAP = 4 * T * TOPK // NE
NP = NE // 2
NW = 4
CH = NKEY // 3
NCH = 24
EPS = 1e-5
HALF = T // 2
NFIRST, NREST = 4, 4 * (G - 1)
PARTS = [((0, 4), (4, B)), ((0, 4), (4, B // 2), (B // 2, B))]
SELF_ROWS = 97

EARLY = 3
OUT_STEP = 13
PREP = ["T0", "T1", "T2", "K0", "K1", "K2", "V0", "V1", "V2"]
MISC = ["T0", "K0", "T1", "K1", "T2", "K2", "sel", "V0", "V1", "V2", "mt", "tr"]
TAIL = {(B - 2, "T0"): "out", (B - 2, "K2"): "norm", (B - 1, "T0"): "logits"}
OFFSET = {"T": 2, "K": 2, "V": 2, "s": -1, "t": -1, "m": 1}
BEFORE_LOOP = 2 * B + 1


def live(r, c):
    return not isinstance(r, int) or 0 <= 3 * r + c < B


def prep_live(r, c):
    return not isinstance(r, int) or EARLY <= 3 * r + c < B


def used(r, c, use):
    return (prep_live if use[0] in "TKV" else live)(r, c + OFFSET[use[0]]) or tail(r, c, use) is not None


def tail(r, c, use):
    return TAIL.get((3 * r + c, use)) if isinstance(r, int) else None


def misc_index(r, c, use):
    if not isinstance(r, int) and c < 1:
        return misc_index(r, c + 3, use) - 3 * len(MISC)
    i = 3 * r + c if isinstance(r, int) else c
    n = BEFORE_LOOP + sum(used(0, j, u) for j in range(-2, i) for u in MISC)
    n += [u for u in MISC if used(0, i, u)].index(use)
    return n if isinstance(r, int) else n + 3 * len(MISC) * r


def batch_index(r, c, use):
    return misc_index(r, c - 2, use)


def early(r, c):
    return isinstance(r, int) and 3 * r + c < EARLY


def self_uses(j):
    return [u for u, lag in (("tr", 3), ("sel", 2)) if 0 <= j - lag < B] + ["out"] * (j == OUT_STEP)


def self_index(r, c, use):
    j = 2 * r + c if isinstance(r, int) else c
    n = sum(len(self_uses(k)) for k in range(j)) + self_uses(j).index(use)
    return n if isinstance(r, int) else n + 2 * 2 * r


def self_live(r, c):
    return not isinstance(r, int) or 0 <= 2 * r + c < B


def chunks(s):
    return [(1, 6 + 2 * s + j) if s < 9 else (2, 2 * (s - 9) + j) for j in range(2)]


def build(nc, x_d, ctx_d, bias_d, qkv_w, qkv_b, proj_w, proj_b, wq, wk, wv, wo,
          wg, w1, w2, w3, ws1, ws2, ws3, out_d):
    with ExitStack() as stack:
        sb = lambda n, s, d: stack.enter_context(nc.sbuf_tensor(n, s, d))
        sem = lambda n: stack.enter_context(nc.semaphore(n))

        ident = sb("ident", [128, 128], F32)
        identh = sb("identh", [128, 128], F16)
        grp = sb("grp", [128, G, HG], F32)
        headmask = sb("headmask", [128, HG], F32)
        pick = sb("pick", [128, 3, 4, 9], F32)
        mhalf = sb("mhalf", [128, TT], F32)
        zero = sb("zero", [128, 1, 1], F32)
        ones_h = sb("ones_h", [128, 128], F16)
        before = sb("before", [128, 128], F16)
        pairsel = sb("pairsel", [64, NP, 2, HE], F16)
        expert_no = sb("expert_no", [128, NE], F32)
        wnat = sb("wnat", [128, 8, 128], F32)
        wt32 = sb("wt32", [128, 2, 128], F32)
        wt1 = sb("wt1", [128, 8, 128], F16)
        wt2 = sb("wt2", [128, 8, 128], F16)
        wk3 = sb("wk3", [128, 2, G, 3, 32], F16)
        wg_sb = sb("wg_sb", [128, NE], F32)
        bq = sb("bq", [128, 2], F32)
        bk = sb("bk", [96, G], F32)
        bv = sb("bv", [S, D], F32)
        bp = sb("bp", [128, D], F32)
        xs = sb("xs", [128, TT, D], F32)
        xn = sb("xn", [128, TT, D], F32)
        stats = sb("stats", [128, TT, 6], F32)
        mv = sb("mv", [128, TT, 2], F32)
        veps = sb("veps", [128, TT], F32)
        rstd = sb("rstd", [128, TT], F32)
        xt1 = sb("xt1", [128, T], F16)
        xt2 = sb("xt2", [128, T], F16)
        q1 = sb("q1", [128, T], F16)
        q2 = sb("q2", [128, T], F16)
        attn = sb("attn", [128, T], F32)
        qs = sb("qs", [SELF_ROWS, B, H, S], F16)
        late = sb("late", [128, 2, T], F32)
        qd = [late[:].rearrange("p a t -> p (a t)").bitcast(F16).rearrange("p (b h q) -> p b h q", b=B, h=HG),
              sb("qd2", [128, B, HG, S], F16)[:]]
        xt32, yt = late[:, 0], late[:, 1]
        qsb = [sb(f"qsb{n}", [128, H, S], F16) for n in range(3)]
        ks = [sb(f"ks{n}", [128, G, NKEY], F16) for n in range(3)]
        kself = ks[2][:, :, 0:T]
        ctx = [sb(f"ctx{n}", [128, KT, D], F32) for n in range(3)]
        ch = [sb(f"ch{n}", [128, 2, KT, D], F16) for n in range(3)]
        ct = sb("ct", [128, 2, KT, 128], F16)
        k12 = sb("k12", [128, 2, NKEY], F16)
        v = [sb(f"v{n}", [128, KT, VW], F32) for n in range(3)]
        bcol = sb("bcol", [KP, B, KT], F32)
        bh = sb("bh", [KP, B, KT], F16)
        bh32 = sb("bh32", [KP, B, KT], F32)
        bres = sb("bres", [KP, B, KT], F32)
        brow = sb("brow", [KT, B, KP], F16)
        p = [sb(f"p{n}", [128, H * S], F32) for n in range(2)]
        mx = sb("mx", [112, 8, 3], F32)
        mcol = sb("mcol", [112, 8], F32)
        mrow = sb("mrow", [8, 112], F16)
        mself = sb("mself", [112, B, 8], F32)
        mrow_self = sb("mrow_self", [128, 112], F16)
        osb = sb("osb", [128, 224], F32)
        rec = sb("rec", [S, 4, 4], F32)
        tok = sb("tok", [128, D], F32)

        flat = lambda t, d, n, o=0: t[:].rearrange("p a b -> p (a b)").bitcast(d)[:, o:o + n]
        wf = [flat(ks[1], F32, 384, 384 * n).rearrange("p (a b) -> p a b", a=3) for n in range(NW)]
        wh = [flat(ks[2], F16, 768, 2048 + 768 * n).rearrange("p (h a b) -> p h a b", h=2, a=3) for n in range(NW)]
        u1_sb = [flat(v[1], F16, HALF, 2 * HALF * 2 + HALF * n) for n in range(2)]
        u2_sb = [flat(v[2], F16, HALF, 2 * HALF * 2 + HALF * n) for n in range(2)]
        act_sb = [flat(v[0], F32, HALF, HALF * n) for n in range(2)]
        mid_sb = [flat(v[1], F32, HALF, HALF * n) for n in range(2)]
        u_sb = [flat(v[2], F32, HALF, HALF * n) for n in range(2)]
        logit = flat(ctx[1], F32, 224).rearrange("p (j e) -> p j e", e=NE)
        prob = flat(ctx[1], F32, 224, 224).rearrange("p (j e) -> p j e", e=NE)
        chosen = flat(ctx[1], F32, 224, 448).rearrange("p (j e) -> p j e", e=NE)
        gate = flat(ctx[1], F32, 224, 672).rearrange("p (j e) -> p j e", e=NE)
        eq = flat(ctx[2], F32, 896).rearrange("p (j k e) -> p j k e", j=TT, k=TOPK)
        top8 = flat(ctx[2], F32, 56, 896).rearrange("p (j k) -> p j k", k=8)
        idx8 = flat(ctx[2], U32, 56, 960).rearrange("p (j k) -> p j k", k=8)
        idxf = flat(ctx[2], F32, 56, 1024).rearrange("p (j k) -> p j k", k=8)
        rmax = flat(ctx[2], F32, TT, 1088)
        rsum = flat(ctx[2], F32, TT, 1096)
        rrec = flat(ctx[2], F32, TT, 1104)
        chosen_h = flat(ks[2], F16, 224).rearrange("p (j e) -> p j e", e=NE)
        gpair = flat(ks[2], F16, 448, 256).rearrange("p (j e) -> p j e", e=64)
        gt = flat(ks[2], F16, T, 1024)[0:64]

        ps = stack.enter_context(nc.psum_tensor("ps", [128, 8, 512], F32))
        sbank = [ps[:, 0:2, :], ps[:, 2:4, :]]
        mbank = [ps[:, 4, :], ps[:, 5, :]]
        misc = ps[:, 6, :]
        obank = ps[:, 7, :]

        ident_ok = sem("ident_ok")
        grp_ok = sem("grp_ok")
        const_ok = sem("const_ok")
        big_ok = sem("big_ok")
        const_step = sem("const_step")
        mask_ok = sem("mask_ok")
        w_loaded = sem("w_loaded")
        b_loaded = sem("b_loaded")
        x_loaded = sem("x_loaded")
        bias_loaded = sem("bias_loaded")
        wt_psum = sem("wt_psum")
        wt1_ok = sem("wt1_ok")
        wt2_ok = sem("wt2_ok")
        ln_step = sem("ln_step")
        rstd_ok = sem("rstd_ok")
        xn_ok = sem("xn_ok")
        xt_psum = sem("xt_psum")
        xt1_ok = sem("xt1_ok")
        xt2_ok = sem("xt2_ok")
        q_psum = sem("q_psum")
        bk_psum = sem("bk_psum")
        k_psum = sem("k_psum")
        q1_ok = sem("q1_ok")
        q2_ok = sem("q2_ok")
        bk_ok = sem("bk_ok")
        ks1_ok = sem("ks1_ok")
        ks2_ok = sem("ks2_ok")
        qd_ok = [sem(f"qd_ok{n}") for n in range(3)]
        qs_ok = [sem(f"qs_ok{n}") for n in range(3)]
        q0_ok = [sem(f"q0_ok{g}") for g in range(G)]
        qsb_ok = [sem(f"qsb_ok{n}") for n in range(3)]
        vself_psum = sem("vself_psum")
        vself_ok = sem("vself_ok")
        mself_psum = sem("mself_psum")
        mself_ok = sem("mself_ok")
        mselft_psum = sem("mselft_psum")
        mselfr_ok = sem("mselfr_ok")
        mself_row = sem("mself_row")
        st_done = sem("st_done")
        exp_done = sem("exp_done")
        pv_done = sem("pv_done")
        o_read = sem("o_read")
        prep_psum = sem("prep_psum")
        prep_read = {u: sem(f"prep_read{u}") for u in "TKV"}
        misc_done = sem("misc_done")
        misc_read = sem("misc_read")
        norm_step = sem("norm_step")
        o_psum = sem("o_psum")
        xb_ok = sem("xb_ok")
        x_ok = sem("x_ok")
        bias_step = sem("bias_step")
        bt_psum = sem("bt_psum")
        brow_ok = sem("brow_ok")
        ctx_loaded = [sem(f"ctx_loaded{n}") for n in range(3)]
        ch_step = sem("ch_step")
        ch_ok = sem("ch_ok")
        k1_ok = sem("k1_ok")
        first_ok = [sem(f"first_ok{n}") for n in range(3)]
        rest_ok = [sem(f"rest_ok{n}") for n in range(3)]
        mrow_in = [sem(f"mrow_in{n}") for n in range(3)]
        mx_psum = sem("mx_psum")
        mx_read = sem("mx_read")
        mcol_ok = sem("mcol_ok")
        ctx_clear = sem("ctx_clear")
        ones_ok = sem("ones_ok")
        o_clear = sem("o_clear")
        clear_ok = sem("clear_ok")

        we_loaded = [sem(f"we_loaded{n}") for n in range(NW)]
        wh_step = sem("wh_step")
        wh_ok = sem("wh_ok")
        lg_psum = sem("lg_psum")
        rt_step = sem("rt_step")
        rt_exp = sem("rt_exp")
        rank_psum = sem("rank_psum")
        gt_psum = sem("gt_psum")
        gt_ok = sem("gt_ok")
        h1_psum = sem("h1_psum")
        h_psum = sem("h_psum")
        silu_ok = sem("silu_ok")
        mid_ok = sem("mid_ok")
        u_ok = sem("u_ok")
        u1_ok = sem("u1_ok")
        u2_ok = sem("u2_ok")
        y_done = sem("y_done")
        yt_ok = sem("yt_ok")
        yt_psum = sem("yt_psum")
        res_ok = sem("res_ok")
        out_ok = sem("out_ok")

        TILES = ((0, 4), (4, TT))
        X = ((0, 512), (512, T))
        OUT_TILES = ((0, HALF // 128), (HALF // 128, TT))
        SELF_W, CROSS_W = 0, 4

        def split_matmul(out, a1, a2, b1, b2):
            nc.tensor.matmul(out, a1, b1, start=True, stop=False)
            nc.tensor.matmul(out, a1, b2, start=False, stop=False)
            return nc.tensor.matmul(out, a2, b1, start=False, stop=True)

        def use_filled(r, c, use):
            if early(r, c):
                return prep_psum, len(PREP) * (3 * r + c) + PREP.index(use) + 1
            return misc_done, batch_index(r, c, use) + 1

        def use_read(r, c, use):
            if early(r, c):
                return prep_read[use[0]], 3 * (3 * r + c) + int(use[1]) + 1
            return misc_read, batch_index(r, c, use) + 1

        def use_bank(r, c, j):
            if not early(r, c):
                return misc
            return ps[:, ((6, 0, 1) if 3 * r + c == 2 else (6, 4, 5))[j], :]

        block = stack.enter_context(nc.Block())

        @block.sync
        def _(sp):
            sp.dma_start(xs[:], x_d.rearrange("b s d -> (b s) d").rearrange("(j p) d -> p j d", p=128)
                         ).then_inc(x_loaded, 16)
            sp.dma_start(wnat[:, 0:3, :], qkv_w.rearrange("(n p) d -> p n d", n=3)).then_inc(w_loaded, 16)
            for n, w in enumerate((proj_w, wq, wk, wv, wo)):
                sp.dma_start(wnat[:, 3 + n, :], w).then_inc(w_loaded, 16)
            qb = qkv_b.rearrange("(n p a) -> n p a", n=3, a=1)
            for n in range(2):
                sp.dma_start(bq[:, n:n + 1], qb[n]).then_inc(b_loaded, 16)
            row = lambda a: a.rearrange("(o n) -> o n", o=1)
            sp.dma_start(bv[:], row(qkv_b[256:384]).to_broadcast([S, D])).then_inc(b_loaded, 16)
            sp.dma_start(bp[:], row(proj_b).to_broadcast([128, D])).then_inc(b_loaded, 16)
            sp.dma_start(wg_sb[:], wg).then_inc(b_loaded, 16)
            sp.dma_start(bcol[:], bias_d.rearrange("b (p t) -> p b t", t=KT)).then_inc(bias_loaded, 16)

            def load_ctx(r, c):
                if not live(r, c):
                    return
                if not isinstance(r, int) or 3 * r + c >= 3:
                    sp.wait_ge(ch_ok, 3 * r + c - 2)
                else:
                    sp.wait_ge(ctx_clear, 1)
                sp.dma_start(ctx[c % 3][0:KP], ctx_d[3 * r + c].rearrange("(p t) d -> p t d", t=KT)
                             ).then_inc(ctx_loaded[c % 3], 16)

            for c in range(3):
                load_ctx(0, c)

            def query_stacks(n, k):
                a, z = PARTS[n][k]
                if n and k == 0:
                    a = 1
                sp.wait_ge(qd_ok[k], 5 * n + 5 if k < 2 else 5)
                for g in range(G):
                    for row0, part in ((0, 0), (32, 0), (64, 1)):
                        sp.dma_start(qs[row0:row0 + 32, a:z, HG * g:HG * g + HG, :],
                                     qd[part][32 * g:32 * g + 32, a:z]).then_inc(qs_ok[k], 16)

            def key_stacks(r, c):
                n, b = c % 3, 3 * r + c
                for g in range(G):
                    sp.dma_start(ks[n][96:97, g, :].rearrange("o (t k) -> o t k", t=KT),
                                 brow[:, bass.ds(b, 1), :]).then_inc((rest_ok if g else first_ok)[n], 16)
                sp.wait_ge(*use_read(r, c, "K2"))
                for g in range(G):
                    for row0, part in ((0, 0), (32, 1), (64, 0)):
                        sp.dma_start(ks[n][row0:row0 + 32, g, :], k12[32 * g:32 * g + 32, part, :]
                                     ).then_inc((rest_ok if g else first_ok)[n], 16)

            def load_queries(r, c):
                n, b = c % 3, 3 * r + c
                if isinstance(r, int) and b < 4:
                    sp.wait_ge(qs_ok[0], 2 * 12 * 16)
                else:
                    sp.wait_ge(qs_ok[1], 2 * 12 * 16)
                    sp.wait_ge(qs_ok[2], 12 * 16)
                sp.dma_start(qsb[n][0:96], qs[0:96, bass.ds(b, 1)].rearrange("p o h q -> p (o h) q")
                             ).then_inc(qsb_ok[n], 16)

            query_stacks(0, 0)
            query_stacks(0, 1)
            sp.wait_ge(brow_ok, 1)
            sp.wait_ge(big_ok, 1)
            key_stacks(0, 0)
            load_ctx(0, 3)
            sp.wait_ge(mselfr_ok, 1)
            sp.dma_start(qs[96:97].rearrange("o b (k h) q -> o (b k) (h q)", k=8), mrow_self[:]
                         ).then_inc(mself_row, 16)

            key_stacks(0, 1)

            sp.wait_ge(st_done, B // 2)
            sp.wait_ge(qd_ok[0], 10)
            for g in range(G):
                for row0, part in ((0, 0), (32, 0), (64, 1)):
                    sp.dma_start(qsb[0][row0:row0 + 32, HG * g:HG * g + HG, :],
                                 qd[part][32 * g:32 * g + 32, 0]).then_inc(q0_ok[g], 16)
            query_stacks(1, 0)
            load_queries(0, 1)
            sp.wait_ge(st_done, B)
            key_stacks(0, 2)
            load_queries(0, 2)

            def iteration(r, c):
                if not isinstance(r, int) or 3 * r + c >= 1:
                    load_ctx(r, c + 3)
                if prep_live(r, c + 2):
                    sp.wait_ge(st_done, B + KT * (3 * r + c))
                    load_queries(r, c + 2)
                    key_stacks(r, c + 2)
                if live(r, c + 1):
                    sp.wait_ge(misc_read, misc_index(r, c, "mt") + 1)
                    sp.dma_start(qsb[(c + 1) % 3][97:98].rearrange("o (k h) q -> o k (h q)", k=8), mrow[:]
                                 ).then_inc(mrow_in[(c + 1) % 3], 16)

            iteration(0, -1)
            query_stacks(1, 1)
            query_stacks(1, 2)
            iteration(0, 0)
            with sp.Fori(0, 4, 1) as r:
                for c in (1, 2, 3):
                    iteration(r, c)
            for c in (1, 2, 3, 4):
                iteration(4, c)

            def load_experts(n, a, b_, c_):
                for k, w in enumerate((a, b_, c_)):
                    dst = wf[n][:, k, :]
                    sp.dma_start(dst.rearrange("p (e h) -> p e h", e=2) if k < 2 and len(w.shape) == 3 else dst, w
                                 ).then_inc(we_loaded[n], 16)

            sp.wait_ge(st_done, B + KT * (B - 2))
            load_experts(0, ws1, ws3, ws2)
            w1v = w1.rearrange("(n e) d h -> n d e h", e=2)
            w3v = w3.rearrange("(n e) d h -> n d e h", e=2)
            w2v = w2.rearrange("(n e) h d -> n (e h) d", e=2)

            def load_pair(u, n):
                if not isinstance(u, int) or u >= NW:
                    sp.wait_ge(wh_ok, u - NW + 1)
                load_experts(n, w1v[u - 1], w3v[u - 1], w2v[u - 1])

            for u in range(1, NW):
                load_pair(u, u)
            with sp.Fori(1, NP // NW, 1) as r:
                for n in range(NW):
                    load_pair(NW * r + n, n)
            load_pair(NP, 0)

            outv = out_d.rearrange("b s d -> (b s) d").rearrange("(j p) d -> p j d", p=128)
            sp.wait_ge(res_ok, 1)
            sp.dma_start(outv[:, 0:OUT_TILES[0][1]], xs[:, 0:OUT_TILES[0][1]]).then_inc(out_ok, 16)
            sp.wait_ge(res_ok, 2)
            sp.dma_start(outv[:, OUT_TILES[1][0]:TT], xs[:, OUT_TILES[1][0]:TT]).then_inc(out_ok, 16)
            sp.wait_ge(out_ok, 32)

        @block.gpsimd
        def _(pool):
            steps = [0]

            def step(ins):
                steps[0] += 1
                ins.then_inc(const_step, 1)
                pool.wait_ge(const_step, steps[0])

            memset, select = nc.gpsimd.memset, nc.gpsimd.affine_select
            memset(mhalf[:], -0.5)
            memset(zero[:], 0.0)
            memset(grp[:], 1.0)
            step(memset(ident[:], 0.0))
            step(select(out=ident[:], in_=ident[:], compare_op=ALU.not_equal, fill=1.0, base=0,
                        pattern=[[-1, 128]], channel_multiplier=1))
            nc.gpsimd.tensor_copy(identh[:], ident[:]).then_inc(ident_ok, 1)
            step(select(out=grp[:], in_=grp[:], compare_op=ALU.is_ge, fill=0.0, base=0,
                        pattern=[[-32, G], [-HD, HG]], channel_multiplier=1))
            select(out=grp[:], in_=grp[:], compare_op=ALU.is_ge, fill=0.0, base=HD - 1,
                   pattern=[[32, G], [HD, HG]], channel_multiplier=-1).then_inc(grp_ok, 1)
            pool.wait_ge(grp_ok, 1)
            for n in range(3):
                last = memset(ctx[n][96:128], 0.0)
            last.then_inc(ctx_clear, 1)
            pool.wait_ge(ctx_clear, 1)

            def rstd_of(n, half):
                pool.wait_ge(ln_step, 3 * (2 * n + half) + 3)
                tiles = slice(*TILES[half])
                nc.gpsimd.tensor_tensor(rstd[:, tiles], veps[:, tiles], mhalf[:, tiles], ALU.pow
                                        ).then_inc(rstd_ok, 1)

            def split_ctx(r, c):
                if not live(r, c):
                    return
                n, b = c % 3, 3 * r + c
                pool.wait_ge(ctx_loaded[n], 16 * (r + c // 3 + 1))
                if not isinstance(r, int) or b >= 3:
                    if isinstance(r, int):
                        pool.wait_ge(*use_filled(r, c - 3, "T2"))
                    else:
                        pool.wait_ge(misc_done, misc_index(r, c - 4, "T0"))
                nc.gpsimd.tensor_tensor(ch[n][:, 0], ctx[n][:], zero[:].to_broadcast([128, KT, D]), ALU.add
                                        ).then_inc(ch_step, 1)
                pool.wait_ge(ch_step, b + 1)
                nc.gpsimd.tensor_tensor(ch[n][:, 1], ctx[n][:], ch[n][:, 0], ALU.subtract).then_inc(ch_ok, 1)

            rstd_of(0, 0)
            rstd_of(0, 1)
            pool.wait_ge(rstd_ok, 2)
            step(memset(ks[2][96:ROWS].rearrange("p g k -> p (g k)").bitcast(F32), TWO_BIGS))
            split_ctx(0, 0)
            pool.wait_ge(ch_ok, 1)
            for n in range(2):
                memset(ks[n][96:ROWS].rearrange("p g k -> p (g k)").bitcast(F32), TWO_BIGS)
            for n in range(3):
                last = memset(qsb[n][96:97], BIG)
            last.then_inc(big_ok, 1)
            pool.wait_ge(big_ok, 1)
            for n in range(3):
                last = memset(v[n][:], 1.0)
            last.then_inc(ones_ok, 1)
            split_ctx(0, 1)
            step(memset(pick[:], 0.0))
            memset(ones_h[:], 1.0)
            memset(before[:], 1.0)
            memset(pairsel[:], 0.0)
            nc.gpsimd.iota(expert_no[:], pattern=[[1, NE]], base=0, channel_multiplier=0,
                           allow_small_or_imprecise_dtypes=True)
            step(select(out=pick[:], in_=pick[:], compare_op=ALU.not_equal, fill=1.0, base=0,
                        pattern=[[-9, 3], [-32, 4], [-1, 9]], channel_multiplier=1))
            select(out=before[:], in_=before[:], compare_op=ALU.is_gt, fill=0.0, base=0,
                   pattern=[[1, 128]], channel_multiplier=-1)
            for row0 in (0, 32):
                last = select(out=pairsel[:], in_=pairsel[:], compare_op=ALU.not_equal, fill=1.0, base=-row0,
                              pattern=[[-2, NP], [-1, 2], [0, HE]], channel_multiplier=1)
                if row0 == 0:
                    step(last)
            last.then_inc(const_ok, 1)
            split_ctx(0, 2)
            rstd_of(1, 0)
            rstd_of(1, 1)
            split_ctx(0, 3)
            for c in (1, 2, 3):
                split_ctx(0, c + 3)
            with pool.Fori(1, 4, 1) as r:
                for c in (1, 2, 3):
                    split_ctx(r, c + 3)
            for c in (1, 2, 3, 4):
                split_ctx(4, c + 3)

            def split_experts(u, n, it):
                pool.wait_ge(we_loaded[n], 48 * (it + 1))
                if not isinstance(u, int) or u >= NW:
                    pool.wait_ge(y_done, 2 * (u - NW) + 2)
                nc.gpsimd.tensor_tensor(wh[n][:, 0], wf[n][:], zero[:].to_broadcast([128, 3, 128]), ALU.add
                                        ).then_inc(wh_step, 1)
                pool.wait_ge(wh_step, u + 1)
                nc.gpsimd.tensor_tensor(wh[n][:, 1], wf[n][:], wh[n][:, 0], ALU.subtract
                                        ).then_inc(wh_ok, 1)

            rstd_of(2, 0)
            pool.wait_ge(st_done, B + KT * (B - 1))
            for u in range(NW):
                split_experts(u, u, 0)
            rstd_of(2, 1)
            with pool.Fori(1, NP // NW, 1) as r:
                for n in range(NW):
                    split_experts(NW * r + n, n, r)
            split_experts(NP, 0, NP // NW)

        @block.tensor
        def _(pe):
            mm, tr = nc.tensor.matmul, nc.tensor.transpose

            pe.wait_ge(ident_ok, 1)
            pe.wait_ge(w_loaded, 6 * 16)
            for half in range(2):
                for n in range(4):
                    last = tr(ps[:, half, 128 * n:128 * n + 128], wnat[:, 4 * half + n], ident[:])
                last.then_inc(wt_psum, 1)

            def transpose_norm(n, half, bank, done):
                a, z = X[half]
                pe.wait_ge(xn_ok, TT * n + z // 128)
                for j in range(a // 128, z // 128):
                    last = tr(ps[:, bank, 128 * j - a:128 * j - a + 128], xn[:, j], ident[:])
                last.then_inc(done, 1)

            def project(weight, half, bank, done):
                cols = slice(HALF * half, HALF * half + HALF)
                split_matmul(ps[:, bank, 0:HALF], wt1[:, weight], wt2[:, weight],
                             xt1[:, cols], xt2[:, cols]).then_inc(done, 1)

            def out_project(n, half, out, done):
                a, z = X[half]
                for j in range(a // 128, z // 128):
                    last = mm(out[:, 128 * j - a:128 * j - a + 128], attn[:, 128 * j:128 * j + 128],
                              wt32[:, n], start=True, stop=True)
                last.then_inc(done, 1)

            def ctx_transpose(r, c, j):
                if not early(r, c):
                    pe.wait_ge(misc_read, batch_index(r, c, f"T{j}"))
                elif 3 * r + c:
                    pe.wait_ge(*use_read(r, c - 1, f"V{j}"))
                pe.wait_ge(ch_ok, 3 * r + c + 1)
                bank = use_bank(r, c, j).bitcast(F16)
                for part in range(2):
                    for t in range(4):
                        o = 512 * part + 128 * t
                        last = tr(bank[:, o:o + 128], ch[c % 3][:, part, 4 * j + t], identh[:])
                last.then_inc(use_filled(r, c, "T0")[0], 1)

            def key_project(r, c, j):
                if early(r, c):
                    pe.wait_ge(*use_read(r, c, f"T{j}"))
                else:
                    pe.wait_ge(misc_read, batch_index(r, c, f"K{j}"))
                c1, c2 = ct[:, 0, 4 * j:4 * j + 4, 0:KP], ct[:, 1, 4 * j:4 * j + 4, 0:KP]
                out = use_bank(r, c, j)[:, 0:CH].rearrange("p (t k) -> p t k", t=4)
                split_matmul(out, wt1[:, CROSS_W + 1], wt2[:, CROSS_W + 1], c1, c2
                             ).then_inc(use_filled(r, c, "K0")[0], 1)

            def value_project(r, c, j):
                if early(r, c):
                    pe.wait_ge(*use_read(r, c, f"K{j}"))
                else:
                    pe.wait_ge(misc_read, batch_index(r, c, f"V{j}"))
                for t in range(4):
                    last = split_matmul(use_bank(r, c, j)[0:KP, 128 * t:128 * t + 128],
                                        ct[:, 0, 4 * j + t, 0:KP], ct[:, 1, 4 * j + t, 0:KP],
                                        wt1[:, CROSS_W + 2], wt2[:, CROSS_W + 2])
                last.then_inc(use_filled(r, c, "V0")[0], 1)

            prepare = {"T": ctx_transpose, "K": key_project, "V": value_project}

            for half in range(2):
                transpose_norm(0, half, 2 + half, xt_psum)
            pe.wait_ge(wt2_ok, 2)
            pe.wait_ge(xt2_ok, 2)
            for half in range(2):
                project(SELF_W, half, 4 + half, q_psum)
            pe.wait_ge(b_loaded, 5 * 16)
            for g in range(G):
                for k in range(3):
                    last = mm(ps[32 * k:32 * k + 32, 0, g:g + 1], ident[:, 32 * g:32 * g + 32], bq[:, 1:2],
                              start=True, stop=True)
            last.then_inc(bk_psum, 1)
            for u in range(2 * G):
                g, cols = u // 2, slice(HALF * (u % 2), HALF * (u % 2) + HALF)
                if u == 3:
                    pe.wait_ge(bk_ok, 1)
                if u >= 4:
                    pe.wait_ge(ks2_ok, u - 3)
                k1w, k2w = (wk3[:, n, g].rearrange("p a c -> p (a c)") for n in range(2))
                split_matmul(ps[0:96, (1, 6, 7, 0)[u % 4], 0:HALF], k1w, k2w, xt1[:, cols], xt2[:, cols]
                             ).then_inc(k_psum, 1)
            def self_maxima(r):
                for k in range(4):
                    b = 4 * r + k
                    if not (isinstance(r, int) and r == 0):
                        pe.wait_ge(mself_ok, b - 3)
                    for pair in range(8):
                        last = mm(ps[0:112, k, S * pair:S * pair + S],
                                  qs[0:96, bass.ds(b, 1), 2 * pair:2 * pair + 2, :].rearrange("p o h q -> p (o h q)"),
                                  kself[0:96, pair // 2, bass.ds(S * b, S)], start=True, stop=True)
                    last.then_inc(mself_psum, 1)

            pe.wait_ge(q2_ok, 2)
            pe.wait_ge(ks2_ok, 6)
            for use in PREP[0:6]:
                prepare[use[0]](0, 0, int(use[1]))
            pe.wait_ge(bias_step, 2)
            pe.wait_ge(ks2_ok, 8)
            for b in range(B):
                last = tr(ps[0:KT, (2, 3, 0, 7)[b // 4], 128 * (b % 4):128 * (b % 4) + KP],
                          bh32[:, b], ident[0:KP, 0:KP])
            last.then_inc(bt_psum, 1)
            for use in PREP[6:]:
                prepare[use[0]](0, 0, int(use[1]))
            pe.wait_ge(brow_ok, 1)
            pe.wait_ge(qs_ok[0], 12 * 16)
            self_maxima(0)
            for use in PREP[0:3]:
                prepare[use[0]](0, 1, int(use[1]))
            pe.wait_ge(qs_ok[1], 12 * 16)
            with pe.Fori(1, B // 4, 1) as r:
                self_maxima(r)
            pe.wait_ge(mself_ok, B)
            tr(ps[:, 0, 0:112], mself[:].rearrange("p b k -> p (b k)"), ident[0:112, 0:112]).then_inc(mselft_psum, 1)
            for use in PREP[3:]:
                prepare[use[0]](0, 1, int(use[1]))
            pe.wait_ge(mselfr_ok, 1)
            pe.wait_ge(mself_row, 16)
            pe.wait_ge(prep_read["V"], 6)

            def times_v(vt, pt, keys, first, last_):
                for quad in range(4):
                    mm(obank[32 * quad:32 * quad + 27, 0:168], vt[0:keys, 27 * quad:27 * quad + 27],
                       pt[0:keys, 168 * quad:168 * quad + 168], start=first, stop=last_, skip_group_check=True)
                for quad in range(4):
                    done = mm(obank[32 * quad:32 * quad + 9, 168:224], vt[0:keys, 108 + 9 * quad:117 + 9 * quad],
                              pt[0:keys, 672 + S * quad:672 + S * quad + S], start=False, stop=last_,
                              skip_group_check=True)
                done.then_inc(pv_done, 1)

            def pick_heads():
                for k in range(4):
                    last = mm(misc[0:S, 36 * k:36 * k + 36], osb[:, S * k:S * k + S],
                              pick[:, k % 3].rearrange("p a b -> p (a b)"), start=True, stop=True)
                last.then_inc(misc_done, 1)

            def self_step(r, c):
                j, k = 2 * r + c, c % 2
                if self_live(r, c):
                    tokens = bass.ds(S * j, S)
                    if not (isinstance(r, int) and j < 2):
                        pe.wait_ge(exp_done, j - 1)
                    for g in range(G):
                        last = mm(sbank[k][0:S, g // 2, 224 * (g % 2):224 * (g % 2) + 224],
                                  kself[0:SELF_ROWS, g, tokens],
                                  qs[0:SELF_ROWS, bass.ds(j, 1), HG * g:HG * g + HG, :].rearrange("p o h q -> p (o h q)"),
                                  start=True, stop=True)
                    last.then_inc(st_done, 1)
                    if not (isinstance(r, int) and j < 2):
                        pe.wait_ge(vself_ok, j - 1)
                    mm(mbank[k][0:S, 0:D], xt1[:, tokens], wt1[:, SELF_W + 2], start=True, stop=False)
                    mm(mbank[k][0:S, 0:D], xt1[:, tokens], wt2[:, SELF_W + 2], start=False, stop=False)
                    mm(mbank[k][0:S, 0:D], xt2[:, tokens], wt1[:, SELF_W + 2], start=False, stop=True
                       ).then_inc(vself_psum, 1)
                if self_live(r, c - 3):
                    pe.wait_ge(misc_read, self_index(r, c, "tr"))
                    tr(misc[:, 0:128], tok[:], ident[:]).then_inc(misc_done, 1)
                if self_live(r, c - 1):
                    pe.wait_ge(vself_ok, j)
                    pe.wait_ge(exp_done, j)
                    if not (isinstance(r, int) and j < 2):
                        pe.wait_ge(o_read, j - 1)
                    times_v(v[2][:, 1 - k], p[1 - k], KP, True, True)
                if self_live(r, c - 2):
                    pe.wait_ge(misc_read, self_index(r, c, "sel"))
                    pe.wait_ge(o_read, j - 1)
                    pick_heads()
                if isinstance(r, int) and j == OUT_STEP:
                    pe.wait_ge(misc_read, self_index(r, c, "out"))
                    out_project(0, 0, misc, misc_done)
                if isinstance(r, int) and j == OUT_STEP + 3:
                    pe.wait_ge(vself_ok, B)
                    transpose_norm(1, 0, 4, xt_psum)
                if isinstance(r, int) and j == OUT_STEP + 4:
                    pe.wait_ge(xt2_ok, 3)
                    project(CROSS_W, 0, 5, q_psum)

            pe.wait_ge(const_ok, 1)
            pe.wait_ge(o_clear, 1)
            for c in (0, 1, 2):
                self_step(0, c)
            with pe.Fori(0, 5, 1) as r:
                for c in (3, 4):
                    self_step(r, c)
            for c in range(3, 9):
                self_step(5, c)

            def router_logits(half, bank):
                a, z = TILES[half]
                pe.wait_ge(xt1_ok, 5 + half)
                for j in range(a, z):
                    last = mm(bank[:, NE * (j - a):NE * (j - a) + NE], xt32[:, 128 * j:128 * j + 128], wg_sb[:],
                              start=True, stop=True)
                return last

            pe.wait_ge(misc_read, BEFORE_LOOP)
            out_project(0, 1, ps[:, 0], o_psum)
            pe.wait_ge(x_ok, 1)
            for use in PREP[0:6]:
                prepare[use[0]](0, 2, int(use[1]))
            pe.wait_ge(q2_ok, 3)

            def max_chunk(r, c, off, k):
                b, n = 3 * r + c + off, (c + off) % 3
                pair, part = k // 3, k % 3
                if isinstance(r, int) and b == 0 and k % 6 == 0:
                    pe.wait_ge(q0_ok[k // 6], 48)
                elif k == 0:
                    pe.wait_ge(qsb_ok[n], 16 * (r + (c + off) // 3 + (1 if n else 0)))
                if k == 0:
                    pe.wait_ge(first_ok[n], 16 * NFIRST * (r + (c + off) // 3 + 1))
                if k == 6:
                    pe.wait_ge(rest_ok[n], 16 * NREST * (r + (c + off) // 3 + 1))
                if not (isinstance(r, int) and NCH * b + k < 2):
                    pe.wait_ge(mx_read, NCH * b + k - 1)
                mm(mbank[k % 2][0:112, 0:CH], qsb[n][0:ROWS - 1, 2 * pair:2 * pair + 2].rearrange("p h q -> p (h q)"),
                   ks[n][0:ROWS - 1, pair // 2, CH * part:CH * part + CH], start=True, stop=True).then_inc(mx_psum, 1)

            def pv_tile(r, c, t):
                tile = B + KT * (3 * r + c) + t
                pe.wait_ge(exp_done, tile + 1)
                if t == 0:
                    if isinstance(r, int):
                        pe.wait_ge(*use_read(r, c, "V2"))
                    else:
                        pe.wait_ge(misc_read, misc_index(r, c, "T0"))
                    pe.wait_ge(o_read, B + 3 * r + c)
                times_v(v[c % 3][:, t], p[t % 2], KP, t == 0, t == KT - 1)

            def iteration(r, c):
                for s in range(KT):
                    use = MISC[s]
                    if used(r, c, use):
                        if use[0] in "TKV" and not tail(r, c, use):
                            prepare[use[0]](r, c + 2, int(use[1]))
                        else:
                            pe.wait_ge(misc_read, misc_index(r, c, use))
                        if tail(r, c, use) == "out":
                            out_project(1, 0, misc, misc_done)
                        if tail(r, c, use) == "norm":
                            transpose_norm(2, 0, 6, misc_done)
                        if tail(r, c, use) == "logits":
                            router_logits(0, misc).then_inc(misc_done, 1)
                        if use == "sel":
                            pe.wait_ge(o_read, B + 3 * r + c)
                            pick_heads()
                        elif use == "tr":
                            tr(misc[:, 0:128], tok[:], ident[:]).then_inc(misc_done, 1)
                        elif use == "mt":
                            pe.wait_ge(mcol_ok, 3 * r + c + 2)
                            tr(misc[0:8, 0:112], mcol[:], ident[0:112, 0:112]).then_inc(misc_done, 1)
                    if live(r, c):
                        if s == 0:
                            pe.wait_ge(mrow_in[c % 3], 16 * (r + c // 3 + 1))
                        pe.wait_ge(exp_done, B + KT * (3 * r + c) + s - 1)
                        for g in range(G):
                            last = mm(sbank[s % 2][0:KP, g // 2, 224 * (g % 2):224 * (g % 2) + 224],
                                      ks[c % 3][0:ROWS, g, KP * s:KP * s + KP],
                                      qsb[c % 3][0:ROWS, HG * g:HG * g + HG].rearrange("p h q -> p (h q)"),
                                      start=True, stop=True)
                        last.then_inc(st_done, 1)
                    (off0, k0), (off1, k1) = chunks(s)
                    if live(r, c + off0):
                        max_chunk(r, c, off0, k0)
                    if s == 0 and live(r, c - 1):
                        pv_tile(r, c - 1, KT - 1)
                    if s > 0 and live(r, c):
                        pv_tile(r, c, s - 1)
                    if live(r, c + off1):
                        max_chunk(r, c, off1, k1)

            iteration(0, -2)
            transpose_norm(1, 1, 2, xt_psum)
            for use in PREP[6:]:
                prepare[use[0]](0, 2, int(use[1]))
            pe.wait_ge(xt2_ok, 4)
            project(CROSS_W, 1, 3, q_psum)
            pe.wait_ge(prep_read["V"], 9)
            iteration(0, -1)
            pe.wait_ge(q2_ok, 4)
            iteration(0, 0)
            with pe.Fori(0, 4, 1) as r:
                for c in (1, 2, 3):
                    iteration(r, c)
            for c in (1, 2, 3, 4):
                iteration(4, c)

            pe.wait_ge(misc_read, misc_index(4, 4, "tr") + 1)
            out_project(1, 1, ps[:, 3], o_psum)

            hb = [[ps[:, 3 * n + k, 0:HALF] for k in range(3)] for n in range(2)]
            yb = [ps[:, 6, 0:HALF], ps[:, 7, 0:HALF]]

            def hidden(u, n, half, part):
                cols = slice(HALF * half, HALF * half + HALF)
                if part == 0 and not (isinstance(u, int) and u == 0):
                    pe.wait_ge(u_ok, 2 * u + half - 1)
                if part == 0 and half == 0:
                    pe.wait_ge(wh_ok, u + 1)
                return split_matmul(hb[half][part], wh[n][:, 0, part], wh[n][:, 1, part], xt1[:, cols], xt2[:, cols])

            def gates(half, pr):
                return mm(hb[half][2], pairsel[:, bass.ds(pr, 1)].rearrange("p o e h -> p (o e h)"),
                          gt[:, HALF * half:HALF * half + HALF], start=True, stop=True)

            def add_ranks(half):
                for j in range(TT):
                    for k in range(TILES[half][0], min(j + 1, TILES[half][1])):
                        last = mm(ps[:, 2, NE * j:NE * j + NE], before[:] if k == j else ones_h[:], chosen_h[:, k],
                                  start=j == 0, stop=half == 1 or k == j, skip_group_check=True)
                return last

            def down(u, n, half, first=False, final=False):
                pe.wait_ge(u2_ok, 2 * u + half + 1)
                for w, uh, k in ((0, u1_sb, 0), (0, u2_sb, 1), (1, u1_sb, 2)):
                    last = mm(yb[half], wh[n][:, w, 2], uh[half], start=first and k == 0, stop=final and k == 2,
                              skip_group_check=True)
                last.then_inc(y_done, 1)

            hidden(0, 0, 0, 0).then_inc(h1_psum, 1)
            hidden(0, 0, 0, 1).then_inc(h_psum, 1)
            pe.wait_ge(rt_step, 10)
            add_ranks(0)
            pe.wait_ge(mx_read, NCH * B)
            transpose_norm(2, 1, 4, xt_psum)
            router_logits(1, ps[:, 7]).then_inc(lg_psum, 1)
            pe.wait_ge(xt2_ok, 5)
            hidden(0, 0, 1, 0).then_inc(h1_psum, 1)
            hidden(0, 0, 1, 1).then_inc(h_psum, 1)
            hidden(1, 1, 0, 0).then_inc(h1_psum, 1)
            hidden(1, 1, 0, 1)
            pe.wait_ge(rt_step, 21)
            add_ranks(1).then_inc(rank_psum, 1)
            hidden(1, 1, 1, 0).then_inc(h1_psum, 1)
            hidden(1, 1, 1, 1)
            down(0, 0, 0, first=True)
            down(0, 0, 1, first=True)
            pe.wait_ge(rt_step, 24)
            for j in range(TT):
                last = tr(ps[0:64, 5, :].bitcast(F16)[:, 128 * j:128 * j + 128], gpair[:, j], identh[:])
            last.then_inc(gt_psum, 1)
            pe.wait_ge(gt_ok, 1)
            for half in range(2):
                gates(half, 0).then_inc(h_psum, 1)

            def unit(u, n):
                for half in range(2):
                    hidden(u, n, half, 0).then_inc(h1_psum, 1)
                    gates(half, u - 1)
                    hidden(u, n, half, 1).then_inc(h_psum, 1)
                    down(u - 1, (n - 1) % NW, half)

            for u in range(2, NW):
                unit(u, u)
            with pe.Fori(1, NP // NW, 1) as r:
                for n in range(NW):
                    unit(NW * r + n, n)
            unit(NP, 0)
            down(NP, 0, 0, final=True)
            down(NP, 0, 1, final=True)
            for half, (a, z) in enumerate(OUT_TILES):
                pe.wait_ge(yt_ok, half + 1)
                for j in range(a, z):
                    last = tr(ps[:, half, 128 * (j - a):128 * (j - a) + 128], yt[:, 128 * j:128 * j + 128], ident[:])
                last.then_inc(yt_psum, 1)

        @block.scalar
        def _(act):
            A = nc.scalar.activation
            for half in range(2):
                act.wait_ge(wt_psum, half + 1)
                src = ps[:, half, :].rearrange("p (n e) -> p n e", n=4)
                if half == 0:
                    A(wk3[:, 0], src[:, SELF_W + 1].rearrange("p (g a c) -> p g a c", g=G, a=1).to_broadcast([128, G, 3, 32]),
                      ACT.Copy)
                A(wt32[:, half], src[:, 3], ACT.Copy)
                A(wt1[:, 4 * half:4 * half + 4], src, ACT.Copy).then_inc(wt1_ok, 1)

            def norm_out(n, half, bank, done, count):
                a, z = X[half]
                act.wait_ge(done, count)
                if n == 2:
                    A(xt32[:, a:z], ps[:, bank, 0:z - a], ACT.Copy)
                A(xt1[:, a:z], ps[:, bank, 0:z - a], ACT.Copy).then_inc(xt1_ok, 1)

            def second_queries(n, k):
                a, z = PARTS[n][k]
                act.wait_ge(q2_ok, 2 * n + (2 if n == 0 or k == 2 else 1))
                if n:
                    for m in range(2):
                        act.wait_ge(qs_ok[m], 12 * 16)
                for h in range(HG):
                    A(qd[1][:, a:z, h, :], q2[:].rearrange("p (b q) -> p b q", b=B)[:, a:z], ACT.Copy,
                      scale=headmask[:, h:h + 1]).then_inc(qd_ok[k], 1)

            for half in range(2):
                norm_out(0, half, 2 + half, xt_psum, half + 1)
            act.wait_ge(b_loaded, 5 * 16)
            for half in range(2):
                act.wait_ge(q_psum, half + 1)
                A(q1[:, HALF * half:HALF * half + HALF], ps[:, 4 + half, 0:HALF], ACT.Identity,
                  bias=bq[:, 0:1]).then_inc(q1_ok, 1)
            act.wait_ge(mask_ok, 1)
            second_queries(0, 0)
            act.wait_ge(bk_psum, 1)
            A(bk[:], ps[0:96, 0, 0:G], ACT.Copy).then_inc(bk_ok, 1)
            act.wait_ge(bk_ok, 1)
            for u in range(2 * G):
                g, cols = u // 2, slice(HALF * (u % 2), HALF * (u % 2) + HALF)
                act.wait_ge(k_psum, u + 1)
                A(kself[0:96, g, cols], ps[0:96, (1, 6, 7, 0)[u % 4], 0:HALF], ACT.Identity,
                  bias=bk[:, g:g + 1]).then_inc(ks1_ok, 1)
            second_queries(0, 1)
            def take_keys(r, c, j):
                act.wait_ge(*use_filled(r, c, f"K{j}"))
                if j == 0:
                    if not isinstance(r, int) or 3 * r + c > 0:
                        act.wait_ge(first_ok[(c - 1) % 3], 16 * NFIRST * (r + (c - 1) // 3 + 1))
                        act.wait_ge(rest_ok[(c - 1) % 3], 16 * NREST * (r + (c - 1) // 3 + 1))
                A(k12[:, 0, CH * j:CH * j + CH], use_bank(r, c, j)[:, 0:CH], ACT.Copy).then_inc(k1_ok, 1)

            def take_values(r, c, j):
                act.wait_ge(*use_filled(r, c, f"V{j}"))
                A(v[c % 3][0:KP, 4 * j:4 * j + 4, :].rearrange("p t (h e) -> p t h e", h=H)[:, :, :, 0:HD],
                  use_bank(r, c, j)[0:KP, :].rearrange("p (t h e) -> p t h e", t=4, h=H), ACT.Copy
                  ).then_inc(use_read(r, c, "V0")[0], 1)

            take = {"K": take_keys, "V": take_values}
            for use in PREP[3:6]:
                take[use[0]](0, 0, int(use[1]))
            act.wait_ge(bt_psum, 1)
            for k, bank in enumerate((2, 3, 0, 7)):
                last = A(brow[:, 4 * k:4 * k + 4, :],
                         ps[0:KT, bank, :].rearrange("p (b k) -> p b k", b=4)[:, :, 0:KP], ACT.Copy)
            last.then_inc(brow_ok, 1)

            act.wait_ge(ones_ok, 1)
            for use in PREP[6:]:
                take[use[0]](0, 0, int(use[1]))
            act.wait_ge(mselft_psum, 1)
            A(mrow_self[:], ps[:, 0, 0:112], ACT.Copy, scale=1.0 / BIG).then_inc(mselfr_ok, 1)
            for use in PREP[3:]:
                take[use[0]](0, 1, int(use[1]))

            def self_step(r, c):
                j, k = 2 * r + c, c % 2
                if self_live(r, c):
                    act.wait_ge(st_done, j + 1)
                    if not (isinstance(r, int) and j < 2):
                        act.wait_ge(pv_done, j - 1)
                    A(p[k][0:S].rearrange("p (a c) -> p a c", a=2), sbank[k][0:S, :, 0:448], ACT.Exp,
                      scale=SCALE).then_inc(exp_done, 1)
                if self_live(r, c - 3):
                    act.wait_ge(misc_done, self_index(r, c, "tr") + 1)
                    A(attn[:, bass.ds(S * (j - 3), S)], misc[:, 0:S], ACT.Copy).then_inc(misc_read, 1)
                if self_live(r, c - 1):
                    act.wait_ge(pv_done, j)
                    if self_live(r, c - 2):
                        act.wait_ge(misc_done, self_index(r, c, "sel") + 1)
                    A(osb[:], obank[:, 0:224], ACT.Copy).then_inc(o_read, 1)
                if isinstance(r, int) and j == OUT_STEP + 3:
                    norm_out(1, 0, 4, xt_psum, 3)
                if isinstance(r, int) and j == OUT_STEP + 4:
                    act.wait_ge(q_psum, 3)
                    A(q1[:, 0:HALF], ps[:, 5, 0:HALF], ACT.Copy).then_inc(q1_ok, 1)
                if isinstance(r, int) and j == OUT_STEP + 5:
                    second_queries(1, 0)
                    second_queries(1, 1)

            act.wait_ge(clear_ok, 1)
            for c in (0, 1, 2):
                self_step(0, c)
            with act.Fori(0, 5, 1) as r:
                for c in (3, 4):
                    self_step(r, c)
            for c in range(3, 9):
                self_step(5, c)

            for use in PREP[3:6]:
                take[use[0]](0, 2, int(use[1]))
            norm_out(1, 1, 2, xt_psum, 4)
            act.wait_ge(pv_done, B)
            for use in PREP[6:]:
                take[use[0]](0, 2, int(use[1]))
            act.wait_ge(bias_step, 3)

            def iteration(r, c):
                i = 3 * r + c
                for s in range(KT):
                    use = MISC[s]
                    if used(r, c, use):
                        if tail(r, c, use) == "norm":
                            norm_out(2, 0, 6, misc_done, misc_index(r, c, use) + 1)
                        elif use[0] in "KV":
                            take[use[0]](r, c + 2, int(use[1]))
                        elif use == "tr":
                            act.wait_ge(misc_done, misc_index(r, c, use) + 1)
                            A(attn[:, bass.ds(S * (i - 1), S)], misc[:, 0:S], ACT.Copy).then_inc(misc_read, 1)
                        elif use == "mt":
                            act.wait_ge(misc_done, misc_index(r, c, use) + 1)
                            A(mrow[:], misc[0:8, 0:112], ACT.Copy, scale=1.0 / BIG).then_inc(misc_read, 1)
                    if live(r, c):
                        tile = B + KT * i + s
                        act.wait_ge(st_done, tile + 1)
                        act.wait_ge(pv_done, tile - 1)
                        A(p[s % 2][0:KP].rearrange("p (a c) -> p a c", a=2), sbank[s % 2][0:KP, :, 0:448],
                          ACT.Exp, scale=SCALE,
                          bias=bres[:, bass.ds(i, 1), s:s + 1].rearrange("p o t -> p (o t)")).then_inc(exp_done, 1)
                    if s == 0 and live(r, c - 1):
                        act.wait_ge(pv_done, B + KT * i)
                        A(osb[:], obank[:, 0:224], ACT.Copy).then_inc(o_read, 1)
                    if s == 3 and isinstance(r, int) and i == B - 1:
                        act.wait_ge(misc_read, misc_index(r, c, "T0") + 1)
                        A(prob[:, 0:4], logit[:, 0:4], ACT.Exp).then_inc(rt_exp, 1)

            act.wait_ge(q_psum, 4)
            A(q1[:, HALF:T], ps[:, 3, 0:HALF], ACT.Copy).then_inc(q1_ok, 1)
            iteration(0, -1)
            second_queries(1, 2)
            iteration(0, 0)
            with act.Fori(0, 4, 1) as r:
                for c in (1, 2, 3):
                    iteration(r, c)
            for c in (1, 2, 3, 4):
                iteration(4, c)

            norm_out(2, 1, 4, xt_psum, 5)
            act.wait_ge(rt_step, 12)
            A(prob[:, 4:TT], logit[:, 4:TT], ACT.Exp).then_inc(rt_exp, 1)

            def silu(u, half):
                step = 2 * u + half
                act.wait_ge(h1_psum, step + 1)
                if not (isinstance(u, int) and u == 0):
                    act.wait_ge(u_ok, step - 1)
                A(act_sb[half], ps[:, 3 * half, 0:HALF], ACT.Silu).then_inc(silu_ok, 1)

            def first_part(u, half):
                step = 2 * u + half
                act.wait_ge(u_ok, step + 1)
                if not (isinstance(u, int) and step < 2):
                    act.wait_ge(y_done, step - 1)
                A(u1_sb[half], u_sb[half], ACT.Copy).then_inc(u1_ok, 1)

            silu(0, 0)
            silu(0, 1)
            first_part(0, 0)
            first_part(0, 1)
            silu(1, 0)
            silu(1, 1)
            first_part(1, 0)
            with act.Fori(2, NP + 1, 1) as u:
                silu(u, 0)
                first_part(u - 1, 1)
                silu(u, 1)
                first_part(u, 0)
            first_part(NP, 1)
            for half in range(2):
                act.wait_ge(y_done, 2 * NP + 1 + half)
                A(yt[:, HALF * half:HALF * half + HALF], ps[:, 6 + half, 0:HALF], ACT.Copy).then_inc(yt_ok, 1)

        @block.vector
        def _(dve):
            V = nc.vector

            def norm_stats(n, half):
                tiles, before = range(*TILES[half]), 3 * (2 * n + half)
                for j in tiles:
                    last = V.bn_stats(stats[:, j], xs[:, j])
                last.then_inc(ln_step, 1)
                dve.wait_ge(ln_step, before + 1)
                for j in tiles:
                    last = V.bn_aggr(mv[:, j], stats[:, j])
                last.then_inc(ln_step, 1)
                dve.wait_ge(ln_step, before + 2)
                V.tensor_scalar_add(veps[:, tiles.start:tiles.stop], mv[:, tiles.start:tiles.stop, 1], EPS
                                    ).then_inc(ln_step, 1)

            def norm_apply(n, half):
                dve.wait_ge(rstd_ok, 2 * n + half + 1)
                for j in range(*TILES[half]):
                    V.tensor_scalar(xn[:, j], xs[:, j], mv[:, j, 0:1], rstd[:, j:j + 1],
                                    ALU.subtract, ALU.mult).then_inc(xn_ok, 1)

            def norm_out(n, half, bank, done):
                a, z = X[half]
                dve.wait_ge(xt1_ok, 2 * n + half + 1)
                V.tensor_tensor(xt2[:, a:z], ps[:, bank, 0:z - a], xt1[:, a:z], ALU.subtract).then_inc(done, 1)

            def first_queries(n, k):
                a, z = PARTS[n][k]
                dve.wait_ge(q1_ok, 2 * n + (2 if n == 0 or k == 2 else 1))
                if n:
                    for m in range(2):
                        dve.wait_ge(qs_ok[m], 12 * 16)
                shape = [128, z - a, HG, S]
                V.tensor_tensor(qd[0][:, a:z],
                                q1[:].rearrange("p (b o q) -> p b o q", b=B, o=1)[:, a:z].to_broadcast(shape),
                                headmask[:].rearrange("p (a h b) -> p a h b", a=1, b=1).to_broadcast(shape),
                                ALU.mult).then_inc(qd_ok[k], 1)

            def add_to_x(tiles, bank, done):
                a, z = tiles
                V.tensor_tensor(xs[:, a:z], xs[:, a:z],
                                bank[:, 0:128 * (z - a)].rearrange("p (j d) -> p j d", d=D), ALU.add
                                ).then_inc(done, 1)

            dve.wait_ge(x_loaded, 16)
            for half in range(2):
                norm_stats(0, half)
            for half in range(2):
                norm_apply(0, half)
            dve.wait_ge(grp_ok, 1)
            V.tensor_reduce(headmask[:], grp[:].rearrange("p g h -> p h g"), axis=AX.X, op=ALU.add).then_inc(mask_ok, 1)
            for half in range(2):
                dve.wait_ge(wt1_ok, half + 1)
                if half == 0:
                    V.tensor_tensor(wk3[:, 1], ps[:, 0, 128:256].rearrange("p (g a c) -> p g a c", g=G, a=1)
                                    .to_broadcast([128, G, 3, 32]), wk3[:, 0], ALU.subtract)
                V.tensor_tensor(wt2[:, 4 * half:4 * half + 4], ps[:, half, :].rearrange("p (n e) -> p n e", n=4),
                                wt1[:, 4 * half:4 * half + 4], ALU.subtract).then_inc(wt2_ok, 1)
            for half in range(2):
                norm_out(0, half, 2 + half, xt2_ok)
            dve.wait_ge(bias_loaded, 16)
            V.tensor_scalar(bh[:], bcol[:], SQ / BIG, None, ALU.mult).then_inc(bias_step, 1)
            dve.wait_ge(bias_step, 1)
            V.tensor_copy(bh32[:], bh[:]).then_inc(bias_step, 1)
            dve.wait_ge(bias_step, 2)
            V.scalar_tensor_tensor(bres[:].rearrange("p b t -> p (b t)"), bh32[:].rearrange("p b t -> p (b t)"),
                                   -BIG / SQ, bcol[:].rearrange("p b t -> p (b t)"), ALU.mult, ALU.add
                                   ).then_inc(bias_step, 1)
            dve.wait_ge(b_loaded, 5 * 16)
            for half in range(2):
                cols = slice(HALF * half, HALF * half + HALF)
                dve.wait_ge(q1_ok, half + 1)
                V.scalar_tensor_tensor(q2[:, cols], ps[:, 4 + half, 0:HALF], bq[:, 0:1], q1[:, cols],
                                       ALU.add, ALU.subtract).then_inc(q2_ok, 1)
            dve.wait_ge(mask_ok, 1)
            first_queries(0, 0)
            for u in range(2 * G):
                g, cols = u // 2, slice(HALF * (u % 2), HALF * (u % 2) + HALF)
                dve.wait_ge(ks1_ok, u + 1)
                V.scalar_tensor_tensor(kself[32:64, g, cols], ps[32:64, (1, 6, 7, 0)[u % 4], 0:HALF], bk[32:64, g:g + 1],
                                       kself[32:64, g, cols], ALU.add, ALU.subtract).then_inc(ks2_ok, 1)
            first_queries(0, 1)

            def take_ctx(r, c, j):
                dve.wait_ge(*use_filled(r, c, f"T{j}"))
                V.tensor_copy(ct[:, :, 4 * j:4 * j + 4, :],
                              use_bank(r, c, j).bitcast(F16).rearrange("p (a t k) -> p a t k", a=2, t=4)
                              ).then_inc(use_read(r, c, "T0")[0], 1)

            def take_keys(r, c, j):
                dve.wait_ge(k1_ok, 3 * (3 * r + c) + j + 1)
                V.tensor_tensor(k12[:, 1, CH * j:CH * j + CH], use_bank(r, c, j)[:, 0:CH],
                                k12[:, 0, CH * j:CH * j + CH], ALU.subtract).then_inc(use_read(r, c, "K0")[0], 1)

            take = {"T": take_ctx, "K": take_keys}

            def self_maxima(r):
                for k in range(4):
                    b = 4 * r + k
                    dve.wait_ge(mself_psum, b + 1)
                    V.tensor_reduce(mself[:, bass.ds(b, 1), :].rearrange("p o k -> p (o k)"),
                                    ps[0:112, k, 0:8 * S].rearrange("p (k s) -> p k s", k=8),
                                    axis=AX.X, op=ALU.max, negate=True).then_inc(mself_ok, 1)

            for n in range(2):
                V.memset(p[n][:], 0.0)
            V.memset(tok[:], 0.0).then_inc(clear_ok, 1)
            for use in PREP[0:6]:
                take[use[0]](0, 0, int(use[1]))
            self_maxima(0)
            for use in PREP[0:3]:
                take[use[0]](0, 1, int(use[1]))
            with dve.Fori(1, B // 4, 1) as r:
                self_maxima(r)
            for use in PREP[3:6]:
                take[use[0]](0, 1, int(use[1]))
            V.tensor_tensor(xs[:], xs[:], bp[:].rearrange("p (o d) -> p o d", o=1).to_broadcast([128, TT, D]),
                            ALU.add).then_inc(xb_ok, 1)

            def normalize(batches):
                part = misc[0:S, 0:144].rearrange("p (k a e) -> p k a e", k=4, a=4)
                V.reciprocal(rec[:], part[:, :, :, HD]).then_inc(norm_step, 1)
                dve.wait_ge(norm_step, batches + 1)
                V.tensor_tensor(tok[0:S, 0:96].rearrange("p (a k e) -> p k a e", a=4, k=3), part[:, 0:3, :, 0:HD],
                                rec[:, 0:3, :].rearrange("p k (a o) -> p k a o", o=1).to_broadcast([S, 3, 4, HD]),
                                ALU.mult)
                V.tensor_tensor(tok[0:S, 96:128].rearrange("p (a e) -> p a e", a=4), part[:, 3, :, 0:HD],
                                rec[:, 3, :].rearrange("p (a o) -> p a o", o=1).to_broadcast([S, 4, HD]),
                                ALU.mult).then_inc(misc_read, 1)

            def self_step(r, c):
                j, k = 2 * r + c, c % 2
                if self_live(r, c):
                    dve.wait_ge(vself_psum, j + 1)
                    if not (isinstance(r, int) and j < 2):
                        dve.wait_ge(pv_done, j - 1)
                    V.tensor_tensor(v[2][0:S, k].rearrange("p (h e) -> p h e", h=H)[:, :, 0:HD],
                                    mbank[k][0:S, 0:D].rearrange("p (h e) -> p h e", h=H),
                                    bv[:].rearrange("p (h e) -> p h e", h=H), ALU.add).then_inc(vself_ok, 1)
                if self_live(r, c - 2):
                    dve.wait_ge(misc_done, self_index(r, c, "sel") + 1)
                    normalize(j - 2)
                if isinstance(r, int) and j == OUT_STEP:
                    dve.wait_ge(xb_ok, 1)
                    dve.wait_ge(misc_done, self_index(r, c, "out") + 1)
                    add_to_x(TILES[0], misc, misc_read)
                    dve.wait_ge(misc_read, self_index(r, c, "out") + 1)
                    norm_stats(1, 0)
                if isinstance(r, int) and j == OUT_STEP + 1:
                    norm_apply(1, 0)
                if isinstance(r, int) and j == OUT_STEP + 3:
                    norm_out(1, 0, 4, xt2_ok)
                if isinstance(r, int) and j == OUT_STEP + 4:
                    dve.wait_ge(q1_ok, 3)
                    V.tensor_tensor(q2[:, 0:HALF], ps[:, 5, 0:HALF], q1[:, 0:HALF], ALU.subtract).then_inc(q2_ok, 1)
                    first_queries(1, 0)
                    first_queries(1, 1)

            dve.wait_ge(ones_ok, 1)
            dve.wait_ge(brow_ok, 1)
            V.memset(obank[:, 0:224], 0.0).then_inc(o_clear, 1)
            for c in (0, 1, 2):
                self_step(0, c)
            with dve.Fori(0, 5, 1) as r:
                for c in (3, 4):
                    self_step(r, c)
            for c in range(3, 9):
                self_step(5, c)

            dve.wait_ge(o_psum, 1)
            add_to_x(TILES[1], ps[:, 0], x_ok)
            dve.wait_ge(x_ok, 1)
            norm_stats(1, 1)
            for use in PREP[0:3]:
                take[use[0]](0, 2, int(use[1]))
            norm_apply(1, 1)
            for use in PREP[3:6]:
                take[use[0]](0, 2, int(use[1]))

            steps = [0]

            def step(ins):
                steps[0] += 1
                ins.then_inc(rt_step, 1)
                dve.wait_ge(rt_step, steps[0])

            def shifted_logits(half, bank, done, count):
                j = slice(*TILES[half])
                n = j.stop - j.start
                lg = bank[:, 0:n * NE].rearrange("p (j e) -> p j e", e=NE)
                step(V.tensor_reduce(rmax[:, j], lg, axis=AX.X, op=ALU.max))
                V.tensor_tensor(logit[:, j], lg, rmax[:, j].rearrange("p (j o) -> p j o", o=1).to_broadcast([128, n, NE]),
                                ALU.subtract).then_inc(done, 1)
                dve.wait_ge(done, count)

            def route(half, part):
                j = slice(*TILES[half])
                n = j.stop - j.start
                if part == 1:
                    dve.wait_ge(rt_exp, half + 1)
                    step(V.tensor_reduce(rsum[:, j], prob[:, j], axis=AX.X, op=ALU.add))
                    step(V.reciprocal(rrec[:, j], rsum[:, j]))
                    step(V.tensor_tensor(prob[:, j], prob[:, j],
                                         rrec[:, j].rearrange("p (j o) -> p j o", o=1).to_broadcast([128, n, NE]), ALU.mult))
                if part == 2:
                    for t in range(*TILES[half]):
                        last = V.max(top8[:, t], prob[:, t])
                    step(last)
                    for t in range(*TILES[half]):
                        last = V.max_index(idx8[:, t], top8[:, t], prob[:, t])
                    step(last)
                    step(V.tensor_copy(idxf[:, j], idx8[:, j]))
                if part == 3:
                    step(V.tensor_tensor(eq[:, j],
                                         idxf[:, j, 0:TOPK].rearrange("p j (k o) -> p j k o", o=1).to_broadcast([128, n, TOPK, NE]),
                                         expert_no[:].rearrange("p (a b e) -> p a b e", a=1, b=1).to_broadcast([128, n, TOPK, NE]),
                                         ALU.is_equal))
                if part == 4:
                    step(V.tensor_reduce(chosen[:, j], eq[:, j].rearrange("p j k e -> p j e k"), axis=AX.X, op=ALU.add))
                    V.tensor_copy(chosen_h[:, j], chosen[:, j])
                    step(V.tensor_tensor(gate[:, j], prob[:, j], chosen[:, j], ALU.mult))

            def iteration(r, c):
                i = 3 * r + c
                for s in range(KT):
                    use = MISC[s]
                    if used(r, c, use):
                        if tail(r, c, use) == "out":
                            dve.wait_ge(misc_done, misc_index(r, c, use) + 1)
                            add_to_x(TILES[0], misc, misc_read)
                            dve.wait_ge(misc_read, misc_index(r, c, use) + 1)
                            norm_stats(2, 0)
                        elif tail(r, c, use) == "norm":
                            norm_out(2, 0, 6, misc_read)
                        elif tail(r, c, use) == "logits":
                            dve.wait_ge(st_done, B + KT * i)
                            dve.wait_ge(misc_done, misc_index(r, c, use) + 1)
                            shifted_logits(0, misc, misc_read, misc_index(r, c, use) + 1)
                        elif use[0] in "TK":
                            take[use[0]](r, c + 2, int(use[1]))
                        elif use == "sel":
                            dve.wait_ge(misc_done, misc_index(r, c, use) + 1)
                            normalize(B + i - 1)
                    if isinstance(r, int) and i == -1 and s == 9:
                        dve.wait_ge(q1_ok, 4)
                        V.tensor_tensor(q2[:, HALF:T], ps[:, 3, 0:HALF], q1[:, HALF:T], ALU.subtract).then_inc(q2_ok, 1)
                    if isinstance(r, int) and i == B - 2 and s == 3:
                        norm_apply(2, 0)
                    if isinstance(r, int) and i == B - 1 and s in (4, 5, 7, 8):
                        route(0, (4, 5, 7, 8).index(s) + 1)
                    for off, k in chunks(s):
                        if not live(r, c + off):
                            continue
                        b = i + off
                        dve.wait_ge(mx_psum, NCH * b + k + 1)
                        if k == 0 and not (isinstance(r, int) and b == 0):
                            dve.wait_ge(mcol_ok, b)
                        V.tensor_reduce(mx[:, k // 3, k % 3:k % 3 + 1], mbank[k % 2][0:112, 0:CH],
                                        axis=AX.X, op=ALU.max).then_inc(mx_read, 1)
                        if k == NCH - 1:
                            dve.wait_ge(mx_read, NCH * (b + 1))
                            V.tensor_reduce(mcol[:], mx[:], axis=AX.X, op=ALU.max, negate=True).then_inc(mcol_ok, 1)

            iteration(0, -2)
            norm_out(1, 1, 2, xt2_ok)
            iteration(0, -1)
            first_queries(1, 2)
            iteration(0, 0)
            with dve.Fori(0, 4, 1) as r:
                for c in (1, 2, 3):
                    iteration(r, c)
            for c in (1, 2, 3, 4):
                iteration(4, c)

            dve.wait_ge(o_psum, 2)
            add_to_x(TILES[1], ps[:, 3], x_ok)
            dve.wait_ge(x_ok, 2)
            norm_stats(2, 1)
            norm_apply(2, 1)
            norm_out(2, 1, 4, xt2_ok)
            def shared(half):
                dve.wait_ge(silu_ok, half + 1)
                dve.wait_ge(h_psum, half + 1)
                V.tensor_tensor(u_sb[half], ps[:, 3 * half + 1, 0:HALF], act_sb[half], ALU.mult).then_inc(u_ok, 1)

            def second_part(u, half):
                dve.wait_ge(u1_ok, 2 * u + half + 1)
                V.tensor_tensor(u2_sb[half], u_sb[half], u1_sb[half], ALU.subtract).then_inc(u2_ok, 1)

            dve.wait_ge(lg_psum, 1)
            shifted_logits(1, ps[:, 7], rt_step, 12)
            steps[0] += 1
            route(1, 1)
            route(1, 2)
            shared(0)
            shared(1)
            route(1, 3)
            route(1, 4)

            second_part(0, 0)
            second_part(0, 1)
            dve.wait_ge(rank_psum, 1)
            step(V.scalar_tensor_tensor(gate, ps[:, 2, 0:TT * NE].rearrange("p (j e) -> p j e", e=NE), float(CAP),
                                        gate, ALU.is_lt, ALU.mult))
            step(V.tensor_copy(gpair[:, :, 0:NE], gate))
            step(V.tensor_tensor(gpair[:, :, NE:64], gate, gpair[:, :, 0:NE], ALU.subtract))
            dve.wait_ge(gt_psum, 1)
            V.tensor_copy(gt, ps[0:64, 5, :].bitcast(F16)[:, 0:T]).then_inc(gt_ok, 1)

            def gated(u, half):
                step = 2 * u + half
                dve.wait_ge(silu_ok, step + 1)
                dve.wait_ge(h_psum, step + 1)
                V.tensor_tensor(mid_sb[half], ps[:, 3 * half + 1, 0:HALF], act_sb[half], ALU.mult).then_inc(mid_ok, 1)
                if not (isinstance(u, int) and step == 2):
                    second_part(*((u, 0) if half else (u - 1, 1)))
                dve.wait_ge(mid_ok, step - 1)
                dve.wait_ge(u1_ok, step - 1)
                V.tensor_tensor(u_sb[half], ps[:, 3 * half + 2, 0:HALF], mid_sb[half], ALU.mult).then_inc(u_ok, 1)

            gated(1, 0)
            with dve.Fori(1, NP, 1) as u:
                gated(u, 1)
                gated(u + 1, 0)
            gated(NP, 1)
            second_part(NP, 1)
            for half in range(2):
                dve.wait_ge(yt_psum, half + 1)
                add_to_x(OUT_TILES[half], ps[:, half], res_ok)


_INS = ["x", "ctx_1024", "fside_BxS2_0", "L0_attn_qkv_w", "L0_attn_qkv_b", "L0_attn_proj_w", "L0_attn_proj_b",
        "L0_xattn_Wq", "L0_xattn_Wk", "L0_xattn_Wv", "L0_xattn_Wo", "L0_ffn_Wg", "L0_ffn_W1", "L0_ffn_W2",
        "L0_ffn_W3", "L0_ffn_Ws1", "L0_ffn_Ws2", "L0_ffn_Ws3"]


def kernel(**inputs):
    import numpy as _np
    import concourse.bacc as _bacc
    from concourse import mybir as _mybir
    from concourse.bass_utils import run_bass_kernel_spmd as _run

    nc = _bacc.Bacc("TRN2", target_bir_lowering=False, num_devices=1)
    arrays, args = {}, []
    for name in _INS:
        a = _np.ascontiguousarray(inputs[name])
        arrays[f"in_{name}"] = a
        args.append(nc.dram_tensor(f"in_{name}", a.shape, _mybir.dt.from_np(a.dtype), kind="ExternalInput").ap())
    out = nc.dram_tensor("out", (B, S, D), _mybir.dt.float32, kind="ExternalOutput").ap()
    (x, ctx, bias, qkv_w, qkv_b, proj_w, proj_b, wq, wk, wv, wo, wg, w1, w2, w3, ws1, ws2, ws3) = args
    build(nc, x, ctx, bias, qkv_w, qkv_b, proj_w, proj_b, wq, wk, wv, wo, wg, w1, w2, w3, ws1, ws2, ws3, out)
    r = _run(nc, [arrays], core_ids=[0])
    return r.results[0]["out"]
```
